# Optimizing a Trainium2 kernel written in Bass

```python
import numpy as np
import jax
import jax.numpy as jnp

def _softmax(x, axis=-1):
    return jax.nn.softmax(x, axis=axis)

def _gelu(x):
    return jax.nn.gelu(x, approximate=True)

def _silu(x):
    return jax.nn.silu(x)

def _sigmoid(x):
    return jax.nn.sigmoid(x)

def _layernorm(x, axis=-1, eps=1e-05):
    m = jnp.mean(x, axis=axis, keepdims=True)
    v = jnp.var(x, axis=axis, keepdims=True)
    return (x - m) / jnp.sqrt(v + eps)

def _scatter_add(tgt, idx, src, axis=0):
    return tgt.at[idx].add(src)

def _segment_sum(src, seg, n):
    return jax.ops.segment_sum(src, seg, n)
kernel_name = 'mk_recurrent_d1_jaxref_r4_871e61'

def setup_inputs(seed: int=0):
    np.random.seed(seed)
    _w = jnp.asarray

    def _L0_attn_setup():
        import jax, jax.numpy as jnp
        import numpy as np
        B, L, E, H = (4, 1024, 256, 16)
        D = E // H
        MLP = 1024
        EPS = 1e-06

        def layer_norm(x, g, b):
            mu = jnp.mean(x, -1, keepdims=True)
            v = jnp.mean((x - mu) ** 2, -1, keepdims=True)
            return (x - mu) * jax.lax.rsqrt(v + 1e-05) * g + b
        key = jax.random.key(seed)
        ks = jax.random.split(key, 16)
        s = 1.0 / np.sqrt(E)
        inp = {'x': jax.random.normal(ks[0], (B, L, E), jnp.float32), 'Wq': jax.random.normal(ks[1], (E, E), jnp.float32) * s, 'bq': jnp.zeros((E,), jnp.float32), 'lnq_g': jnp.ones((E,), jnp.float32), 'lnq_b': jnp.zeros((E,), jnp.float32), 'Wk': jax.random.normal(ks[2], (E, E), jnp.float32) * s, 'bk': jnp.zeros((E,), jnp.float32), 'lnk_g': jnp.ones((E,), jnp.float32), 'lnk_b': jnp.zeros((E,), jnp.float32), 'Wv': jax.random.normal(ks[3], (E, E), jnp.float32) * s, 'bv': jnp.zeros((E,), jnp.float32), 'lnv_g': jnp.ones((E,), jnp.float32), 'lnv_b': jnp.zeros((E,), jnp.float32), 'Wphi_q': jax.random.normal(ks[4], (E, E), jnp.float32) * s, 'bphi_q': jax.random.normal(ks[5], (E,), jnp.float32) * 0.01, 'Wphi_k': jax.random.normal(ks[6], (E, E), jnp.float32) * s, 'bphi_k': jax.random.normal(ks[7], (E,), jnp.float32) * 0.01, 'lna_g': jnp.ones((E,), jnp.float32), 'lna_b': jnp.zeros((E,), jnp.float32), 'W1': jax.random.normal(ks[8], (E, MLP), jnp.float32) * s, 'b1': jnp.zeros((MLP,), jnp.float32), 'W2': jax.random.normal(ks[9], (MLP, E), jnp.float32) * (1.0 / np.sqrt(MLP)), 'b2': jnp.zeros((E,), jnp.float32), 'gamma': jnp.float32(0.1), 'conv_w': jax.random.normal(ks[10], (E, E // H, 5), jnp.float32) * (1.0 / np.sqrt(E // H * 5)), 'conv_b': jnp.zeros((E,), jnp.float32)}
        return inp
    _L0_attn_in = _L0_attn_setup()

    def _L0_ffn_setup():
        import jax, jax.numpy as jnp
        import numpy as np
        S, B, H = (512, 2, 256)
        NUM_HEADS, NUM_KV_HEADS = (16, 4)
        HEAD_DIM = H // NUM_HEADS
        E, TOP_K, FFN = (16, 2, 512)
        CAP_FACTOR = 1.25
        EPS = 1e-05

        def _layernorm(x, w, b):
            mu = jnp.mean(x, axis=-1, keepdims=True)
            var = jnp.mean((x - mu) ** 2, axis=-1, keepdims=True)
            return (x - mu) * jax.lax.rsqrt(var + EPS) * w + b
        key = jax.random.key(seed)
        ks = jax.random.split(key, 6)
        qkv_out = (NUM_HEADS + 2 * NUM_KV_HEADS) * HEAD_DIM
        sdH = 1.0 / np.sqrt(H)
        sdF = 1.0 / np.sqrt(FFN)
        return {'hidden_states': jax.random.normal(ks[0], (S, B, H), jnp.float32), 'ln1_weight': jnp.ones((H,), jnp.float32), 'ln1_bias': jnp.zeros((H,), jnp.float32), 'ln2_weight': jnp.ones((H,), jnp.float32), 'ln2_bias': jnp.zeros((H,), jnp.float32), 'qkv_weight': jax.random.normal(ks[1], (qkv_out, H), jnp.float32) * sdH, 'proj_weight': jax.random.normal(ks[2], (H, H), jnp.float32) * sdH, 'router_weight': jax.random.normal(ks[3], (E, H), jnp.float32) * sdH, 'moe_w1': jax.random.normal(ks[4], (E, FFN, H), jnp.float32) * sdH, 'moe_w2': jax.random.normal(ks[5], (E, H, FFN), jnp.float32) * sdF}
    _L0_ffn_in = _L0_ffn_setup()
    _d = {'L0_attn_x': _L0_attn_in['x'], 'L0_attn_Wq': _L0_attn_in['Wq'], 'L0_attn_bq': _L0_attn_in['bq'], 'L0_attn_lnq_g': _L0_attn_in['lnq_g'], 'L0_attn_lnq_b': _L0_attn_in['lnq_b'], 'L0_attn_Wk': _L0_attn_in['Wk'], 'L0_attn_bk': _L0_attn_in['bk'], 'L0_attn_lnk_g': _L0_attn_in['lnk_g'], 'L0_attn_lnk_b': _L0_attn_in['lnk_b'], 'L0_attn_Wv': _L0_attn_in['Wv'], 'L0_attn_bv': _L0_attn_in['bv'], 'L0_attn_lnv_g': _L0_attn_in['lnv_g'], 'L0_attn_lnv_b': _L0_attn_in['lnv_b'], 'L0_attn_Wphi_q': _L0_attn_in['Wphi_q'], 'L0_attn_bphi_q': _L0_attn_in['bphi_q'], 'L0_attn_Wphi_k': _L0_attn_in['Wphi_k'], 'L0_attn_bphi_k': _L0_attn_in['bphi_k'], 'L0_attn_lna_g': _L0_attn_in['lna_g'], 'L0_attn_lna_b': _L0_attn_in['lna_b'], 'L0_attn_W1': _L0_attn_in['W1'], 'L0_attn_b1': _L0_attn_in['b1'], 'L0_attn_W2': _L0_attn_in['W2'], 'L0_attn_b2': _L0_attn_in['b2'], 'L0_attn_gamma': _L0_attn_in['gamma'], 'L0_attn_conv_w': _L0_attn_in['conv_w'], 'L0_attn_conv_b': _L0_attn_in['conv_b'], 'L0_ffn_ln1_weight': _L0_ffn_in['ln1_weight'], 'L0_ffn_ln1_bias': _L0_ffn_in['ln1_bias'], 'L0_ffn_ln2_weight': _L0_ffn_in['ln2_weight'], 'L0_ffn_ln2_bias': _L0_ffn_in['ln2_bias'], 'L0_ffn_qkv_weight': _L0_ffn_in['qkv_weight'], 'L0_ffn_proj_weight': _L0_ffn_in['proj_weight'], 'L0_ffn_router_weight': _L0_ffn_in['router_weight'], 'L0_ffn_moe_w1': _L0_ffn_in['moe_w1'], 'L0_ffn_moe_w2': _L0_ffn_in['moe_w2']}
    _x0 = _d['L0_attn_x']
    _d['L0_attn_x'] = jax.random.normal(jax.random.fold_in(jax.random.key(seed), 1), (4, 2048, 256), dtype=_x0.dtype)
    del _x0
    return _d

def reference(L0_attn_x, L0_attn_Wq, L0_attn_bq, L0_attn_lnq_g, L0_attn_lnq_b, L0_attn_Wk, L0_attn_bk, L0_attn_lnk_g, L0_attn_lnk_b, L0_attn_Wv, L0_attn_bv, L0_attn_lnv_g, L0_attn_lnv_b, L0_attn_Wphi_q, L0_attn_bphi_q, L0_attn_Wphi_k, L0_attn_bphi_k, L0_attn_lna_g, L0_attn_lna_b, L0_attn_W1, L0_attn_b1, L0_attn_W2, L0_attn_b2, L0_attn_gamma, L0_attn_conv_w, L0_attn_conv_b, L0_ffn_ln1_weight, L0_ffn_ln1_bias, L0_ffn_ln2_weight, L0_ffn_ln2_bias, L0_ffn_qkv_weight, L0_ffn_proj_weight, L0_ffn_router_weight, L0_ffn_moe_w1, L0_ffn_moe_w2):

    def _L0_attn_ref(x, Wq, bq, lnq_g, lnq_b, Wk, bk, lnk_g, lnk_b, Wv, bv, lnv_g, lnv_b, Wphi_q, bphi_q, Wphi_k, bphi_k, lna_g, lna_b, W1, b1, W2, b2, gamma, conv_w, conv_b):
        import jax, jax.numpy as jnp
        import numpy as np
        B, L, E, H = (4, 1024, 256, 16)
        D = E // H
        MLP = 1024
        EPS = 1e-06

        def layer_norm(x, g, b):
            mu = jnp.mean(x, -1, keepdims=True)
            v = jnp.mean((x - mu) ** 2, -1, keepdims=True)
            return (x - mu) * jax.lax.rsqrt(v + 1e-05) * g + b
        Bx, Lq, Ex = x.shape
        Q = layer_norm(x @ Wq + bq, lnq_g, lnq_b)
        K = layer_norm(x @ Wk + bk, lnk_g, lnk_b)
        V = layer_norm(x @ Wv + bv, lnv_g, lnv_b)
        Z = jnp.zeros((Bx, 1, Ex), x.dtype)
        K = jnp.concatenate([Z, K], axis=1)
        V = jnp.concatenate([Z, V], axis=1)
        phiQ = jnp.tanh(Q @ Wphi_q + bphi_q) + 1.0
        phiK = jnp.tanh(K @ Wphi_k + bphi_k) + 1.0
        sh = lambda t: t.reshape(Bx, -1, H, D)
        Qh, Kh, Vh, pQ, pK = (sh(Q), sh(K), sh(V), sh(phiQ), sh(phiK))
        qg = jnp.mean(Qh, axis=1, keepdims=True) / np.sqrt(D)
        scores = jnp.einsum('bihd,blhd->bihl', qg, Kh)
        alpha = jax.nn.softmax(scores, axis=-1) * Lq
        alpha = jnp.transpose(alpha[:, 0], (0, 2, 1))[..., None]
        pKs = pK * alpha
        K_sum = pKs.sum(axis=1)
        KV = jnp.einsum('blhd,blhe->bhde', pKs, Vh)
        num = jnp.einsum('blhd,bhde->blhe', pQ, KV)
        den = jnp.einsum('blhd,bhd->blh', pQ, K_sum)[..., None] + EPS
        attn = (num / den).reshape(Bx, Lq, Ex)
        xt = jnp.transpose(attn, (0, 2, 1))
        conv = jax.lax.conv_general_dilated(xt, conv_w, (1,), [(2, 2)], feature_group_count=H)
        local = gamma * (conv + conv_b[None, :, None])
        attn = attn + jnp.transpose(local, (0, 2, 1))
        attn = layer_norm(attn, lna_g, lna_b)
        h = jax.nn.gelu(attn @ W1 + b1, approximate=False) @ W2 + b2
        return attn + h + x

    def _L0_ffn_ref(hidden_states, ln1_weight, ln1_bias, ln2_weight, ln2_bias, qkv_weight, proj_weight, router_weight, moe_w1, moe_w2):
        import jax, jax.numpy as jnp
        import numpy as np
        S, B, H = (512, 2, 256)
        NUM_HEADS, NUM_KV_HEADS = (16, 4)
        HEAD_DIM = H // NUM_HEADS
        E, TOP_K, FFN = (16, 2, 512)
        CAP_FACTOR = 1.25
        EPS = 1e-05

        def _layernorm(x, w, b):
            mu = jnp.mean(x, axis=-1, keepdims=True)
            var = jnp.mean((x - mu) ** 2, axis=-1, keepdims=True)
            return (x - mu) * jax.lax.rsqrt(var + EPS) * w + b
        S_, B_, H_ = hidden_states.shape
        dtype = hidden_states.dtype
        ln1 = _layernorm(hidden_states, ln1_weight, ln1_bias)
        qkv = jnp.einsum('sbh,oh->sbo', ln1, qkv_weight)
        q_sz = NUM_HEADS * HEAD_DIM
        kv_sz = NUM_KV_HEADS * HEAD_DIM
        q = qkv[..., :q_sz].reshape(S_, B_, NUM_HEADS, HEAD_DIM)
        k = qkv[..., q_sz:q_sz + kv_sz].reshape(S_, B_, NUM_KV_HEADS, HEAD_DIM)
        v = qkv[..., q_sz + kv_sz:].reshape(S_, B_, NUM_KV_HEADS, HEAD_DIM)
        rep = NUM_HEADS // NUM_KV_HEADS
        k = jnp.repeat(k, rep, axis=2)
        v = jnp.repeat(v, rep, axis=2)
        scale = 1.0 / np.sqrt(HEAD_DIM)
        scores = jnp.einsum('qbhd,kbhd->bhqk', q, k) * scale
        causal = jnp.tril(jnp.ones((S_, S_), bool))
        scores = jnp.where(causal, scores, jnp.asarray(-1e+30, dtype))
        attn = jax.nn.softmax(scores, axis=-1)
        attn_out = jnp.einsum('bhqk,kbhd->qbhd', attn, v).reshape(S_, B_, H_)
        proj_out = jnp.einsum('sbh,oh->sbo', attn_out, proj_weight)
        hidden_after_attn = hidden_states + proj_out
        ln2 = _layernorm(hidden_after_attn, ln2_weight, ln2_bias).reshape(-1, H_)
        T = ln2.shape[0]
        logits = ln2 @ router_weight.T
        probs = jax.nn.softmax(logits, axis=-1)
        top_p, top_i = jax.lax.top_k(probs, TOP_K)
        cap = int(np.ceil(T * TOP_K / E * CAP_FACTOR))
        exp_idx = top_i.reshape(-1)
        gate = top_p.reshape(-1).astype(dtype)
        tok = jnp.repeat(jnp.arange(T), TOP_K)
        onehot = jax.nn.one_hot(exp_idx, E, dtype=jnp.int32)
        pos = (jnp.cumsum(onehot, axis=0) * onehot).sum(-1) - 1
        keep = pos < cap
        pos_c = jnp.where(keep, pos, cap)
        buf = jnp.zeros((E, cap + 1, H_), dtype)
        buf = buf.at[exp_idx, pos_c].add(ln2[tok] * keep[:, None].astype(dtype))
        h1 = jax.nn.gelu(jnp.einsum('ech,efh->ecf', buf, moe_w1))
        h2 = jnp.einsum('ecf,ehf->ech', h1, moe_w2)
        out_ent = h2[exp_idx, pos_c] * (gate * keep.astype(dtype))[:, None]
        moe_out = jnp.zeros((T, H_), dtype).at[tok].add(out_ent)
        return hidden_after_attn + moe_out.reshape(S_, B_, H_)
    x = L0_attn_x
    xn = _layernorm(x, axis=-1)
    s = _L0_attn_ref(xn, L0_attn_Wq, L0_attn_bq, L0_attn_lnq_g, L0_attn_lnq_b, L0_attn_Wk, L0_attn_bk, L0_attn_lnk_g, L0_attn_lnk_b, L0_attn_Wv, L0_attn_bv, L0_attn_lnv_g, L0_attn_lnv_b, L0_attn_Wphi_q, L0_attn_bphi_q, L0_attn_Wphi_k, L0_attn_bphi_k, L0_attn_lna_g, L0_attn_lna_b, L0_attn_W1, L0_attn_b1, L0_attn_W2, L0_attn_b2, L0_attn_gamma, L0_attn_conv_w, L0_attn_conv_b)
    g = _silu(_L0_ffn_ref(xn, L0_ffn_ln1_weight, L0_ffn_ln1_bias, L0_ffn_ln2_weight, L0_ffn_ln2_bias, L0_ffn_qkv_weight, L0_ffn_proj_weight, L0_ffn_router_weight, L0_ffn_moe_w1, L0_ffn_moe_w2))
    x = x + s * g
    return x

_drawn_inputs = setup_inputs


def setup_inputs(seed=0):
    import zlib

    import numpy as np

    out = dict(_drawn_inputs(seed))
    spreads = {'L0_attn_bq': (0.0, 0.292),
     'L0_attn_lnq_g': (1.0, 0.6),
     'L0_attn_lnq_b': (0.0, 0.327),
     'L0_attn_bk': (0.0, 0.8),
     'L0_attn_lnk_g': (1.0, 0.6),
     'L0_attn_lnk_b': (0.0, 0.8),
     'L0_attn_bv': (0.0, 0.1),
     'L0_attn_lnv_g': (1.0, 0.2),
     'L0_attn_lnv_b': (0.0, 0.1),
     'L0_attn_lna_g': (1.0, 0.2),
     'L0_attn_lna_b': (0.0, 0.1),
     'L0_attn_b1': (0.0, 0.338),
     'L0_attn_b2': (0.0, 0.1),
     'L0_attn_conv_b': (0.0, 0.1),
     'L0_ffn_ln1_weight': (1.0, 0.2),
     'L0_ffn_ln1_bias': (0.0, 0.1),
     'L0_ffn_ln2_weight': (1.0, 0.2),
     'L0_ffn_ln2_bias': (0.0, 0.363)}
    factors = {'L0_attn_bphi_q': 8.0, 'L0_attn_bphi_k': 8.0}
    for name, (base, spread) in spreads.items():
        noise = np.random.default_rng([zlib.crc32(name.encode()), seed]).standard_normal(out[name].shape)
        drawn = base * np.exp(spread * noise) if base else spread * noise
        out[name] = jnp.asarray(drawn.astype(out[name].dtype))
    for name, factor in factors.items():
        out[name] = (out[name] * factor).astype(out[name].dtype)
    return out
```

```python
from contextlib import ExitStack

import concourse.bass as bass
from concourse import mybir

F32 = mybir.dt.float32
F32R = mybir.dt.float32r
BF16 = mybir.dt.bfloat16
I32 = mybir.dt.int32
U32 = mybir.dt.uint32
ALU = mybir.AluOpType
ACT = mybir.ActivationFunctionType
AX_X = mybir.AxisListType.X

P = 128
S, NB, E = 4, 2048, 256
HALVES = E // P
T = S * NB
TILES = T // P
BT = NB // P
H, D = 16, 16
KVH, REP = 4, 4
QKV = E + 2 * KVH * D
MLP = 1024
NX, FFN = 16, 512
CAP = 1280
SLOTS = NX * CAP
FAR = 1 << 20
EPS = 1e-5
EPS_DEN = 1e-6
GROUP = 4
GROUPS = BT // GROUP


class Step:

    def __init__(self, half, odd):
        self.half, self.odd, self.n = half, odd, half * 2 + odd

    def back(self, lag):
        turn = self.odd - lag
        return Step(self.half + turn // 2, turn % 2)


def turns(eng, count, lag, body, reach):
    lead = (reach + 1) // 2
    for t in range(2 * lead):
        body(Step(t // 2, t % 2))
    with eng.Fori(lead, count // 2) as half:
        body(Step(half, 0))
        body(Step(half, 1))
    for t in range(count, count + lag):
        body(Step(t // 2, t % 2))


def exists(step, count):
    return not isinstance(step.n, int) or 0 <= step.n < count


def later(step, k):
    return not isinstance(step.n, int) or step.n >= k


def hold(eng, sem, value, passed):
    eng.wait_ge(sem, value)
    if not isinstance(value, int):
        eng.sem_inc(passed, 1)


class Chain:

    def __init__(self, eng, sem, base=0, passed=None):
        self.eng, self.sem, self.base, self.passed, self.done = eng, sem, base, passed, 0

    def __call__(self, ins, held=None):
        ins.then_inc(self.sem, 1)
        self.done += 1
        value = self.base + self.done
        if self.passed or held:
            hold(self.eng, self.sem, value, self.passed or held)
        else:
            self.eng.wait_ge(self.sem, value)


def col(ap):
    return ap.rearrange("(j p) -> p j", p=P)


def row(ap):
    return ap.rearrange("(a n) -> a n", a=1)


def split_product(pe, dst, stationary, moving, start=True, stop=True):
    for i, ((hi, lo), (mhi, mlo)) in enumerate(zip(stationary, moving)):
        end = stop and i == len(moving) - 1
        pe.matmul(dst, hi, mhi, start=start and i == 0, stop=False)
        pe.matmul(dst, hi, mlo, start=False, stop=False)
        mm = pe.matmul(dst, lo, mhi, start=False, stop=end)
    return mm


def build(nc, a, out):
    nc.disable_value_cache = True
    ctx = ExitStack()
    with ctx:
        def sb(name, shape, dt=F32, into=ctx):
            return into.enter_context(nc.sbuf_tensor(name, shape, dt))

        def sem(name):
            return ctx.enter_context(nc.semaphore(name))

        bank = [ctx.enter_context(nc.psum_tensor(f"bank{i}", [P, 512], F32)) for i in range(8)]

        dve_passed, pool_passed, pe_passed, sp_passed, act_passed = (
            sem("dve_passed"), sem("pool_passed"), sem("pe_passed"), sem("sp_passed"), sem("act_passed"))

        ln2_d = nc.dram_tensor("ln2_d", (T, E), F32).ap()
        after_d = nc.dram_tensor("after_d", (T, E), F32).ap()
        s_d = nc.dram_tensor("s_d", (T, E), F32).ap()
        buf_d = nc.dram_tensor("buf_d", (SLOTS, E), F32).ap()
        h2_d = nc.dram_tensor("h2_d", (SLOTS + P, E), F32).ap()

        ident = sb("ident", [P, P])
        one_row = sb("one_row", [2, P], F32R)
        brow2 = sb("brow2", [2, 1536], F32R)
        ROW_Q, ROW_V, ROW_PHIK, ROW_CONV, ROW_OUT = 0, 512, 768, 1024, 1280
        diag = sb("diag", [P, P])
        headmask = sb("headmask", [P, HALVES, H])
        headmask_t = sb("headmask_t", [H, HALVES * P])
        tri = sb("tri", [P, P], BF16)
        ones_b = sb("ones_b", [P, P], BF16)
        earlier = sb("earlier", [TILES, TILES], BF16)
        iota_e = sb("iota_e", [P, H])
        neg_half = sb("neg_half", [P, 32])
        ln1w, ln1b = sb("ln1w", [P, HALVES]), sb("ln1b", [P, HALVES])
        ln2w, ln2b = sb("ln2w", [P, HALVES]), sb("ln2b", [P, HALVES])
        gate = sb("gate", [P, TILES, 2])
        to_row = sb("to_row", [P, TILES, 2], I32)
        from_row = sb("from_row", [P, TILES, 2], I32)
        wa = sb("wa", [P, HALVES, 3 * E])
        wphi = sb("wphi", [P, 2, HALVES, E])
        wconv = sb("wconv", [P, HALVES, 5, P])
        w1_s = [sb(f"w1_{w}", [P, HALVES, MLP], F32R) for w in ("hi", "lo")]
        w2_s = [sb(f"w2_{w}", [P, MLP // P, E], F32R) for w in ("hi", "lo")]
        lnq = sb("lnq", [P, 2, HALVES])
        lnk = sb("lnk", [P, 2, HALVES])
        lna = sb("lna", [P, 2, HALVES])
        bphi = sb("bphi", [P, 2, HALVES])
        phiq_bias = sb("phiq_bias", [P, HALVES])
        phik_zero = sb("phik_zero", [P, HALVES])
        b1c = sb("b1c", [P, MLP // P])
        gv_row, bv_row, ga_row = sb("gv_row", [P, E]), sb("bv_row", [P, E]), sb("ga_row", [P, E])

        front_only = ExitStack()
        wqkv = sb("wqkv", [P, HALVES, QKV], into=front_only)
        qkv_bias = sb("qkv_bias", [P, QKV], into=front_only)
        wproj = sb("wproj", [P, HALVES, E], into=front_only)
        wrouter = sb("wrouter", [P, HALVES, P], into=front_only)
        router_bias = sb("router_bias", [P, NX], into=front_only)
        top_p = sb("top_p", [P, S, BT, 2], into=front_only)
        top_e = sb("top_e", [P, S, BT, 2], into=front_only)

        with ExitStack() as own:
            w1 = sb("w1", [P, HALVES, MLP], F32, own)
            w2 = sb("w2", [P, MLP // P, E], F32, own)
            brow = sb("brow", [1, 1536], F32, own)
            brow_lo = sb("brow_lo", [1, 1536], F32R, own)
            brow_hi = sb("brow_hi", [1, 1536], F32R, own)
            extra = sb("extra", [1, 4 * E], F32, own)
            gamma = sb("gamma", [P, 1], F32, own)
            ones_f = sb("ones_f", [P, P], F32, own)
            bcast = sb("bcast", [P, 2, HALVES, P], F32, own)
            zeros = sb("zeros", [P, 4096], F32, own)
            masks_made, loaded, pool_step = sem("masks_made"), sem("loaded"), sem("pool_step")
            conv_blank, conv_in = sem("conv_blank"), sem("conv_in")
            sums_made, zero_fill, rows_split, row_two = (
                sem("sums_made"), sem("zero_fill"), sem("rows_split"), sem("row_two"))
            zeroed, phi_zero, router_in = sem("zeroed"), sem("phi_zero"), sem("router_in")
            setup_step = sem("setup_step")
            LOADS = 33

            with nc.Block() as block:
                @block.gpsimd
                def _(pool):
                    pool.memset(wconv[:], 0.0).then_inc(conv_blank, 1)
                    pool.memset(zeros[:], 0.0).then_inc(zeroed, 1)
                    step = Chain(pool, pool_step)
                    step(pool.memset(wrouter[:], 0.0))
                    pool.dma_start(wrouter[:, :, 0:NX], a["router_t"].rearrange("(j p) n -> p j n", p=P)).then_inc(router_in, 16)
                    for t in (ident, diag, headmask, headmask_t, tri, earlier, ones_f, ones_b):
                        step(pool.memset(t[:], 1.0))
                    step(pool.memset(neg_half[:], -0.5))
                    step(pool.affine_select(out=ident[:], in_=ident[:], compare_op=ALU.is_equal, fill=0.0,
                                            base=0, pattern=[[-1, P]], channel_multiplier=1))
                    step(pool.affine_select(out=tri[:], in_=tri[:], compare_op=ALU.is_gt, fill=0.0,
                                            base=0, pattern=[[1, P]], channel_multiplier=-1))
                    step(pool.affine_select(out=earlier[:], in_=earlier[:], compare_op=ALU.is_gt, fill=0.0,
                                            base=0, pattern=[[1, TILES]], channel_multiplier=-1))
                    for view, width, base in ((diag[:].rearrange("p (h d) -> p h d", d=D), [[-D, P // D], [0, D]], 0),
                                              (headmask[:], [[P, HALVES], [-D, H]], 0)):
                        step(pool.affine_select(out=view, in_=view, compare_op=ALU.is_ge, fill=0.0,
                                                base=base, pattern=width, channel_multiplier=1))
                        flipped = [[-s, n] for s, n in width]
                        step(pool.affine_select(out=view, in_=view, compare_op=ALU.is_ge, fill=0.0,
                                                base=D - 1, pattern=flipped, channel_multiplier=-1))
                    step(pool.affine_select(out=headmask_t[:], in_=headmask_t[:], compare_op=ALU.is_ge, fill=0.0,
                                            base=0, pattern=[[1, E]], channel_multiplier=-D))
                    step(pool.affine_select(out=headmask_t[:], in_=headmask_t[:], compare_op=ALU.is_ge, fill=0.0,
                                            base=D - 1, pattern=[[-1, E]], channel_multiplier=D))
                    pool.iota(iota_e[:], pattern=[[1, H]], base=0, channel_multiplier=0,
                              allow_small_or_imprecise_dtypes=True).then_inc(masks_made, 1)

                @block.sync
                def _(sp):
                    def load(dst, src):
                        sp.dma_start(dst, src).then_inc(loaded, 16)

                    load(wqkv[:], a["qkv_t"].rearrange("(j p) n -> p j n", p=P))
                    load(wproj[:], a["proj_t"].rearrange("(j p) n -> p j n", p=P))
                    for i, name in enumerate(("Wq", "Wk", "Wv")):
                        load(wa[:, :, i * E:(i + 1) * E], a[name].rearrange("(j p) n -> p j n", p=P))
                    load(wphi[:, 0], a["Wphi_q"].rearrange("(j p) n -> p j n", p=P))
                    load(wphi[:, 1], a["Wphi_k"].rearrange("(j p) n -> p j n", p=P))
                    load(w1[:], a["W1"].rearrange("(j p) n -> p j n", p=P))
                    load(w2[:], a["W2"].rearrange("(j p) n -> p j n", p=P))
                    for i, name in enumerate(("bq", "bk", "bv")):
                        load(brow[:, i * E:(i + 1) * E], row(a[name]))
                    for i, name in enumerate(("bphi_k", "conv_b", "lna_b", "b2")):
                        load(extra[:, i * E:(i + 1) * E], row(a[name]))
                    load(gamma[:], a["gamma"].to_broadcast((P, 1)))
                    for dst, name in ((gv_row, "lnv_g"), (bv_row, "lnv_b"), (ga_row, "lna_g")):
                        load(dst[:], row(a[name]).to_broadcast((P, E)))
                    sp.wait_ge(conv_blank, 1)
                    for g in range(H):
                        c = D * (g % 8)
                        sp.dma_start(wconv[c:c + D, g // 8, :, c:c + D], a["conv_t"][g]).then_inc(conv_in, 16)
                    sp.wait_ge(zeroed, 1)
                    rows = 16 * P
                    for i in range(SLOTS // rows):
                        sp.dma_start(buf_d[i * rows:(i + 1) * rows].rearrange("(p n) e -> p (n e)", p=P),
                                     zeros[:]).then_inc(zero_fill, 16)
                    sp.dma_start(h2_d[SLOTS:SLOTS + P], zeros[:, 0:E]).then_inc(zero_fill, 16)
                    sp.wait_ge(rows_split, 2)
                    sp.dma_start(brow2[0:1, :].bitcast(F32), brow_hi[:].bitcast(F32)).then_inc(row_two, 16)
                    sp.dma_start(brow2[1:2, :].bitcast(F32), brow_lo[:].bitcast(F32)).then_inc(row_two, 16)
                    sp.wait_ge(row_two, 32)
                    sp.wait_ge(zero_fill, 16 * (SLOTS // rows + 1))

                @block.scalar
                def _(act):
                    def load(dst, name):
                        with nc.allow_non_contiguous_dma(reason="vectors down the partitions"):
                            act.dma_start(dst, col(a[name])).then_inc(loaded, 16)

                    for dst, name in ((ln1w[:], "ln1_weight"), (ln1b[:], "ln1_bias"), (ln2w[:], "ln2_weight"),
                                      (ln2b[:], "ln2_bias"), (lnq[:, 0], "lnq_g"), (lnq[:, 1], "lnq_b"),
                                      (lnk[:, 0], "lnk_g"), (lnk[:, 1], "lnk_b"), (lna[:, 0], "lna_g"),
                                      (lna[:, 1], "lna_b"), (bphi[:, 0], "bphi_q"), (bphi[:, 1], "bphi_k"),
                                      (b1c[:], "b1")):
                        load(dst, name)
                    act.wait_ge(loaded, 16 * LOADS)
                    act.activation(phik_zero[:], bphi[:, 1], ACT.Tanh).then_inc(phi_zero, 1)

                @block.tensor
                def _(pe):
                    pe.wait_ge(setup_step, 5)
                    for j in range(HALVES):
                        pe.matmul(bank[0][:, 0:QKV], bcast[:, 0, j], wqkv[:, j], start=j == 0, stop=j == 1)
                    for j in range(HALVES):
                        pe.matmul(bank[1][:, 0:P], bcast[:, 1, j], wrouter[:, j], start=j == 0, stop=j == 1)
                    for n in range(HALVES):
                        for j in range(HALVES):
                            pe.matmul(bank[2][:, n:n + 1], wphi[:, 0, j, n * P:(n + 1) * P], lnq[:, 1, j:j + 1],
                                      start=j == 0, stop=j == 1)
                    for j in range(HALVES):
                        pe.matmul(bank[3][0:1, 0:E], lnk[:, 1, j:j + 1], wphi[:, 1, j], start=j == 0, stop=j == 1)
                    for n in range(MLP // P):
                        for j in range(HALVES):
                            last = pe.matmul(bank[4][:, n:n + 1], w1[:, j, n * P:(n + 1) * P], lna[:, 1, j:j + 1],
                                             start=j == 0, stop=j == 1)
                    last.then_inc(sums_made, 1)

                @block.vector
                def _(dve):
                    step = Chain(dve, setup_step)
                    dve.wait_ge(loaded, 16 * LOADS)
                    dve.wait_ge(router_in, 16)
                    dve.wait_ge(masks_made, 1)
                    for i, b in enumerate((ln1b, ln2b)):
                        for j in range(HALVES):
                            step(dve.tensor_scalar(bcast[:, i, j], ones_f[:], b[:, j:j + 1], None, ALU.mult))
                    step(dve.tensor_copy(one_row[:], ones_f[0:2, :]))
                    dve.wait_ge(sums_made, 1)
                    step(dve.tensor_copy(qkv_bias[:], bank[0][:, 0:QKV]))
                    step(dve.tensor_copy(router_bias[:], bank[1][:, 0:NX]))
                    step(dve.tensor_tensor(phiq_bias[:], bank[2][:, 0:HALVES], bphi[:, 0], ALU.add))
                    step(dve.tensor_tensor(brow[:, ROW_PHIK:ROW_PHIK + E], bank[3][0:1, 0:E], extra[:, 0:E], ALU.add))
                    step(dve.tensor_tensor(b1c[:], bank[4][:, 0:MLP // P], b1c[:], ALU.add))
                    step(dve.tensor_scalar(brow[:, ROW_CONV:ROW_CONV + E], extra[:, E:2 * E], gamma[0:1, 0:1], None, ALU.mult))
                    step(dve.tensor_tensor(brow[:, ROW_OUT:ROW_OUT + E], extra[:, 2 * E:3 * E], extra[:, 3 * E:4 * E], ALU.add))
                    for j in range(HALVES):
                        for w, g in ((wqkv, ln1w), (wrouter, ln2w)):
                            step(dve.tensor_scalar(w[:, j], w[:, j], g[:, j:j + 1], None, ALU.mult))
                        for w, g in ((wphi[:, 0], lnq[:, 0]), (wphi[:, 1], lnk[:, 0]), (w1, lna[:, 0])):
                            step(dve.tensor_scalar(w[:, j], w[:, j], g[:, j:j + 1], None, ALU.mult))
                    for w, (hi, lo) in ((w1, w1_s), (w2, w2_s)):
                        step(dve.tensor_copy(hi[:], w[:]))
                        step(dve.tensor_tensor(lo[:], w[:], hi[:], ALU.subtract))
                    dve.wait_ge(conv_in, 16 * H)
                    step(dve.tensor_scalar(wconv[:], wconv[:], gamma[:, 0:1], None, ALU.mult))
                    for j in range(HALVES):
                        step(dve.tensor_tensor(wconv[:, j, 2], wconv[:, j, 2], ident[:], ALU.add))
                    dve.tensor_copy(brow_hi[:], brow[:]).then_inc(rows_split, 1)
                    dve.wait_ge(rows_split, 1)
                    dve.tensor_tensor(brow_lo[:], brow[:], brow_hi[:], ALU.subtract).then_inc(rows_split, 1)
                    dve.wait_ge(phi_zero, 1)
                    step(dve.tensor_scalar(phik_zero[:], phik_zero[:], 1.0, None, ALU.add))

        with ExitStack() as own:
            x = [sb(f"x{p}", [P, S, E], F32, own) for p in range(2)]
            xn = [sb(f"xn{p}", [P, S, E], F32, own) for p in range(2)]
            stats = sb("stats", [P, S, 6], F32, own)
            mv = [sb(f"mv{p}", [P, S, 2], F32, own) for p in range(2)]
            norm = [sb(f"norm{p}", [P, 8, S], F32, own) for p in range(2)]
            xnt = sb("xnt", [P, HALVES, S * P], F32, own)
            qkv = [sb(f"qkv{p}", [P, S, QKV], F32, own) for p in range(2)]
            prod = sb("prod", [P, 10, E], F32, own)
            weighed = sb("weighed", [P, 7, E], F32, own)
            score = sb("score", [P, S, H, S], F32, own)
            shifted = sb("shifted", [P, S, H, S], F32, own)
            prob = sb("prob", [P, S, H, S], F32, own)
            top = sb("top", [P, S * H], F32, own)
            total = sb("total", [P, S * H], F32, own)
            att = [sb(f"att{p}", [P, S, E], F32, own) for p in range(2)]
            attt = sb("attt", [P, HALVES, S * P], F32, own)
            after = [sb(f"after{p}", [P, S, E], F32, own) for p in range(2)]
            stats2 = sb("stats2", [P, S, 6], F32, own)
            mv2 = [sb(f"mv2{p}", [P, S, 2], F32, own) for p in range(2)]
            norm2 = [sb(f"norm2{p}", [P, 4, S], F32, own) for p in range(2)]
            ln2 = [sb(f"ln2{p}", [P, S, E], F32, own) for p in range(2)]
            ln2t = sb("ln2t", [P, HALVES, S * P], F32, own)
            logit = sb("logit", [P, S, NX], F32, own)
            rprob = sb("rprob", [P, S, NX], F32, own)
            rtop = sb("rtop", [P, S], F32, own)
            rsum = sb("rsum", [P, S], F32, own)
            best = sb("best", [P, S, 8], F32, own)
            best_e = sb("best_e", [P, S, 8], U32, own)

            PAIRS = [(s, t) for s in range(S) for t in range(s + 1)]
            x_in = [sem("x_in0"), sem("x_in1")]
            x_stats, x_mv, x_norm, xn_made = sem("x_stats"), sem("x_mv"), sem("x_norm"), sem("xn_made")
            xn_turned, xnt_made = sem("xn_turned"), sem("xnt_made")
            qkv_done, qkv_made = sem("qkv_done"), sem("qkv_made")
            mha_step, score_ready, exp_done, prob_made = sem("mha_step"), sem("score_ready"), sem("exp_done"), sem("prob_made")
            weighed_made = sem("weighed_made")
            att_turned, attt_made, proj_done, after_made = sem("att_turned"), sem("attt_made"), sem("proj_done"), sem("after_made")
            a_stats, a_mv, a_norm, ln2_made = sem("a_stats"), sem("a_mv"), sem("a_norm"), sem("ln2_made")
            ln2_turned, ln2t_made, router_done = sem("ln2_turned"), sem("ln2t_made"), sem("router_done")
            router_step, rexp_done = sem("router_step"), sem("rexp_done")
            ln2_out, after_out = [sem("ln2_out0"), sem("ln2_out1")], [sem("after_out0"), sem("after_out1")]
            masked_out = sem("masked_out")
            X_NORM, A_NORM = 8, 4
            MHA, ROUTE = 9, 10

            def rows_of(dram, step):
                return dram.rearrange("(s b p) e -> p b s e", s=S, p=P)[:, bass.ds(step.n, 1)].rearrange("p b s e -> p (b s) e")

            with nc.Block() as block:
                @block.sync
                def _(sp):
                    def turn(t):
                        if exists(t, BT):
                            if later(t, 2):
                                sp.wait_ge(xn_made, t.n * S - S)
                            sp.dma_start(x[t.odd][:], rows_of(a["x"], t)).then_inc(x_in[t.odd], 16)
                        t = t.back(3)
                        if exists(t, BT):
                            sp.wait_ge(after_made, t.n * 2 + 2)
                            sp.dma_start(rows_of(after_d, t), after[t.odd][:]).then_inc(after_out[t.odd], 16)
                            sp.wait_ge(ln2_made, t.n * S + S)
                            sp.dma_start(rows_of(ln2_d, t), ln2[t.odd][:]).then_inc(ln2_out[t.odd], 16)
                    turns(sp, BT, 3, turn, 5)
                    for q in (*ln2_out, *after_out):
                        sp.wait_ge(q, 16 * BT // 2)

                @block.gpsimd
                def _(pool):
                    def inverse_root(out_, var, eps, step, tmp):
                        step(pool.tensor_scalar(tmp, var, eps, None, ALU.add))
                        step(pool.tensor_tensor(out_, tmp, neg_half[:, 0:S], ALU.pow))

                    def turn(t0):
                        t = t0
                        if exists(t, BT):
                            mean, var = mv[t.odd][:, :, 0], mv[t.odd][:, :, 1]
                            n = norm[t.odd]
                            hold(pool, x_mv, t.n * S + S, pool_passed)
                            step = Chain(pool, x_norm, t.n * X_NORM, pool_passed)
                            inverse_root(n[:, 0], var, EPS, step, n[:, 3])
                            step(pool.tensor_tensor(n[:, 4], mean, n[:, 0], ALU.mult))
                            step(pool.tensor_scalar(n[:, 1], n[:, 4], -1.0, None, ALU.mult))
                            step(pool.tensor_tensor(n[:, 5], n[:, 0], n[:, 0], ALU.mult))
                            step(pool.tensor_tensor(n[:, 6], n[:, 5], var, ALU.mult))
                            inverse_root(n[:, 2], n[:, 6], EPS, step, n[:, 7])
                        t = t0.back(2)
                        if exists(t, BT):
                            mean, var = mv2[t.odd][:, :, 0], mv2[t.odd][:, :, 1]
                            n = norm2[t.odd]
                            hold(pool, a_mv, t.n * S + S, pool_passed)
                            step = Chain(pool, a_norm, t.n * A_NORM, pool_passed)
                            inverse_root(n[:, 0], var, EPS, step, n[:, 2])
                            step(pool.tensor_tensor(n[:, 3], mean, n[:, 0], ALU.mult))
                            step(pool.tensor_scalar(n[:, 1], n[:, 3], -1.0, None, ALU.mult))
                        t = t0.back(1)
                        if exists(t, BT):
                            pool.wait_ge(prob_made, t.n + 1)
                            if later(t, 1):
                                pool.wait_ge(mha_step, t.n * MHA)
                            for i, (s, u) in enumerate(PAIRS[3:]):
                                value = qkv[t.odd][:, u, E + KVH * D:].rearrange("p (g d) -> p g d", d=D)
                                pool.tensor_tensor(
                                    weighed[:, i].rearrange("p (g r d) -> p g r d", r=REP, d=D),
                                    value.unsqueeze(2).to_broadcast((P, KVH, REP, D)),
                                    prob[:, s, :, u].rearrange("p (g r) -> p g r", r=REP).unsqueeze(3).to_broadcast((P, KVH, REP, D)),
                                    ALU.mult).then_inc(weighed_made, 1)
                    turns(pool, BT, 2, turn, 4)

                @block.scalar
                def _(act):
                    def turn(t0):
                        t = t0.back(2)
                        if exists(t, BT):
                            act.wait_ge(att_turned, t.n + 1)
                            if later(t, 1):
                                act.wait_ge(proj_done, t.n * 2)
                            for j in range(HALVES):
                                act.activation(attt[:, j], bank[2 + j][:], ACT.Copy).then_inc(attt_made, 1)
                        t = t0.back(3)
                        if exists(t, BT):
                            act.wait_ge(ln2_turned, t.n + 1)
                            if later(t, 1):
                                act.wait_ge(router_done, t.n)
                            for j in range(HALVES):
                                act.activation(ln2t[:, j], bank[2 + j][:], ACT.Copy).then_inc(ln2t_made, 1)
                        t = t0.back(1)
                        if exists(t, BT):
                            act.wait_ge(score_ready, t.n + 1)
                            act.activation(prob[:], shifted[:], ACT.Exp, scale=float(D) ** -0.5).then_inc(exp_done, 1)
                        t = t0.back(3)
                        if exists(t, BT):
                            act.wait_ge(router_step, t.n * ROUTE + 3)
                            act.activation(rprob[:], logit[:], ACT.Exp).then_inc(rexp_done, 1)
                        t = t0
                        if exists(t, BT):
                            act.wait_ge(x_norm, t.n * X_NORM + 4)
                            if later(t, 2):
                                act.wait_ge(after_made, t.n * 2 - 2)
                            for s in range(S):
                                act.activation(xn[t.odd][:, s], x[t.odd][:, s], ACT.Identity,
                                               bias=norm[t.odd][:, 1, s:s + 1], scale=norm[t.odd][:, 0, s:s + 1]).then_inc(xn_made, 1)
                        t = t0.back(2)
                        if exists(t, BT):
                            act.wait_ge(a_norm, t.n * A_NORM + A_NORM)
                            if later(t, 2):
                                act.wait_ge(ln2_out[t.odd], t.half * 16)
                                act.wait_ge(ln2_turned, t.n - 1)
                            for s in range(S):
                                act.activation(ln2[t.odd][:, s], after[t.odd][:, s], ACT.Identity,
                                               bias=norm2[t.odd][:, 1, s:s + 1], scale=norm2[t.odd][:, 0, s:s + 1]).then_inc(ln2_made, 1)
                        t = t0
                        if exists(t, BT):
                            act.wait_ge(xn_turned, t.n + 1)
                            if later(t, 1):
                                act.wait_ge(qkv_done, t.n * S)
                            for j in range(HALVES):
                                act.activation(xnt[:, j], bank[j][:], ACT.Copy).then_inc(xnt_made, 1)
                    turns(act, BT, 3, turn, 5)

                @block.tensor
                def _(pe):
                    def turned(src, banks, done):
                        for j in range(HALVES):
                            for s in range(S):
                                last = pe.transpose(banks[j][:, s * P:(s + 1) * P], src[:, s, j * P:(j + 1) * P], ident[:])
                        last.then_inc(done, 1)

                    def turn(t0):
                        t = t0.back(1)
                        if exists(t, BT):
                            pe.wait_ge(xnt_made, t.n * 2 + 2)
                            for s in range(S):
                                if s == 0 and later(t, 3):
                                    pe.wait_ge(router_step, t.n * ROUTE - 3 * ROUTE + 1)
                                if s >= 2 or later(t, 1):
                                    pe.wait_ge(qkv_made, t.n * S + s - 1)
                                for j in range(HALVES):
                                    mm = pe.matmul(bank[4 + s % 2][:, 0:QKV], xnt[:, j, s * P:(s + 1) * P], wqkv[:, j],
                                                   start=j == 0, stop=j == 1)
                                mm.then_inc(qkv_done, 1)
                        t = t0.back(2)
                        if exists(t, BT):
                            pe.wait_ge(mha_step, t.n * MHA + MHA)
                            if later(t, 2):
                                pe.wait_ge(ln2t_made, t.n * 2 - 2)
                            turned(att[t.odd], bank[2:4], att_turned)
                        t = t0.back(2)
                        if exists(t, BT):
                            pe.wait_ge(attt_made, t.n * 2 + 2)
                            if later(t, 1):
                                pe.wait_ge(after_made, t.n * 2)
                            for s in range(S):
                                for j in range(HALVES):
                                    mm = pe.matmul(bank[6 + s // 2][:, s % 2 * E:(s % 2 + 1) * E], attt[:, j, s * P:(s + 1) * P],
                                                   wproj[:, j], start=j == 0, stop=j == 1)
                                if s % 2:
                                    mm.then_inc(proj_done, 1)
                        t = t0.back(3)
                        if exists(t, BT):
                            pe.wait_ge(ln2_made, t.n * S + S)
                            if exists(t.back(-1), BT):
                                pe.wait_ge(attt_made, t.n * 2 + 4)
                            turned(ln2[t.odd], bank[2:4], ln2_turned)
                            pe.wait_ge(ln2t_made, t.n * 2 + 2)
                            pe.wait_ge(qkv_made, MIN_QKV(t))
                            for s in range(S):
                                for j in range(HALVES):
                                    mm = pe.matmul(bank[4][:, s * P:(s + 1) * P], ln2t[:, j, s * P:(s + 1) * P], wrouter[:, j],
                                                   start=j == 0, stop=j == 1)
                            mm.then_inc(router_done, 1)
                        t = t0
                        if exists(t, BT):
                            pe.wait_ge(xn_made, t.n * S + S)
                            if later(t, 1):
                                pe.wait_ge(xnt_made, t.n * 2)
                            turned(xn[t.odd], bank[0:2], xn_turned)

                    def MIN_QKV(t):
                        ahead = t.back(-2)
                        if not exists(ahead, BT):
                            return BT * S
                        return ahead.n * S + S
                    turns(pe, BT, 3, turn, 5)

                @block.vector
                def _(dve):
                    dve.memset(score[:], -1e30).then_inc(masked_out, 1)
                    dve.wait_ge(masked_out, 1)

                    def moments(src, tmp, dst, done_stats, done, t):
                        if later(t, 1):
                            dve.wait_ge(done, t.n * S)
                        for s in range(S):
                            dve.bn_stats(tmp[:, s], src[:, s]).then_inc(done_stats, 1)
                        hold(dve, done_stats, t.n * S + S, dve_passed)
                        for s in range(S):
                            dve.bn_aggr(dst[:, s], tmp[:, s]).then_inc(done, 1)

                    def front_stats(t):
                        dve.wait_ge(x_in[t.odd], t.half * 16 + 16)
                        moments(x[t.odd], stats, mv[t.odd], x_stats, x_mv, t)

                    def residual(t):
                        if later(t, 2):
                            dve.wait_ge(after_out[t.odd], t.half * 16)
                            dve.wait_ge(ln2_made, t.n * S - S)
                        for k in range(2):
                            dve.wait_ge(proj_done, t.n * 2 + k + 1)
                            dve.tensor_tensor(after[t.odd][:, 2 * k:2 * k + 2], bank[6 + k][:].rearrange("p (s e) -> p s e", s=2),
                                              xn[t.odd][:, 2 * k:2 * k + 2], ALU.add).then_inc(after_made, 1)
                        dve.wait_ge(after_made, t.n * 2 + 2)
                        moments(after[t.odd], stats2, mv2[t.odd], a_stats, a_mv, t)

                    def attention(t):
                        q = qkv[t.odd]
                        for s in range(S):
                            dve.wait_ge(qkv_done, t.n * S + s + 1)
                            if s == 0:
                                dve.wait_ge(x_norm, t.n * X_NORM + X_NORM)
                            dve.scalar_tensor_tensor(q[:, s], bank[4 + s % 2][:, 0:QKV], norm[t.odd][:, 2, s:s + 1], qkv_bias[:],
                                                     ALU.mult, ALU.add).then_inc(qkv_made, 1)
                        dve.wait_ge(qkv_made, t.n * S + S)
                        step = Chain(dve, mha_step, t.n * MHA)
                        if later(t, 1):
                            dve.wait_ge(mha_step, t.n * MHA)
                        for i, (s, u) in enumerate(PAIRS):
                            key = q[:, u, E:E + KVH * D].rearrange("p (g d) -> p g d", d=D).unsqueeze(2).to_broadcast((P, KVH, REP, D))
                            mul = dve.tensor_tensor(prod[:, i].rearrange("p (g r d) -> p g r d", r=REP, d=D),
                                                    q[:, s, 0:E].rearrange("p (g r d) -> p g r d", r=REP, d=D), key, ALU.mult)
                        step(mul)
                        for s in range(S):
                            first = PAIRS.index((s, 0))
                            red = dve.tensor_reduce(score[:, s, :, 0:s + 1].rearrange("p h u -> p u h"),
                                                    prod[:, first:first + s + 1].rearrange("p u (h d) -> p u h d", d=D), AX_X, ALU.add)
                        step(red)
                        step(dve.tensor_reduce(top[:], score[:].rearrange("p s h u -> p (s h) u"), AX_X, ALU.max))
                        dve.tensor_tensor(shifted[:].rearrange("p s h u -> p (s h) u"), score[:].rearrange("p s h u -> p (s h) u"),
                                          top[:].unsqueeze(2).to_broadcast((P, S * H, S)), ALU.subtract).then_inc(score_ready, 1)
                        return step

                    def weigh(t, step):
                        dve.wait_ge(exp_done, t.n + 1)
                        flat = prob[:].rearrange("p s h u -> p (s h) u")
                        step(dve.tensor_reduce(total[:], flat, AX_X, ALU.add))
                        step(dve.reciprocal(total[:], total[:]))
                        dve.tensor_tensor(flat, flat, total[:].unsqueeze(2).to_broadcast((P, S * H, S)), ALU.mult).then_inc(prob_made, 1)
                        dve.wait_ge(prob_made, t.n + 1)
                        for i, (s, u) in enumerate(PAIRS[:3]):
                            value = qkv[t.odd][:, u, E + KVH * D:].rearrange("p (g d) -> p g d", d=D)
                            mul = dve.tensor_tensor(
                                (att[t.odd][:, 0] if s == 0 else prod[:, i]).rearrange("p (g r d) -> p g r d", r=REP, d=D),
                                value.unsqueeze(2).to_broadcast((P, KVH, REP, D)),
                                prob[:, s, :, u].rearrange("p (g r) -> p g r", r=REP).unsqueeze(3).to_broadcast((P, KVH, REP, D)),
                                ALU.mult)
                        step(mul)
                        step(dve.tensor_tensor(att[t.odd][:, 1], prod[:, 1], prod[:, 2], ALU.add))

                    def weigh_rest(t, step):
                        dve.wait_ge(weighed_made, t.n * 7 + 3)
                        step(dve.tensor_reduce(att[t.odd][:, 2], weighed[:, 0:3].rearrange("p u c -> p c u"), AX_X, ALU.add))
                        dve.wait_ge(weighed_made, t.n * 7 + 7)
                        step(dve.tensor_reduce(att[t.odd][:, 3], weighed[:, 3:7].rearrange("p u c -> p c u"), AX_X, ALU.add))

                    def route_scores(t):
                        step = Chain(dve, router_step, t.n * ROUTE)
                        dve.wait_ge(router_done, t.n + 1)
                        step(dve.tensor_tensor(logit[:], bank[4][:].rearrange("p (s n) -> p s n", s=S)[:, :, 0:NX],
                                               router_bias[:].unsqueeze(1).to_broadcast((P, S, NX)), ALU.add))
                        step(dve.tensor_reduce(rtop[:], logit[:], AX_X, ALU.max))
                        step(dve.tensor_tensor(logit[:], logit[:], rtop[:].unsqueeze(2).to_broadcast((P, S, NX)), ALU.subtract))
                        return step

                    def pick(t, step):
                        dve.wait_ge(rexp_done, t.n + 1)
                        step(dve.tensor_reduce(rsum[:], rprob[:], AX_X, ALU.add))
                        step(dve.reciprocal(rsum[:], rsum[:]))
                        step(dve.tensor_tensor(rprob[:], rprob[:], rsum[:].unsqueeze(2).to_broadcast((P, S, NX)), ALU.mult), dve_passed)
                        for s in range(S):
                            largest = dve.max(best[:, s], rprob[:, s])
                        step(largest, dve_passed)
                        for s in range(S):
                            at = dve.max_index(best_e[:, s], best[:, s], rprob[:, s])
                        step(at)
                        for dst, src in ((top_p, best), (top_e, best_e)):
                            step(dve.tensor_copy(dst[:, :, bass.ds(t.n, 1), :].rearrange("p s b k -> p (s b) k"), src[:, :, 0:2]))

                    def turn(t0):
                        if exists(t0, BT):
                            front_stats(t0)
                        if exists(t0.back(1), BT):
                            mha = attention(t0.back(1))
                        if exists(t0.back(2), BT):
                            residual(t0.back(2))
                        if exists(t0.back(3), BT):
                            route = route_scores(t0.back(3))
                        if exists(t0.back(1), BT):
                            weigh(t0.back(1), mha)
                        if exists(t0.back(3), BT):
                            pick(t0.back(3), route)
                            assert route.done == ROUTE, route.done
                        if exists(t0.back(1), BT):
                            weigh_rest(t0.back(1), mha)
                            assert mha.done == MHA, mha.done
                    turns(dve, BT, 3, turn, 5)

        with ExitStack() as own:
            hot = [sb(f"hot{k}", [P, TILES, NX], F32, own) for k in range(2)]
            chosen = sb("chosen", [P, TILES, NX], BF16, own)
            counts = sb("counts", [TILES, NX], F32, own)
            before = sb("before", [TILES, TILES, NX], BF16, own)
            place = sb("place", [P, TILES, NX], F32, own)
            pos = sb("pos", [P, TILES, 2], F32, own)
            keep = sb("keep", [P, TILES, 2], F32, own)
            slot = sb("slot", [P, TILES, 2], F32, own)
            route_step, counted, placed = sem("route_step"), sem("counted"), sem("placed")
            experts_of = top_e[:].rearrange("p s b k -> p (s b) k")
            probs_of = top_p[:].rearrange("p s b k -> p (s b) k")

            with nc.Block() as block:
                @block.tensor
                def _(pe):
                    pe.wait_ge(route_step, 3)
                    for e in range(NX):
                        mm = pe.matmul(bank[0][0:TILES, e:e + 1], chosen[:, :, e], ones_b[:, 0:1], start=True, stop=True)
                    mm.then_inc(counted, 1)
                    for half in range(2):
                        pe.matmul(bank[1 + half][:], tri[:], chosen[:, half * 32:half * 32 + 32].rearrange("p t e -> p (t e)"),
                                  start=True, stop=False)
                    pe.wait_ge(route_step, 5)
                    for half in range(2):
                        mm = pe.matmul(bank[1 + half][:], ones_b[0:TILES, :],
                                       before[:, half * 32:half * 32 + 32].rearrange("p t e -> p (t e)"), start=False, stop=True)
                    mm.then_inc(placed, 1)

                @block.vector
                def _(dve):
                    step = Chain(dve, route_step)
                    for k in range(2):
                        step(dve.tensor_tensor(hot[k][:], iota_e[:].unsqueeze(1).to_broadcast((P, TILES, NX)),
                                               experts_of[:, :, k].unsqueeze(2).to_broadcast((P, TILES, NX)), ALU.is_equal))
                    step(dve.tensor_tensor(chosen[:], hot[0][:], hot[1][:], ALU.add))
                    dve.wait_ge(counted, 1)
                    step(dve.tensor_copy(counts[:], bank[0][0:TILES, 0:NX]))
                    step(dve.tensor_tensor(before[:], earlier[:].unsqueeze(2).to_broadcast((TILES, TILES, NX)),
                                           counts[:].unsqueeze(1).to_broadcast((TILES, TILES, NX)), ALU.mult))
                    dve.wait_ge(placed, 1)
                    for k in range(2):
                        for half in range(2):
                            part = slice(half * 32, half * 32 + 32)
                            mul = dve.tensor_tensor(place[:, part], bank[1 + half][:].rearrange("p (t e) -> p t e", e=NX),
                                                    hot[k][:, part], ALU.mult)
                        step(mul)
                        step(dve.tensor_reduce(pos[:, :, k], place[:], AX_X, ALU.add))
                    step(dve.tensor_scalar(keep[:], pos[:], float(CAP), None, ALU.is_lt))
                    step(dve.scalar_tensor_tensor(slot[:], experts_of, float(CAP), pos[:], ALU.mult, ALU.add))
                    step(dve.tensor_tensor(gate[:], probs_of, keep[:], ALU.mult))
                    for dst, other in ((to_row, FAR), (from_row, SLOTS)):
                        step(dve.scalar_tensor_tensor(pos[:], slot[:], float(-other), keep[:], ALU.add, ALU.mult))
                        step(dve.tensor_scalar(dst[:], pos[:], float(other), None, ALU.add))

        front_only.close()
        with ExitStack() as own:
            xa = [sb(f"xa{p}", [P, GROUP, E], F32, own) for p in range(2)]
            xstats = sb("xstats", [P, GROUP, 6], F32, own)
            xmv = [sb(f"xmv{p}", [P, GROUP, 2], F32, own) for p in range(2)]
            xnorm = [sb(f"xnorm{p}", [P, 4, GROUP], F32, own) for p in range(2)]
            xnb = sb("xnb", [P, BT, E], F32, own)
            xtile = [sb(f"xtile{p}", [P, HALVES, P], F32, own) for p in range(2)]
            qstats = sb("qstats", [P, 3, 6], F32, own)
            qmv = [sb(f"qmv{p}", [P, 3, 2], F32, own) for p in range(2)]
            qnorm = [sb(f"qnorm{p}", [P, 4, 3], F32, own) for p in range(2)]
            qkn = [sb(f"qkn{p}", [P, 2 * E], F32, own) for p in range(2)]
            vn = sb("vn", [P, BT, HALVES, P + 1], F32, own)
            knt = sb("knt", [P, HALVES, NB + 4], F32, own)
            attnt = knt
            qpart = sb("qpart", [P, HALVES, BT], F32, own)
            tk = sb("tk", [P, BT, E], F32, own)
            tq = sb("tq", [P, HALVES, NB], F32, own)
            qmean = sb("qmean", [P, HALVES], F32, own)
            qmean_k = sb("qmean_k", [P, HALVES], F32, own)
            qheads = sb("qheads", [P, HALVES, H], F32, own)
            qheads_k = sb("qheads_k", [P, HALVES, H], F32, own)
            small = sb("small", [H, 24], F32, own)
            alpha = sb("alpha", [P, BT, H], F32, own)
            spread = sb("spread", [P, HALVES, 2], F32, own)
            pks = [sb(f"pks{p}", [P, E], F32, own) for p in range(2)]
            kvt = sb("kvt", [P, P], F32, own)
            ksum = sb("ksum", [P, HALVES, 2], F32, own)
            kvblk = sb("kvblk", [P, HALVES, P + 8], F32, own)
            den = sb("den", [P, HALVES, 8], F32, own)
            attn = [sb(f"attn{p}", [P, E], F32, own) for p in range(2)]
            cstats = sb("cstats", [P, 6], F32, own)
            cmv = [sb(f"cmv{p}", [P, 2], F32, own) for p in range(2)]
            cnorm = [sb(f"cnorm{p}", [P, 4], F32, own) for p in range(2)]
            an = [sb(f"an{p}", [P, E], F32, own) for p in range(2)]
            gained = sb("gained", [P, E], F32, own)
            PAIR = 2
            ant_s = [[sb(f"ant_{w}{p}", [P, HALVES, PAIR * P], F32R, own) for w in ("hi", "lo")] for p in range(2)]
            gel = sb("gel", [P, 4, PAIR * P], F32, own)
            gel_s = [sb(f"gel_{w}", [P, MLP // P, PAIR * P], F32R, own) for w in ("hi", "lo")]
            alpha_t = sb("alpha_t", [H, NB], F32, own)
            sout = [sb(f"sout{p}", [P, E], F32, own) for p in range(2)]
            lt = [sb(f"lt{p}", [P, E], F32, own) for p in range(2)]
            where = sb("where", [P, BT, 2], I32, own)

            ax_in = [sem("ax_in0"), sem("ax_in1")]
            ax_stats, ax_mv, ax_norm, axn_made = sem("ax_stats"), sem("ax_mv"), sem("ax_norm"), sem("axn_made")
            xt_done, xt_made = sem("xt_done"), sem("xt_made")
            aq_done, aq_stats, aq_mv, aq_norm, qkvn_made = (
                sem("aq_done"), sem("aq_stats"), sem("aq_mv"), sem("aq_norm"), sem("qkvn_made"))
            qkt_done, qt_made, kt_made = sem("qkt_done"), sem("qt_made"), sem("kt_made")
            phik_done, tk_made, phiq_done, tq_made = sem("phik_done"), sem("tk_made"), sem("phiq_done"), sem("tq_made")
            mean_step, score_done, max_step, alpha_exp, norm_step = (
                sem("mean_step"), sem("score_done"), sem("max_step"), sem("alpha_exp"), sem("norm_step"))
            alpha_turned, alpha_made, pks_made, kv_done, kv_step = (
                sem("alpha_turned"), sem("alpha_made"), sem("pks_made"), sem("kv_done"), sem("kv_step"))
            tq_plus, nd_done, attn_step, attn_turned, attnt_made = (
                sem("tq_plus"), sem("nd_done"), sem("attn_step"), sem("attn_turned"), sem("attnt_made"))
            conv_done, c_stats, c_mv, c_norm, an_made, res_step = (
                sem("conv_done"), sem("c_stats"), sem("c_mv"), sem("c_norm"), sem("an_made"), sem("res_step"))
            an_turned, ant_made, up_done, gel_made, down_done, s_made = (
                sem("an_turned"), sem("ant_made"), sem("up_done"), sem("gel_made"), sem("down_done"), sem("s_made"))
            s_out = [sem("s_out0"), sem("s_out1")]
            lt_in, scattered, where_made = [sem("lt_in0"), sem("lt_in1")], [sem("scattered0"), sem("scattered1")], sem("where_made")
            ant_high, gel_split = sem("ant_high"), sem("gel_split")
            vn_ones = sem("vn_ones")
            ends_zero = sem("ends_zero")
            F_CHUNKS = MLP // P
            PHI_BANKS = ((6, 7), (6, 7), (2, 3), (4, 5))
            PAIRS_A = BT // PAIR
            MEANS, MAXS, NORMS, KVS = 10, 7, 4, 14

            with nc.Block() as block:
                @block.sync
                def _(sp):
                    with sp.Fori(0, S) as b:
                        def load_x(g):
                            if g >= 2:
                                hold(sp, axn_made, b * BT + (g - 1) * GROUP, sp_passed)
                            sp.dma_start(xa[g % 2][:], a["x"].rearrange("(b g i p) e -> p (b g) i e", b=S, g=GROUPS, p=P)
                                         [:, bass.ds(b * GROUPS + g, 1)].rearrange("p a i e -> p (a i) e")).then_inc(ax_in[g % 2], 16)

                        load_x(0)
                        load_x(1)
                        load_x(2)
                        load_x(3)
                        for i in range(BT + 6):
                            if i < BT:
                                if i >= 2:
                                    hold(sp, scattered[i % 2], b * (BT // 2 * 32) + i // 2 * 32, sp_passed)
                                sp.dma_start(lt[i % 2][:], ln2_d.rearrange("(t p) e -> p t e", p=P)[:, bass.ds(b * BT + i, 1)]
                                             .rearrange("p a e -> p (a e)")).then_inc(lt_in[i % 2], 16)
                            i -= 6
                            if i >= 0:
                                hold(sp, s_made, b * BT + i + 1, sp_passed)
                                sp.dma_start(s_d.rearrange("(t p) e -> p t e", p=P)[:, bass.ds(b * BT + i, 1)]
                                             .rearrange("p a e -> p (a e)"), sout[i % 2][:]).then_inc(s_out[i % 2], 16)
                        for q in scattered:
                            hold(sp, q, b * (BT // 2 * 32) + BT // 2 * 32, sp_passed)
                    for q in s_out:
                        sp.wait_ge(q, 16 * TILES // 2)

                @block.gpsimd
                def _(pool):
                    pool.memset(vn[:, :, :, P:P + 1].rearrange("p i j c -> p (i j) c"), 1.0).then_inc(vn_ones, 1)

                    def inverse_root(n, mv_, step):
                        width = n[0].shape[-1]
                        step(pool.tensor_scalar(n[2], mv_[1], EPS, None, ALU.add))
                        step(pool.tensor_tensor(n[0], n[2], neg_half[:, 0:width], ALU.pow))
                        step(pool.tensor_tensor(n[3], mv_[0], n[0], ALU.mult))
                        step(pool.tensor_scalar(n[1], n[3], -1.0, None, ALU.mult))

                    with pool.Fori(0, S) as b:
                        def norm_x(g):
                            hold(pool, ax_mv, b * BT + g * GROUP + GROUP, pool_passed)
                            inverse_root([xnorm[g % 2][:, k] for k in range(4)], [xmv[g % 2][:, :, k] for k in range(2)],
                                         Chain(pool, ax_norm, b * 4 * GROUPS + 4 * g, pool_passed))

                        def scatter(i):
                            if i >= 2:
                                hold(pool, scattered[i % 2], b * (BT // 2 * 32) + i // 2 * 32, pool_passed)
                            hold(pool, lt_in[i % 2], b * (BT // 2 * 16) + i // 2 * 16 + 16, pool_passed)
                            for k in range(2):
                                pool.indirect_dma_start(buf_d, bass.IndirectOffsetOnAxis(where[:, i, k:k + 1], axis=0),
                                                        lt[i % 2][:], None, bounds_check=SLOTS - 1,
                                                        oob_is_err=False).then_inc(scattered[i % 2], 16)

                        pool.tensor_copy(where[:], to_row[:, bass.ds(b * BT, BT)]).then_inc(where_made, 1)
                        norm_x(0)
                        for i in range(BT + 2):
                            if i % 4 == 1 and i // 4 + 1 < GROUPS:
                                norm_x(i // 4 + 1)
                            if 1 <= i <= BT:
                                k = i - 1
                                hold(pool, aq_mv, b * (3 * BT) + 3 * k + 3, pool_passed)
                                inverse_root([qnorm[k % 2][:, r] for r in range(4)], [qmv[k % 2][:, :, r] for r in range(2)],
                                             Chain(pool, aq_norm, b * (4 * BT) + 4 * k, pool_passed))
                        hold(pool, where_made, b + 1, pool_passed)
                        for i in range(BT):
                            hold(pool, c_mv, b * BT + i + 1, pool_passed)
                            inverse_root([cnorm[i % 2][:, r:r + 1] for r in range(4)], [cmv[i % 2][:, r:r + 1] for r in range(2)],
                                         Chain(pool, c_norm, b * (4 * BT) + 4 * i, pool_passed))
                            scatter(i)
                            step = Chain(pool, res_step, b * (2 * BT) + 2 * i)
                            pool.wait_ge(an_made, b * BT + i + 1)
                            step(pool.tensor_tensor(gained[:], an[i % 2][:], ga_row[:], ALU.mult))
                            step(pool.tensor_tensor(xnb[:, i], xnb[:, i], gained[:], ALU.add))
                        for q in scattered:
                            hold(pool, q, b * (BT // 2 * 32) + BT // 2 * 32, pool_passed)
                        pool.wait_ge(s_made, b * BT + BT)

                @block.scalar
                def _(act):
                    with act.Fori(0, S) as b:
                        def norm_x(g):
                            act.wait_ge(ax_norm, b * 4 * GROUPS + 4 * g + 4)
                            for k in range(GROUP):
                                act.activation(xnb[:, g * GROUP + k], xa[g % 2][:, k], ACT.Identity,
                                               bias=xnorm[g % 2][:, 1, k:k + 1], scale=xnorm[g % 2][:, 0, k:k + 1]).then_inc(axn_made, 1)

                        norm_x(0)
                        for i in range(BT + 3):
                            if i < BT:
                                act.wait_ge(xt_done, b * BT + i + 1)
                                if i >= 2:
                                    act.wait_ge(aq_done, b * BT + i - 1)
                                act.activation(xtile[i % 2][:].rearrange("p j c -> p (j c)"), bank[0][:, 0:E], ACT.Copy).then_inc(xt_made, 1)
                            if i % 4 == 2 and i // 4 + 1 < GROUPS:
                                norm_x(i // 4 + 1)
                            k = i - 2
                            if 0 <= k < BT:
                                act.wait_ge(aq_norm, b * (4 * BT) + 4 * k + 4)
                                if k == 0:
                                    act.wait_ge(vn_ones, 1)
                                if k >= 2:
                                    act.wait_ge(qkt_done, b * BT + k - 1)
                                n = qnorm[k % 2]
                                for r in range(3):
                                    src = bank[2 + 2 * (k % 2)][:, r * E:(r + 1) * E] if r < 2 else bank[3 + 2 * (k % 2)][:, 0:E]
                                    if r < 2:
                                        dst = qkn[k % 2][:, r * E:(r + 1) * E]
                                    else:
                                        dst, src = vn[:, k, :, 0:P], src.rearrange("p (j c) -> p j c", j=HALVES)
                                    act.activation(dst, src, ACT.Identity, bias=n[:, 1, r:r + 1],
                                                   scale=n[:, 0, r:r + 1]).then_inc(qkvn_made, 1)
                                act.wait_ge(qkt_done, b * BT + k + 1)
                                act.wait_ge(kt_made, b * BT + k + 1)
                                for j in range(HALVES):
                                    act.activation(tq[:, j, k * P:(k + 1) * P],
                                                   bank[6][:, j * P:(j + 1) * P], ACT.Identity,
                                                   accum_out=qpart[:, j, k:k + 1]).then_inc(qt_made, 1)
                            k = i - 3
                            if 0 <= k < BT:
                                act.wait_ge(phik_done, b * BT + k + 1)
                                act.activation(tk[:, k], bank[1][:, 0:E], ACT.Tanh).then_inc(tk_made, 1)

                        def phi_q(g):
                            act.wait_ge(phiq_done, b * (2 * GROUPS) + 2 * g + 2)
                            for j in range(HALVES):
                                act.activation(tq[:, j, g * GROUP * P:(g + 1) * GROUP * P], bank[PHI_BANKS[g][j]][:], ACT.Tanh,
                                               bias=phiq_bias[:, j:j + 1]).then_inc(tq_made, 1)

                        phi_q(0)
                        act.wait_ge(max_step, b * MAXS + MAXS)
                        for c in range(4):
                            act.activation(alpha_t[:, c * 512:(c + 1) * 512], bank[2 + c][0:H, :], ACT.Exp, bias=small[:, 8:9],
                                           accum_out=small[:, 10 + c:11 + c]).then_inc(alpha_exp, 1)
                        act.activation(small[:, 14:15], small[:, 9:10], ACT.Exp).then_inc(alpha_exp, 1)
                        phi_q(1)
                        act.wait_ge(alpha_turned, b + 1)
                        act.activation(alpha[:].rearrange("p i h -> p (i h)"), bank[0][:, 0:BT * H], ACT.Copy).then_inc(alpha_made, 1)
                        phi_q(2)
                        phi_q(3)
                        for i in range(BT + 7):
                            k = i - 5
                            if 0 <= k < BT:
                                act.wait_ge(c_norm, b * (4 * BT) + 4 * k + 4)
                                if k >= 2:
                                    act.wait_ge(an_turned, b * BT + k - 1)
                                    act.wait_ge(res_step, b * (2 * BT) + 2 * (k - 1))
                                act.activation(an[k % 2][:], bank[6][:, 0:E], ACT.Identity, bias=cnorm[k % 2][:, 1:2],
                                               scale=cnorm[k % 2][:, 0:1]).then_inc(an_made, 1)
                            k = i - 1
                            if 0 <= k < BT:
                                act.wait_ge(attn_turned, b * BT + k + 1)
                                if k == 0:
                                    act.wait_ge(score_done, b * 2 + 2)
                                act.activation(attnt[:, :, 2 + k * P:2 + (k + 1) * P],
                                               bank[4][:, 0:E].rearrange("p (j c) -> p j c", j=HALVES), ACT.Copy).then_inc(attnt_made, 1)
                            k = i - 5
                            if 0 <= k < BT:
                                g, r = k // PAIR, k % PAIR
                                act.wait_ge(an_turned, b * BT + k + 1)
                                if r == 0 and g >= 2:
                                    act.wait_ge(up_done, b * (PAIRS_A * F_CHUNKS) + (g - 1) * F_CHUNKS)
                                act.activation(ant_s[g % 2][0][:, :, r * P:(r + 1) * P],
                                               bank[5][:, 0:E].rearrange("p (j c) -> p j c", j=HALVES), ACT.Copy).then_inc(ant_high, 1)
                            k = i - 6
                            if 0 <= k < BT and k % PAIR == PAIR - 1:
                                g = k // PAIR
                                for f in range(F_CHUNKS):
                                    at = b * (PAIRS_A * F_CHUNKS) + g * F_CHUNKS + f
                                    act.wait_ge(up_done, at + 1)
                                    if g * F_CHUNKS + f >= 4:
                                        act.wait_ge(gel_split, b * (2 * PAIRS_A * F_CHUNKS) + 2 * (g * F_CHUNKS + f - 3))
                                    act.activation(gel[:, f % 4], bank[f % 2][:, 0:PAIR * P], ACT.Gelu, bias=b1c[:, f:f + 1]).then_inc(gel_made, 1)
                        act.wait_ge(s_made, b * BT + BT)

                @block.tensor
                def _(pe):
                    with pe.Fori(0, S) as b:
                        for i in range(BT + 3):
                            if i < BT:
                                pe.wait_ge(axn_made, b * BT + i + 1)
                                if i >= 1:
                                    pe.wait_ge(xt_made, b * BT + i)
                                for j in range(HALVES):
                                    mm = pe.transpose(bank[0][:, j * P:(j + 1) * P], xnb[:, i, j * P:(j + 1) * P], ident[:])
                                mm.then_inc(xt_done, 1)
                            k = i - 1
                            if 0 <= k < BT:
                                pe.wait_ge(xt_made, b * BT + k + 1)
                                if k >= 2:
                                    pe.wait_ge(qkvn_made, b * (3 * BT) + 3 * (k - 1))
                                qk_bank, v_bank = bank[2 + 2 * (k % 2)], bank[3 + 2 * (k % 2)]
                                for dst, c, w in ((qk_bank[:], ROW_Q, 2 * E), (v_bank[:, 0:E], ROW_V, E)):
                                    pe.matmul(dst, one_row[:], brow2[:, c:c + w], start=True, stop=False)
                                    for j in range(HALVES):
                                        mm = pe.matmul(dst, xtile[k % 2][:, j], wa[:, j, c:c + w], start=False, stop=j == 1)
                                mm.then_inc(aq_done, 1)
                            k = i - 2
                            if 0 <= k < BT:
                                pe.wait_ge(qkvn_made, b * (3 * BT) + 3 * k + 2)
                                if k >= 1:
                                    pe.wait_ge(qt_made, b * (2 * BT) + 2 * k)
                                    pe.wait_ge(kt_made, b * BT + k)
                                for c in range(4):
                                    mm = pe.transpose(bank[6][:, c * P:(c + 1) * P], qkn[k % 2][:, c * P:(c + 1) * P], ident[:])
                                mm.then_inc(qkt_done, 1)
                            k = i - 3
                            if 0 <= k < BT:
                                pe.wait_ge(kt_made, b * BT + k + 1)
                                if k >= 1:
                                    pe.wait_ge(tk_made, b * BT + k)
                                pe.matmul(bank[1][:, 0:E], one_row[:], brow2[:, ROW_PHIK:ROW_PHIK + E], start=True, stop=False)
                                for j in range(HALVES):
                                    mm = pe.matmul(bank[1][:, 0:E], knt[:, j, k * P:(k + 1) * P], wphi[:, 1, j], start=False, stop=j == 1)
                                mm.then_inc(phik_done, 1)

                        def phi_q(g):
                            if g == 0:
                                pe.wait_ge(qt_made, b * (2 * BT) + 2 * BT)
                            if g == 1:
                                pe.wait_ge(tq_made, b * (2 * GROUPS) + 2)
                            for n in range(HALVES):
                                for j in range(HALVES):
                                    mm = pe.matmul(bank[PHI_BANKS[g][n]][:], wphi[:, 0, j, n * P:(n + 1) * P],
                                                   tq[:, j, g * GROUP * P:(g + 1) * GROUP * P], start=j == 0, stop=j == 1)
                                mm.then_inc(phiq_done, 1)

                        phi_q(0)
                        pe.wait_ge(mean_step, b * MEANS + MEANS)
                        pe.wait_ge(tk_made, b * BT + BT)
                        for j in range(HALVES):
                            mm = pe.matmul(bank[1][0:H, 0:1], qheads[:, j], lnk[:, 1, j:j + 1], start=j == 0, stop=j == 1)
                        mm.then_inc(score_done, 1)
                        pe.wait_ge(qkvn_made, b * (3 * BT) + 3 * BT)
                        for c in range(4):
                            for j in range(HALVES):
                                mm = pe.matmul(bank[2 + c][0:H, :], qheads_k[:, j], knt[:, j, c * 512:(c + 1) * 512], start=j == 0, stop=j == 1)
                        mm.then_inc(score_done, 1)
                        phi_q(1)
                        hold(pe, alpha_exp, b * 5 + 5, pe_passed)
                        for i in range(BT):
                            mm = pe.transpose(bank[0][:, i * H:(i + 1) * H], alpha_t[:, i * P:(i + 1) * P], ident[0:H, 0:H])
                        mm.then_inc(alpha_turned, 1)
                        pe.wait_ge(norm_step, b * NORMS + NORMS)
                        for j in range(HALVES):
                            pe.matmul(bank[1][:, 2 * j:2 * j + 2], headmask_t[:, j * P:(j + 1) * P], small[:, 14:16], start=True, stop=True)
                        phi_q(2)
                        phi_q(3)
                        pe.wait_ge(tq_made, b * (2 * GROUPS) + 4)
                        for i in range(BT):
                            pe.wait_ge(pks_made, b * BT + i + 1)
                            for j in range(HALVES):
                                mm = pe.matmul(bank[6 + j][:, 0:P + 1], pks[i % 2][:, j * P:(j + 1) * P], vn[:, i, j], start=i == 0, stop=i == BT - 1)
                            mm.then_inc(kv_done, 1)
                        for i in range(BT + 7):
                            if i < BT:
                                if i == 0:
                                    pe.wait_ge(kv_step, b * KVS + KVS)
                                if i % GROUP == 0:
                                    pe.wait_ge(tq_plus, b * GROUPS + i // GROUP + 1)
                                if i >= 1:
                                    pe.wait_ge(attn_step, b * (3 * BT) + 3 * i)
                                for j in range(HALVES):
                                    mm = pe.matmul(bank[2][:, j * (P + 8):(j + 1) * (P + 8)], tq[:, j, i * P:(i + 1) * P], kvblk[:, j], start=True, stop=True)
                                mm.then_inc(nd_done, 1)
                            k = i - 1
                            if 0 <= k < BT:
                                pe.wait_ge(attn_step, b * (3 * BT) + 3 * k + 3)
                                if k >= 1:
                                    pe.wait_ge(attnt_made, b * BT + k)
                                for j in range(HALVES):
                                    mm = pe.transpose(bank[4][:, j * P:(j + 1) * P], attn[k % 2][:, j * P:(j + 1) * P], ident[:])
                                mm.then_inc(attn_turned, 1)
                            k = i - 4
                            if 0 <= k < BT:
                                pe.wait_ge(attnt_made, b * BT + min(k + 2, BT))
                                pe.wait_ge(ends_zero, b + 1)
                                if k >= 1:
                                    pe.wait_ge(an_made, b * BT + k)
                                pe.matmul(bank[6][:, 0:E], one_row[:], brow2[:, ROW_CONV:ROW_CONV + E], start=True, stop=False)
                                for j in range(HALVES):
                                    for tap in range(5):
                                        mm = pe.matmul(bank[6][:, j * P:(j + 1) * P], attnt[:, j, k * P + tap:k * P + tap + P], wconv[:, j, tap],
                                                       start=False, stop=j == 1 and tap == 4)
                                mm.then_inc(conv_done, 1)
                            k = i - 5
                            if 0 <= k < BT:
                                pe.wait_ge(an_made, b * BT + k + 1)
                                if k >= 1:
                                    pe.wait_ge(ant_made, b * BT + k)
                                for j in range(HALVES):
                                    mm = pe.transpose(bank[5][:, j * P:(j + 1) * P], an[k % 2][:, j * P:(j + 1) * P], ident[:])
                                mm.then_inc(an_turned, 1)
                            k = i - 6
                            if 0 <= k < BT and k % PAIR == PAIR - 1:
                                g = k // PAIR
                                pe.wait_ge(ant_made, b * BT + k + 1)
                                for f in range(F_CHUNKS):
                                    if g * F_CHUNKS + f >= 2:
                                        pe.wait_ge(gel_made, b * (PAIRS_A * F_CHUNKS) + g * F_CHUNKS + f - 1)
                                    mm = split_product(pe, bank[f % 2][:, 0:PAIR * P],
                                                       [[w[:, j, f * P:(f + 1) * P] for w in w1_s] for j in range(HALVES)],
                                                       [[w[:, j] for w in ant_s[g % 2]] for j in range(HALVES)])
                                    mm.then_inc(up_done, 1)
                            k = i - 7
                            if 0 <= k < BT and k % PAIR == PAIR - 1:
                                g = k // PAIR
                                pe.wait_ge(gel_split, b * (2 * PAIRS_A * F_CHUNKS) + 2 * (g + 1) * F_CHUNKS)
                                for r in range(PAIR):
                                    n = g * PAIR + r
                                    if n >= 2:
                                        pe.wait_ge(s_made, b * BT + n - 1)
                                    dst = bank[7 if n % 2 == 0 else 3][:, 0:E]
                                    pe.matmul(dst, one_row[:], brow2[:, ROW_OUT:ROW_OUT + E], start=True, stop=False)
                                    mm = split_product(pe, dst, [[w[:, f, r * P:(r + 1) * P] for w in gel_s] for f in range(F_CHUNKS)],
                                                       [[w[:, f] for w in w2_s] for f in range(F_CHUNKS)], start=False)
                                    mm.then_inc(down_done, 1)
                        pe.wait_ge(s_made, b * BT + BT)

                @block.vector
                def _(dve):
                    with dve.Fori(0, S) as b:
                        def stats_x(g):
                            dve.wait_ge(ax_in[g % 2], b * 32 + g // 2 * 16 + 16)
                            if g >= 1:
                                dve.wait_ge(ax_mv, b * BT + g * GROUP)
                            for k in range(GROUP):
                                dve.bn_stats(xstats[:, k], xa[g % 2][:, k]).then_inc(ax_stats, 1)
                            hold(dve, ax_stats, b * BT + g * GROUP + GROUP, dve_passed)
                            for k in range(GROUP):
                                dve.bn_aggr(xmv[g % 2][:, k], xstats[:, k]).then_inc(ax_mv, 1)

                        stats_x(0)
                        for i in range(BT + 3):
                            if i % 4 == 0 and i // 4 + 1 < GROUPS:
                                stats_x(i // 4 + 1)
                            k = i - 1
                            if 0 <= k < BT:
                                dve.wait_ge(aq_done, b * BT + k + 1)
                                if k >= 1:
                                    dve.wait_ge(aq_mv, b * (3 * BT) + 3 * k)
                                for r in range(3):
                                    src = bank[2 + 2 * (k % 2)][:, r * E:(r + 1) * E] if r < 2 else bank[3 + 2 * (k % 2)][:, 0:E]
                                    dve.bn_stats(qstats[:, r], src).then_inc(aq_stats, 1)
                                hold(dve, aq_stats, b * (3 * BT) + 3 * k + 3, dve_passed)
                                if k >= 2:
                                    hold(dve, aq_norm, b * (4 * BT) + 4 * (k - 1), dve_passed)
                                for r in range(3):
                                    dve.bn_aggr(qmv[k % 2][:, r], qstats[:, r]).then_inc(aq_mv, 1)
                            k = i - 2
                            if 0 <= k < BT:
                                dve.wait_ge(qkt_done, b * BT + k + 1)
                                dve.tensor_copy(knt[:, :, k * P:(k + 1) * P], bank[6][:, 2 * P:4 * P].rearrange("p (j c) -> p j c", j=HALVES)).then_inc(kt_made, 1)
                        step = Chain(dve, mean_step, b * MEANS)
                        dve.wait_ge(qt_made, b * (2 * BT) + 2 * BT)
                        step(dve.tensor_reduce(qmean[:], qpart[:], AX_X, ALU.add))
                        step(dve.tensor_scalar(qmean[:], qmean[:], 1.0 / NB, None, ALU.mult))
                        step(dve.tensor_tensor(qmean[:], qmean[:], lnq[:, 0], ALU.mult))
                        step(dve.tensor_tensor(qmean[:], qmean[:], lnq[:, 1], ALU.add))
                        step(dve.tensor_scalar(qmean[:], qmean[:], float(D) ** -0.5, None, ALU.mult))
                        step(dve.tensor_tensor(qmean_k[:], qmean[:], lnk[:, 0], ALU.mult))
                        for j in range(HALVES):
                            step(dve.tensor_scalar(qheads[:, j], headmask[:, j], qmean[:, j:j + 1], None, ALU.mult))
                            step(dve.tensor_scalar(qheads_k[:, j], headmask[:, j], qmean_k[:, j:j + 1], None, ALU.mult))
                        step = Chain(dve, max_step, b * MAXS)
                        dve.wait_ge(score_done, b * 2 + 1)
                        step(dve.tensor_copy(small[:, 0:1], bank[1][0:H, 0:1]))
                        dve.wait_ge(score_done, b * 2 + 2)
                        for c in range(4):
                            mx = dve.tensor_reduce(small[:, 1 + c:2 + c], bank[2 + c][0:H, :], AX_X, ALU.max)
                        step(mx)
                        step(dve.tensor_reduce(small[:, 5:6], small[:, 1:5], AX_X, ALU.max))
                        step(dve.tensor_tensor(small[:, 6:7], small[:, 5:6], small[:, 0:1], ALU.add))
                        step(dve.tensor_scalar(small[:, 7:8], small[:, 6:7], 0.0, None, ALU.max))
                        step(dve.tensor_tensor(small[:, 8:9], small[:, 0:1], small[:, 7:8], ALU.subtract))
                        step(dve.tensor_scalar(small[:, 9:10], small[:, 7:8], -1.0, None, ALU.mult))
                        step = Chain(dve, norm_step, b * NORMS)
                        dve.wait_ge(alpha_exp, b * 5 + 5)
                        step(dve.tensor_reduce(small[:, 16:17], small[:, 10:14], AX_X, ALU.add))
                        step(dve.tensor_tensor(small[:, 16:17], small[:, 16:17], small[:, 14:15], ALU.add))
                        step(dve.reciprocal(small[:, 17:18], small[:, 16:17]))
                        step(dve.tensor_scalar(small[:, 15:16], small[:, 17:18], float(NB), None, ALU.mult))

                        def plus_one(g):
                            dve.wait_ge(tq_made, b * (2 * GROUPS) + 2 * g + 2)
                            part = tq[:, :, g * GROUP * P:(g + 1) * GROUP * P]
                            dve.tensor_scalar(part, part, 1.0, None, ALU.add).then_inc(tq_plus, 1)

                        plus_one(0)
                        plus_one(1)
                        dve.wait_ge(alpha_made, b + 1)
                        for i in range(BT):
                            if i >= 2:
                                dve.wait_ge(kv_done, b * BT + i - 1)
                            dve.scalar_tensor_tensor(pks[i % 2][:].rearrange("p (h d) -> p h d", d=D), tk[:, i].rearrange("p (h d) -> p h d", d=D),
                                                     1.0, alpha[:, i].unsqueeze(2).to_broadcast((P, H, D)), ALU.add, ALU.mult).then_inc(pks_made, 1)
                        plus_one(2)
                        plus_one(3)
                        dve.wait_ge(score_done, b * 2 + 2)
                        dve.memset(attnt[:, :, 0:2], 0.0)
                        dve.memset(attnt[:, :, NB + 2:NB + 4], 0.0).then_inc(ends_zero, 1)
                        step = Chain(dve, kv_step, b * KVS)
                        dve.wait_ge(kv_done, b * BT + BT)
                        step(dve.tensor_copy(spread[:].rearrange("p j c -> p (j c)"), bank[1][:, 0:4]))
                        step(dve.tensor_tensor(ksum[:, :, 0], phik_zero[:], spread[:, :, 0], ALU.mult))
                        for j in range(HALVES):
                            raw = bank[6 + j]
                            half = slice(j * P, (j + 1) * P)
                            step(dve.tensor_tensor(kvt[:], raw[:, 0:P], gv_row[:, half], ALU.mult))
                            step(dve.tensor_tensor(ksum[:, j, 1:2], raw[:, P:P + 1], ksum[:, j, 0:1], ALU.add))
                            step(dve.scalar_tensor_tensor(kvt[:], bv_row[:, half], raw[:, P:P + 1], kvt[:], ALU.mult, ALU.add))
                            step(dve.tensor_scalar(ksum[:, j, 1:2], ksum[:, j, 1:2], spread[:, j, 1:2], None, ALU.mult))
                            step(dve.scalar_tensor_tensor(kvblk[:, j, 0:P], kvt[:], spread[:, j, 1:2], diag[:], ALU.mult, ALU.mult))
                            step(dve.tensor_scalar(kvblk[:, j, P:P + 8], diag[:, 0:P:D], ksum[:, j, 1:2], None, ALU.mult))
                        for i in range(BT + 7):
                            if i < BT:
                                step = Chain(dve, attn_step, b * (3 * BT) + 3 * i)
                                dve.wait_ge(nd_done, b * BT + i + 1)
                                both = bank[2][:, 0:2 * (P + 8)].rearrange("p (j c) -> p j c", j=HALVES)
                                step(dve.tensor_scalar(den[:], both[:, :, P:P + 8], EPS_DEN, None, ALU.add))
                                step(dve.reciprocal(den[:], den[:]))
                                if i >= 2:
                                    dve.wait_ge(attn_turned, b * BT + i - 1)
                                step(dve.tensor_tensor(attn[i % 2][:].rearrange("p (j h d) -> p j h d", j=HALVES, d=D),
                                                       both[:, :, 0:P].rearrange("p j (h d) -> p j h d", d=D),
                                                       den[:].unsqueeze(3).to_broadcast((P, HALVES, 8, D)), ALU.mult))
                            k = i - 4
                            if 0 <= k < BT:
                                dve.wait_ge(conv_done, b * BT + k + 1)
                                if k >= 1:
                                    dve.wait_ge(c_mv, b * BT + k)
                                dve.bn_stats(cstats[:], bank[6][:, 0:E]).then_inc(c_stats, 1)
                                hold(dve, c_stats, b * BT + k + 1, dve_passed)
                                dve.bn_aggr(cmv[k % 2][:], cstats[:]).then_inc(c_mv, 1)
                            k = i - 5
                            if 0 <= k < BT:
                                g, r = k // PAIR, k % PAIR
                                dve.wait_ge(ant_high, b * BT + k + 1)
                                part = slice(r * P, (r + 1) * P)
                                dve.tensor_tensor(ant_s[g % 2][1][:, :, part], bank[5][:, 0:E].rearrange("p (j c) -> p j c", j=HALVES),
                                                  ant_s[g % 2][0][:, :, part], ALU.subtract).then_inc(ant_made, 1)
                            k = i - 6
                            if 0 <= k < BT and k % PAIR == PAIR - 1:
                                g = k // PAIR
                                if g >= 1:
                                    dve.wait_ge(down_done, b * BT + g * PAIR)
                                for f in range(F_CHUNKS):
                                    at = b * (2 * PAIRS_A * F_CHUNKS) + 2 * (g * F_CHUNKS + f)
                                    hi, lo = gel_s
                                    dve.wait_ge(gel_made, b * (PAIRS_A * F_CHUNKS) + g * F_CHUNKS + f + 1)
                                    dve.tensor_copy(hi[:, f], gel[:, f % 4]).then_inc(gel_split, 1)
                                    dve.wait_ge(gel_split, at + 1)
                                    dve.tensor_tensor(lo[:, f], gel[:, f % 4], hi[:, f], ALU.subtract).then_inc(gel_split, 1)
                            k = i - 7
                            if 0 <= k < BT and k % PAIR == PAIR - 1:
                                for n in range(k - PAIR + 1, k + 1):
                                    dve.wait_ge(down_done, b * BT + n + 1)
                                    dve.wait_ge(res_step, b * (2 * BT) + 2 * n + 2)
                                    if n >= 2:
                                        dve.wait_ge(s_out[n % 2], b * (BT // 2 * 16) + n // 2 * 16)
                                    dve.tensor_tensor(sout[n % 2][:], bank[7 if n % 2 == 0 else 3][:, 0:E], xnb[:, n], ALU.add).then_inc(s_made, 1)
                        for q in s_out:
                            dve.wait_ge(q, b * (BT // 2 * 16) + BT // 2 * 16)

        with ExitStack() as own:
            CHUNK = 2 * P
            CHUNKS = CAP // CHUNK
            UNROLL = 2 * CHUNKS
            FC = FFN // P
            rows_in = [sb(f"rows_in{p}", [P, 2, E], F32, own) for p in range(2)]
            rows_t = sb("rows_t", [P, HALVES, CHUNK], F32, own)
            up_w = [sb(f"up_w{p}", [P, HALVES, FFN], F32, own) for p in range(2)]
            down_w = [sb(f"down_w{p}", [P, FC, E], F32, own) for p in range(2)]
            hid = [sb(f"hid{p}", [P, FC, CHUNK], F32, own) for p in range(2)]
            rows_s = [[sb(f"rows_{w}{p}", [P, HALVES, CHUNK], F32R, own) for w in ("hi", "lo")] for p in range(2)]
            up_s = [[sb(f"up_{w}{p}", [P, HALVES, FFN], F32R, own) for w in ("hi", "lo")] for p in range(2)]
            down_s = [[sb(f"down_{w}{p}", [P, FC, E], F32R, own) for w in ("hi", "lo")] for p in range(2)]
            hid_s = [[sb(f"hid_{w}{p}", [P, FC, CHUNK], F32R, own) for w in ("hi", "lo")] for p in range(2)]
            h2 = [sb(f"h2_{p}", [P, 2, E], F32, own) for p in range(2)]
            rows_loaded, weights_in = [sem("rows_loaded0"), sem("rows_loaded1")], [sem("weights_in0"), sem("weights_in1")]
            h2_out = [sem("h2_out0"), sem("h2_out1")]
            rows_turned, rows_made, e_up, e_hid, e_down, h2_made = (
                sem("rows_turned"), sem("rows_made"), sem("e_up"), sem("e_hid"), sem("e_down"), sem("h2_made"))
            rows_split, hid_split, weights_split = sem("e_rows_split"), sem("e_hid_split"), sem("weights_split")
            AHEAD, HID_AHEAD, EXPERTS_AHEAD = 2, 4, CHUNKS + 1

            def steps(b):
                for i in range(UNROLL):
                    yield i, i // CHUNKS, i % CHUNKS, i % 2

            with nc.Block() as block:
                @block.sync
                def _(sp):
                    with sp.Fori(0, NX // 2) as b:
                        for i, odd, c, p in steps(b):
                            hold(sp, rows_turned, b * UNROLL + i + 1, sp_passed)
                            sp.dma_start(rows_in[p][:], buf_d.rearrange("(t i p) e -> p t i e", p=P, i=2)
                                         [:, bass.ds(b * UNROLL + i, 1)].rearrange("p a i e -> p (a i) e")).then_inc(rows_loaded[p], 16)

                @block.scalar
                def _(act):
                    act.sem_inc(e_hid, HID_AHEAD)
                    for q in h2_out:
                        act.sem_inc(q, 16)
                    with act.Fori(0, NX // 2) as b:
                        def store(i):
                            hold(act, h2_made, b * UNROLL + i + 1 + AHEAD, act_passed)
                            act.dma_start(h2_d[0:SLOTS].rearrange("(t i p) e -> p t i e", p=P, i=2)
                                          [:, bass.ds(b * UNROLL + i, 1)].rearrange("p a i e -> p (a i) e"),
                                          h2[i % 2][:]).then_inc(h2_out[i % 2], 16)

                        for i, odd, c, p in steps(b):
                            for half in range(2):
                                act.wait_ge(e_up, b * (2 * UNROLL) + 2 * i + half + 1 + 2 * AHEAD)
                                if half == 0:
                                    act.wait_ge(e_down, b * UNROLL + i + 1 - AHEAD + EXPERTS_AHEAD)
                                for dst in (hid[p], hid_s[p][0]):
                                    act.activation(dst[:, 2 * half:2 * half + 2].rearrange("p f c -> p (f c)"),
                                                   bank[half][:], ACT.Gelu_apprx_tanh).then_inc(e_hid, 1)
                            if i:
                                store(i - 1)
                        store(UNROLL - 1)
                    for q in h2_out:
                        act.wait_ge(q, 16 * NX * CHUNKS // 2 + 16)

                @block.tensor
                def _(pe):
                    pe.sem_inc(rows_turned, AHEAD)
                    pe.sem_inc(e_up, 2 * AHEAD)
                    pe.sem_inc(e_down, EXPERTS_AHEAD)

                    with pe.Fori(0, NX // 2) as b:
                        def turn_rows(i):
                            p = i % 2
                            pe.wait_ge(rows_loaded[p], b * (UNROLL // 2 * 16) + i // 2 * 16 + 16)
                            pe.wait_ge(rows_made, b * (2 * UNROLL) + 2 * i + 2)
                            for j in range(HALVES):
                                for r in range(2):
                                    mm = pe.transpose(bank[2 + p][:, j * CHUNK + r * P:j * CHUNK + r * P + P],
                                                      rows_in[p][:, r, j * P:(j + 1) * P], ident[:])
                            mm.then_inc(rows_turned, 1)

                        def down(i):
                            odd, p = i // CHUNKS, i % 2
                            pe.wait_ge(h2_made, b * UNROLL + i + 1)
                            pe.wait_ge(hid_split, b * (2 * UNROLL) + 2 * i + 2)
                            for r in range(2):
                                mm = split_product(pe, bank[4 + p][:, r * E:(r + 1) * E],
                                                   [[w[:, f, r * P:(r + 1) * P] for w in hid_s[p]] for f in range(FC)],
                                                   [[w[:, f] for w in down_s[odd]] for f in range(FC)])
                            mm.then_inc(e_down, 1)

                        turn_rows(0)
                        for i, odd, c, p in steps(b):
                            if i + 1 < UNROLL:
                                turn_rows(i + 1)
                            if c == 0:
                                pe.wait_ge(weights_split, b * 8 + 4 * odd + 4)
                            pe.wait_ge(rows_split, b * (2 * UNROLL) + 2 * i + 2 + 1)
                            for f in range(FC):
                                if f % 2 == 0:
                                    pe.wait_ge(e_hid, b * (4 * UNROLL) + 4 * i - 4 + f + 2 + HID_AHEAD)
                                mm = split_product(pe, bank[f // 2][:, f % 2 * CHUNK:f % 2 * CHUNK + CHUNK],
                                                   [[w[:, j, f * P:(f + 1) * P] for w in up_s[odd]] for j in range(HALVES)],
                                                   [[w[:, j] for w in rows_s[p]] for j in range(HALVES)])
                                if f % 2:
                                    mm.then_inc(e_up, 1)
                            if i:
                                down(i - 1)
                        down(UNROLL - 1)

                @block.gpsimd
                def _(pool):
                    with pool.Fori(0, NX // 2) as b:
                        for odd in range(2):
                            pool.dma_start(up_w[odd][:], a["w1_t"][bass.ds(b * 2 + odd, 1)]
                                           .rearrange("a (j p) f -> p (a j) f", p=P)).then_inc(weights_in[odd], 16)
                            pool.dma_start(down_w[odd][:], a["w2_t"][bass.ds(b * 2 + odd, 1)]
                                           .rearrange("a (j p) f -> p (a j) f", p=P)).then_inc(weights_in[odd], 16)
                            hold(pool, e_down, b * UNROLL + (odd - 1) * CHUNKS + EXPERTS_AHEAD, pool_passed)
                            hold(pool, weights_in[odd], b * 32 + 32, pool_passed)
                            step = Chain(pool, weights_split, b * 8 + 4 * odd, pool_passed)
                            for w, (hi, lo) in ((up_w[odd], up_s[odd]), (down_w[odd], down_s[odd])):
                                step(pool.tensor_copy(hi[:], w[:]))
                                step(pool.tensor_tensor(lo[:], w[:], hi[:], ALU.subtract))

                @block.vector
                def _(dve):
                    dve.sem_inc(rows_made, 2 * AHEAD)
                    dve.sem_inc(h2_made, AHEAD)
                    dve.sem_inc(rows_split, 1)
                    with dve.Fori(0, NX // 2) as b:
                        def rows_out(i):
                            p = i % 2
                            hi, lo = rows_s[p]
                            dve.wait_ge(rows_turned, b * UNROLL + i + 1 + AHEAD)
                            dve.wait_ge(rows_split, b * (2 * UNROLL) + 2 * i + 1)
                            for j in range(HALVES):
                                dve.tensor_scalar(rows_t[:, j], bank[2 + p][:, j * CHUNK:(j + 1) * CHUNK],
                                                  ln2w[:, j:j + 1], ln2b[:, j:j + 1], ALU.mult, ALU.add).then_inc(rows_made, 1)
                            dve.wait_ge(rows_made, b * (2 * UNROLL) + 2 * i + 2 + 2 * AHEAD)
                            dve.wait_ge(e_up, b * (2 * UNROLL) + 2 * i + 2)
                            dve.tensor_copy(hi[:], rows_t[:]).then_inc(rows_split, 1)
                            dve.wait_ge(rows_split, b * (2 * UNROLL) + 2 * i + 1 + 1)
                            dve.tensor_tensor(lo[:], rows_t[:], hi[:], ALU.subtract).then_inc(rows_split, 1)

                        def result_out(i):
                            dve.wait_ge(e_down, b * UNROLL + i + 1 + EXPERTS_AHEAD)
                            dve.wait_ge(h2_out[i % 2], b * (UNROLL // 2 * 16) + i // 2 * 16 + 16)
                            dve.tensor_copy(h2[i % 2][:].rearrange("p r e -> p (r e)"), bank[4 + i % 2][:]).then_inc(h2_made, 1)

                        rows_out(0)
                        for i, odd, c, p in steps(b):
                            if i + 1 < UNROLL:
                                rows_out(i + 1)
                            hi, lo = hid_s[p]
                            for half in range(2):
                                part = slice(2 * half, 2 * half + 2)
                                dve.wait_ge(e_hid, b * (4 * UNROLL) + 4 * i + 2 * half + 2 + HID_AHEAD)
                                if half == 0:
                                    dve.wait_ge(e_down, b * UNROLL + i + 1 - AHEAD + EXPERTS_AHEAD)
                                dve.tensor_tensor(lo[:, part], hid[p][:, part], hi[:, part], ALU.subtract).then_inc(hid_split, 1)
                            if i:
                                result_out(i - 1)
                        result_out(UNROLL - 1)

        with ExitStack() as own:
            TURNS = T // (GROUP * P)
            rows_of = [sb(f"rows_of{p}", [P, GROUP, 2], I32, own) for p in range(2)]
            picked = [sb(f"picked{p}", [P, GROUP, 2, E], F32, own) for p in range(2)]
            after_c = [sb(f"after_c{p}", [P, GROUP, E], F32, own) for p in range(2)]
            s_c = [sb(f"s_c{p}", [P, GROUP, E], F32, own) for p in range(2)]
            x_c = [sb(f"x_c{p}", [P, GROUP, E], F32, own) for p in range(2)]
            ffn = [sb(f"ffn{p}", [P, GROUP, E], F32, own) for p in range(2)]
            silu = [sb(f"silu{p}", [P, GROUP, E], F32, own) for p in range(2)]
            result = [sb(f"result{p}", [P, GROUP, E], F32, own) for p in range(2)]
            group_in, picked_in, group_out = (
                [sem("group_in0"), sem("group_in1")], [sem("picked_in0"), sem("picked_in1")], [sem("group_out0"), sem("group_out1")])
            rows_staged, ffn_made, silu_made, result_made, comb_step = (
                sem("rows_staged"), sem("ffn_made"), sem("silu_made"), sem("result_made"), sem("comb_step"))
            DSTEPS = 2 * GROUP + 1
            FFN_AHEAD, RESULT_AHEAD = 2, 2

            def tiles_of(ap, turn):
                return ap.rearrange("(t i p) e -> p t i e", p=P, i=GROUP)[:, bass.ds(turn, 1)].rearrange("p a i e -> p (a i) e")

            with nc.Block() as block:
                @block.sync
                def _(sp):
                    with sp.Fori(0, TURNS // 2) as b:
                        for p in range(2):
                            hold(sp, result_made, b * 2 + p - 1 + RESULT_AHEAD, sp_passed)
                            for dst, src in ((after_c, after_d), (s_c, s_d), (x_c, a["x"])):
                                sp.dma_start(dst[p][:], tiles_of(src, b * 2 + p)).then_inc(group_in[p], 16)

                @block.gpsimd
                def _(pool):
                    with pool.Fori(0, TURNS // 2) as b:
                        for p in range(2):
                            hold(pool, ffn_made, b * 2 + p - 1 + FFN_AHEAD, pool_passed)
                            pool.tensor_copy(rows_of[p][:], from_row[:, bass.ds(b * (2 * GROUP) + p * GROUP, GROUP)]).then_inc(rows_staged, 1)
                            hold(pool, rows_staged, b * 2 + p + 1, pool_passed)
                            for i in range(GROUP):
                                for k in range(2):
                                    pool.indirect_dma_start(picked[p][:, i, k], None, h2_d,
                                                            bass.IndirectOffsetOnAxis(rows_of[p][:, i, k:k + 1], axis=0)
                                                            ).then_inc(picked_in[p], 16)

                @block.scalar
                def _(act):
                    with act.Fori(0, TURNS // 2) as b:
                        def store(p):
                            hold(act, result_made, b * 2 + p + 1 + RESULT_AHEAD, act_passed)
                            act.dma_start(tiles_of(out, b * 2 + p), result[p][:]).then_inc(group_out[p], 16)

                        for p in range(2):
                            act.wait_ge(ffn_made, b * 2 + p + 1 + FFN_AHEAD)
                            act.activation(silu[p][:], ffn[p][:], ACT.Silu).then_inc(silu_made, 1)
                            store(p)
                    for q in group_out:
                        act.wait_ge(q, 16 * TURNS // 2 + 16)

                @block.vector
                def _(dve):
                    dve.sem_inc(ffn_made, FFN_AHEAD)
                    dve.sem_inc(result_made, RESULT_AHEAD)
                    for q in group_out:
                        dve.sem_inc(q, 16)
                    with dve.Fori(0, TURNS // 2) as b:
                        for p in range(2):
                            dve.wait_ge(picked_in[p], b * (32 * GROUP) + 32 * GROUP)
                            dve.wait_ge(group_in[p], b * 48 + 48)
                            base = b * (2 * DSTEPS) + p * DSTEPS

                            def weight(i, k):
                                return gate[:, bass.ds(b * (2 * GROUP) + p * GROUP + i, 1), k]

                            for i in range(GROUP):
                                dve.tensor_scalar(ffn[p][:, i], picked[p][:, i, 0], weight(i, 0), None, ALU.mult).then_inc(comb_step, 1)
                            dve.wait_ge(comb_step, base + GROUP)
                            for i in range(GROUP):
                                dve.scalar_tensor_tensor(ffn[p][:, i], picked[p][:, i, 1], weight(i, 1), ffn[p][:, i],
                                                         ALU.mult, ALU.add).then_inc(comb_step, 1)
                            dve.wait_ge(comb_step, base + 2 * GROUP)
                            dve.tensor_tensor(ffn[p][:], ffn[p][:], after_c[p][:], ALU.add).then_inc(ffn_made, 1)
                            dve.wait_ge(silu_made, b * 2 + p + 1)
                            dve.wait_ge(group_out[p], b * 16 + 16)
                            dve.tensor_tensor(silu[p][:], silu[p][:], s_c[p][:], ALU.mult).then_inc(comb_step, 1)
                            dve.wait_ge(comb_step, base + 2 * GROUP + 1)
                            dve.tensor_tensor(result[p][:], silu[p][:], x_c[p][:], ALU.add).then_inc(result_made, 1)


def kernel(**inputs):
    import numpy as _np
    import concourse.bacc as _bacc
    from concourse.bass_utils import run_bass_kernel_spmd as _run

    x = {k: _np.asarray(v) for k, v in inputs.items()}
    f, g = "L0_attn_", "L0_ffn_"
    arrays = {k[len(f):]: v for k, v in x.items() if k.startswith(f)}
    arrays["gamma"] = _np.reshape(arrays["gamma"], (1, 1))
    arrays["conv_t"] = _np.transpose(_np.reshape(arrays.pop("conv_w"), (H, D, D, 5)), (0, 2, 3, 1))
    for k in ("ln1_weight", "ln1_bias", "ln2_weight", "ln2_bias"):
        arrays[k] = x[g + k]
    arrays["qkv_t"] = x[g + "qkv_weight"].T
    arrays["proj_t"] = x[g + "proj_weight"].T
    arrays["router_t"] = x[g + "router_weight"].T
    arrays["w1_t"] = _np.transpose(x[g + "moe_w1"], (0, 2, 1))
    arrays["w2_t"] = _np.transpose(x[g + "moe_w2"], (0, 2, 1))
    arrays["x"] = _np.reshape(arrays["x"], (T, E))
    arrays = {k: _np.ascontiguousarray(v) for k, v in arrays.items()}

    nc = _bacc.Bacc("TRN2", target_bir_lowering=False, num_devices=1)
    a = {k: nc.dram_tensor(f"in_{k}", v.shape, F32, kind="ExternalInput").ap() for k, v in arrays.items()}
    out = nc.dram_tensor("out_0", (T, E), F32, kind="ExternalOutput").ap()
    build(nc, a, out)
    r = _run(nc, [{f"in_{k}": v for k, v in arrays.items()}], core_ids=[0])
    return _np.reshape(r.results[0]["out_0"], (S, NB, E))
```

```python
from contextlib import ExitStack

import concourse.bass as bass
from concourse import mybir

F32 = mybir.dt.float32
F32R = mybir.dt.float32r
BF16 = mybir.dt.bfloat16
I32 = mybir.dt.int32
U32 = mybir.dt.uint32
ALU = mybir.AluOpType
ACT = mybir.ActivationFunctionType
AX_X = mybir.AxisListType.X

P = 128
S, NB, E = 4, 2048, 256
HALVES = E // P
T = S * NB
TILES = T // P
BT = NB // P
H, D = 16, 16
KVH, REP = 4, 4
QKV = E + 2 * KVH * D
MLP = 1024
NX, FFN = 16, 512
CAP = 1280
SLOTS = NX * CAP
FAR = 1 << 20
EPS = 1e-5
EPS_DEN = 1e-6
GROUP = 4
GROUPS = BT // GROUP


class Step:

    def __init__(self, half, odd):
        self.half, self.odd, self.n = half, odd, half * 2 + odd

    def back(self, lag):
        turn = self.odd - lag
        return Step(self.half + turn // 2, turn % 2)


def turns(eng, count, lag, body, reach):
    lead = (reach + 1) // 2
    for t in range(2 * lead):
        body(Step(t // 2, t % 2))
    with eng.Fori(lead, count // 2) as half:
        body(Step(half, 0))
        body(Step(half, 1))
    for t in range(count, count + lag):
        body(Step(t // 2, t % 2))


def exists(step, count):
    return not isinstance(step.n, int) or 0 <= step.n < count


def later(step, k):
    return not isinstance(step.n, int) or step.n >= k


def hold(eng, sem, value, passed):
    eng.wait_ge(sem, value)
    if not isinstance(value, int):
        eng.sem_inc(passed, 1)


class Chain:

    def __init__(self, eng, sem, base=0, passed=None):
        self.eng, self.sem, self.base, self.passed, self.done = eng, sem, base, passed, 0

    def __call__(self, ins, held=None):
        ins.then_inc(self.sem, 1)
        self.done += 1
        value = self.base + self.done
        if self.passed or held:
            hold(self.eng, self.sem, value, self.passed or held)
        else:
            self.eng.wait_ge(self.sem, value)

    def also(self, ins):
        ins.then_inc(self.sem, 1)
        self.done += 1


def col(ap):
    return ap.rearrange("(j p) -> p j", p=P)


def row(ap):
    return ap.rearrange("(a n) -> a n", a=1)


def split_product(pe, dst, stationary, moving, start=True, stop=True):
    for i, ((hi, lo), (mhi, mlo)) in enumerate(zip(stationary, moving)):
        end = stop and i == len(moving) - 1
        pe.matmul(dst, hi, mhi, start=start and i == 0, stop=False)
        pe.matmul(dst, hi, mlo, start=False, stop=False)
        mm = pe.matmul(dst, lo, mhi, start=False, stop=end)
    return mm


def build(nc, a, out):
    nc.disable_value_cache = True
    ctx = ExitStack()
    with ctx:
        def sb(name, shape, dt=F32, into=ctx):
            return into.enter_context(nc.sbuf_tensor(name, shape, dt))

        def sem(name):
            return ctx.enter_context(nc.semaphore(name))

        bank = [ctx.enter_context(nc.psum_tensor(f"bank{i}", [P, 512], F32)) for i in range(8)]

        dve_passed, pool_passed, pe_passed, sp_passed, act_passed = (
            sem("dve_passed"), sem("pool_passed"), sem("pe_passed"), sem("sp_passed"), sem("act_passed"))

        ln2_d = nc.dram_tensor("ln2_d", (T, E), F32).ap()
        after_d = nc.dram_tensor("after_d", (T, E), F32).ap()
        s_d = nc.dram_tensor("s_d", (T, E), F32).ap()
        buf_d = nc.dram_tensor("buf_d", (SLOTS, E), F32).ap()
        h2_d = nc.dram_tensor("h2_d", (SLOTS + P, E), F32).ap()

        ident = sb("ident", [P, P])
        one_row = sb("one_row", [2, P], F32R)
        ROW_Q, ROW_V, ROW_PHIK, ROW_CONV, ROW_OUT, ROW_QKV, ROWS = 0, 512, 768, 1024, 1280, 1536, 1536 + QKV
        brow2 = sb("brow2", [2, ROWS], F32R)
        diag = sb("diag", [P, P])
        headmask = sb("headmask", [P, HALVES, H])
        headmask_t = sb("headmask_t", [H, HALVES * P])
        neg_half = sb("neg_half", [P, 4])
        ln1w, ln1b = sb("ln1w", [P, HALVES]), sb("ln1b", [P, HALVES])
        ln2w, ln2b = sb("ln2w", [P, HALVES]), sb("ln2b", [P, HALVES])
        gate = sb("gate", [P, TILES, 2])
        to_row = sb("to_row", [P, TILES, 2], I32)
        from_row = sb("from_row", [P, TILES, 2], I32)
        wa_s = [sb(f"wa_{w}", [P, HALVES, 3 * E], F32R) for w in ("hi", "lo")]
        wphi = sb("wphi", [P, 2, HALVES, E])
        wconv = sb("wconv", [P, HALVES, 5, P])
        w1_s = [sb(f"w1_{w}", [P, HALVES, MLP], F32R) for w in ("hi", "lo")]
        w2_s = [sb(f"w2_{w}", [P, MLP // P, E], F32R) for w in ("hi", "lo")]
        lnq = sb("lnq", [P, 2, HALVES])
        lnk = sb("lnk", [P, 2, HALVES])
        lna = sb("lna", [P, 2, HALVES])
        bphi = sb("bphi", [P, 2, HALVES])
        phiq_bias = sb("phiq_bias", [P, HALVES])
        phik_zero = sb("phik_zero", [P, HALVES])
        b1c = sb("b1c", [P, MLP // P])
        gv_row, bv_row, ga_row = sb("gv_row", [P, E]), sb("bv_row", [P, E]), sb("ga_row", [P, E])

        front_only = ExitStack()
        tri = sb("tri", [P, P], BF16, into=front_only)
        ones_b = sb("ones_b", [P, P], BF16, into=front_only)
        earlier = sb("earlier", [TILES, TILES], BF16, into=front_only)
        iota_e = sb("iota_e", [P, H], into=front_only)
        wqkv = sb("wqkv", [P, HALVES, QKV], into=front_only)
        wproj = sb("wproj", [P, HALVES, E], into=front_only)
        wrouter = sb("wrouter", [P, HALVES, P], into=front_only)
        router_bias = sb("router_bias", [P, NX], into=front_only)
        top_p = sb("top_p", [P, S, BT, 2], into=front_only)
        top_e = sb("top_e", [P, S, BT, 2], into=front_only)

        zeros = sb("zeros", [P, CAP // P, E], into=front_only)
        zero_row, zero_fill = sem("zero_row"), sem("zero_fill")

        with ExitStack() as own:
            w1 = sb("w1", [P, HALVES, MLP], F32, own)
            w2 = sb("w2", [P, MLP // P, E], F32, own)
            wa = sb("wa", [P, HALVES, 3 * E], F32, own)
            brow = sb("brow", [1, ROWS], F32, own)
            brow_lo = sb("brow_lo", [1, ROWS], F32R, own)
            brow_hi = sb("brow_hi", [1, ROWS], F32R, own)
            extra = sb("extra", [1, 4 * E], F32, own)
            gamma = sb("gamma", [P, 1], F32, own)
            ones_f = sb("ones_f", [P, P], F32, own)
            bcast = sb("bcast", [P, 2, HALVES, P], F32, own)
            masks_made, loaded, pool_step = sem("masks_made"), sem("loaded"), sem("pool_step")
            conv_blank, conv_in = sem("conv_blank"), sem("conv_in")
            sums_made, rows_split, row_two = (
                sem("sums_made"), sem("rows_split"), sem("row_two"))
            act_step, w1_split, wa_high = sem("act_step"), sem("w1_split"), sem("wa_high")
            zeroed, phi_zero, router_in = sem("zeroed"), sem("phi_zero"), sem("router_in")
            setup_step = sem("setup_step")
            LOADS = 33

            with nc.Block() as block:
                @block.gpsimd
                def _(pool):
                    pool.memset(wconv[:], 0.0).then_inc(conv_blank, 1)
                    pool.memset(zeros[:], 0.0).then_inc(zeroed, 1)
                    step = Chain(pool, pool_step)
                    step(pool.memset(wrouter[:], 0.0))
                    pool.dma_start(wrouter[:, :, 0:NX], a["router_t"].rearrange("(j p) n -> p j n", p=P)).then_inc(router_in, 16)
                    for t in (ident, diag, headmask, headmask_t, tri, earlier, ones_f, ones_b):
                        step(pool.memset(t[:], 1.0))
                    step(pool.memset(neg_half[:], -0.5))
                    step(pool.affine_select(out=ident[:], in_=ident[:], compare_op=ALU.is_equal, fill=0.0,
                                            base=0, pattern=[[-1, P]], channel_multiplier=1))
                    step(pool.affine_select(out=tri[:], in_=tri[:], compare_op=ALU.is_gt, fill=0.0,
                                            base=0, pattern=[[1, P]], channel_multiplier=-1))
                    step(pool.affine_select(out=earlier[:], in_=earlier[:], compare_op=ALU.is_gt, fill=0.0,
                                            base=0, pattern=[[1, TILES]], channel_multiplier=-1))
                    for view, width, base in ((diag[:].rearrange("p (h d) -> p h d", d=D), [[-D, P // D], [0, D]], 0),
                                              (headmask[:], [[P, HALVES], [-D, H]], 0)):
                        step(pool.affine_select(out=view, in_=view, compare_op=ALU.is_ge, fill=0.0,
                                                base=base, pattern=width, channel_multiplier=1))
                        flipped = [[-s, n] for s, n in width]
                        step(pool.affine_select(out=view, in_=view, compare_op=ALU.is_ge, fill=0.0,
                                                base=D - 1, pattern=flipped, channel_multiplier=-1))
                    step(pool.affine_select(out=headmask_t[:], in_=headmask_t[:], compare_op=ALU.is_ge, fill=0.0,
                                            base=0, pattern=[[1, E]], channel_multiplier=-D))
                    step(pool.affine_select(out=headmask_t[:], in_=headmask_t[:], compare_op=ALU.is_ge, fill=0.0,
                                            base=D - 1, pattern=[[-1, E]], channel_multiplier=D))
                    pool.iota(iota_e[:], pattern=[[1, H]], base=0, channel_multiplier=0,
                              allow_small_or_imprecise_dtypes=True).then_inc(masks_made, 1)
                    pool.wait_ge(loaded, 16 * LOADS)
                    pool.wait_ge(conv_in, 16 * H)
                    step(pool.tensor_scalar(wconv[:], wconv[:], gamma[:, 0:1], None, ALU.mult))
                    for j in range(HALVES):
                        step(pool.tensor_tensor(wconv[:, j, 2], wconv[:, j, 2], ident[:], ALU.add))
                    pool.wait_ge(act_step, 1)
                    step(pool.tensor_tensor(w2_s[1][:], w2[:], w2_s[0][:], ALU.subtract))
                    pool.wait_ge(sums_made, 1)
                    for i, g in enumerate((lnq, lnk)):
                        for j in range(HALVES):
                            step(pool.tensor_scalar(wphi[:, i, j], wphi[:, i, j], g[:, 0, j:j + 1], None, ALU.mult))

                @block.sync
                def _(sp):
                    def load(dst, src):
                        sp.dma_start(dst, src).then_inc(loaded, 16)

                    load(wqkv[:], a["qkv_t"].rearrange("(j p) n -> p j n", p=P))
                    load(wproj[:], a["proj_t"].rearrange("(j p) n -> p j n", p=P))
                    for i, name in enumerate(("Wq", "Wk", "Wv")):
                        load(wa[:, :, i * E:(i + 1) * E], a[name].rearrange("(j p) n -> p j n", p=P))
                    load(wphi[:, 0], a["Wphi_q"].rearrange("(j p) n -> p j n", p=P))
                    load(wphi[:, 1], a["Wphi_k"].rearrange("(j p) n -> p j n", p=P))
                    load(w1[:], a["W1"].rearrange("(j p) n -> p j n", p=P))
                    load(w2[:], a["W2"].rearrange("(j p) n -> p j n", p=P))
                    for i, name in enumerate(("bq", "bk", "bv")):
                        load(brow[:, i * E:(i + 1) * E], row(a[name]))
                    for i, name in enumerate(("bphi_k", "conv_b", "lna_b", "b2")):
                        load(extra[:, i * E:(i + 1) * E], row(a[name]))
                    load(gamma[:], a["gamma"].to_broadcast((P, 1)))
                    for dst, name in ((gv_row, "lnv_g"), (bv_row, "lnv_b"), (ga_row, "lna_g")):
                        load(dst[:], row(a[name]).to_broadcast((P, E)))
                    sp.wait_ge(conv_blank, 1)
                    for g in range(H):
                        c = D * (g % 8)
                        sp.dma_start(wconv[c:c + D, g // 8, :, c:c + D], a["conv_t"][g]).then_inc(conv_in, 16)
                    sp.wait_ge(zeroed, 1)
                    sp.dma_start(h2_d[SLOTS:SLOTS + P], zeros[:, 0]).then_inc(zero_row, 16)
                    sp.wait_ge(rows_split, 2)
                    sp.dma_start(brow2[0:1, :].bitcast(F32), brow_hi[:].bitcast(F32)).then_inc(row_two, 16)
                    sp.dma_start(brow2[1:2, :].bitcast(F32), brow_lo[:].bitcast(F32)).then_inc(row_two, 16)
                    sp.wait_ge(row_two, 32)
                    sp.wait_ge(zero_row, 16)

                @block.scalar
                def _(act):
                    def load(dst, name):
                        with nc.allow_non_contiguous_dma(reason="vectors down the partitions"):
                            act.dma_start(dst, col(a[name])).then_inc(loaded, 16)

                    for dst, name in ((ln1w[:], "ln1_weight"), (ln1b[:], "ln1_bias"), (ln2w[:], "ln2_weight"),
                                      (ln2b[:], "ln2_bias"), (lnq[:, 0], "lnq_g"), (lnq[:, 1], "lnq_b"),
                                      (lnk[:, 0], "lnk_g"), (lnk[:, 1], "lnk_b"), (lna[:, 0], "lna_g"),
                                      (lna[:, 1], "lna_b"), (bphi[:, 0], "bphi_q"), (bphi[:, 1], "bphi_k"),
                                      (b1c[:], "b1")):
                        load(dst, name)
                    act.wait_ge(loaded, 16 * LOADS)
                    act.activation(phik_zero[:], bphi[:, 1], ACT.Tanh).then_inc(phi_zero, 1)
                    step = Chain(act, act_step)
                    step(act.activation(w2_s[0][:], w2[:], ACT.Copy))
                    act.activation(wa_s[0][:], wa[:], ACT.Copy).then_inc(wa_high, 1)
                    act.wait_ge(sums_made, 1)
                    for j in range(HALVES):
                        step(act.activation(w1[:, j], w1[:, j], ACT.Copy, scale=lna[:, 0, j:j + 1]))
                    step(act.activation(w1_s[0][:], w1[:], ACT.Copy))

                @block.tensor
                def _(pe):
                    pe.wait_ge(setup_step, 5)
                    for j in range(HALVES):
                        pe.matmul(bank[0][:, 0:QKV], bcast[:, 0, j], wqkv[:, j], start=j == 0, stop=j == 1)
                    for j in range(HALVES):
                        pe.matmul(bank[1][:, 0:P], bcast[:, 1, j], wrouter[:, j], start=j == 0, stop=j == 1)
                    for n in range(HALVES):
                        for j in range(HALVES):
                            pe.matmul(bank[2][:, n:n + 1], wphi[:, 0, j, n * P:(n + 1) * P], lnq[:, 1, j:j + 1],
                                      start=j == 0, stop=j == 1)
                    for j in range(HALVES):
                        pe.matmul(bank[3][0:1, 0:E], lnk[:, 1, j:j + 1], wphi[:, 1, j], start=j == 0, stop=j == 1)
                    for n in range(MLP // P):
                        for j in range(HALVES):
                            last = pe.matmul(bank[4][:, n:n + 1], w1[:, j, n * P:(n + 1) * P], lna[:, 1, j:j + 1],
                                             start=j == 0, stop=j == 1)
                    last.then_inc(sums_made, 1)

                @block.vector
                def _(dve):
                    step = Chain(dve, setup_step)
                    dve.wait_ge(loaded, 16 * LOADS)
                    dve.wait_ge(router_in, 16)
                    dve.wait_ge(masks_made, 1)
                    for i, b in enumerate((ln1b, ln2b)):
                        for j in range(HALVES):
                            step(dve.tensor_scalar(bcast[:, i, j], ones_f[:], b[:, j:j + 1], None, ALU.mult))
                    step(dve.tensor_copy(one_row[:], ones_f[0:2, :]))
                    dve.wait_ge(sums_made, 1)
                    step(dve.tensor_copy(brow[:, ROW_QKV:], bank[0][0:1, 0:QKV]))
                    step(dve.tensor_copy(router_bias[:], bank[1][:, 0:NX]))
                    step(dve.tensor_tensor(phiq_bias[:], bank[2][:, 0:HALVES], bphi[:, 0], ALU.add))
                    step(dve.tensor_tensor(brow[:, ROW_PHIK:ROW_PHIK + E], bank[3][0:1, 0:E], extra[:, 0:E], ALU.add))
                    step(dve.tensor_tensor(b1c[:], bank[4][:, 0:MLP // P], b1c[:], ALU.add))
                    step(dve.tensor_scalar(brow[:, ROW_CONV:ROW_CONV + E], extra[:, E:2 * E], gamma[0:1, 0:1], None, ALU.mult))
                    step(dve.tensor_tensor(brow[:, ROW_OUT:ROW_OUT + E], extra[:, 2 * E:3 * E], extra[:, 3 * E:4 * E], ALU.add))
                    for j in range(HALVES):
                        for w, g in ((wqkv, ln1w), (wrouter, ln2w)):
                            step(dve.tensor_scalar(w[:, j], w[:, j], g[:, j:j + 1], None, ALU.mult))
                    dve.tensor_copy(brow_hi[:], brow[:]).then_inc(rows_split, 1)
                    dve.wait_ge(rows_split, 1)
                    dve.tensor_tensor(brow_lo[:], brow[:], brow_hi[:], ALU.subtract).then_inc(rows_split, 1)
                    dve.wait_ge(wa_high, 1)
                    dve.tensor_tensor(wa_s[1][:], wa[:], wa_s[0][:], ALU.subtract).then_inc(wa_high, 1)
                    dve.wait_ge(act_step, 4)
                    dve.tensor_tensor(w1_s[1][:], w1[:], w1_s[0][:], ALU.subtract).then_inc(w1_split, 1)
                    dve.wait_ge(phi_zero, 1)
                    step(dve.tensor_scalar(phik_zero[:], phik_zero[:], 1.0, None, ALU.add))

        with ExitStack() as own:
            x = [sb(f"x{p}", [P, S, E], F32, own) for p in range(2)]
            xn = [sb(f"xn{p}", [P, S, E], F32, own) for p in range(2)]
            stats = sb("stats", [P, S, 6], F32, own)
            mv = [sb(f"mv{p}", [P, S, 2], F32, own) for p in range(2)]
            norm = [sb(f"norm{p}", [P, 8, S], F32, own) for p in range(2)]
            xn1 = sb("xn_twice", [P, S, E], F32, own)
            xnt = sb("xnt", [P, HALVES, S * P], F32, own)
            qkv = [sb(f"qkv{p}", [P, S, QKV], F32, own) for p in range(2)]
            prod = sb("prod", [P, 10, E], F32, own)
            weighed = sb("weighed", [P, 7, E], F32, own)
            att = [sb(f"att{p}", [P, S, E], F32, own) for p in range(2)]
            score = sb("score", [P, S, H, S], F32, own)
            shifted = sb("shifted", [P, S, H, S], F32, own)
            prob = sb("prob", [P, S, H, S], F32, own)
            top = sb("top", [P, S * H], F32, own)
            total = sb("total", [P, S * H], F32, own)
            attt = sb("attt", [P, HALVES, S * P], F32, own)
            after = [sb(f"after{p}", [P, S, E], F32, own) for p in range(2)]
            stats2 = sb("stats2", [P, S, 6], F32, own)
            mv2 = [sb(f"mv2{p}", [P, S, 2], F32, own) for p in range(2)]
            norm2 = [sb(f"norm2{p}", [P, 4, S], F32, own) for p in range(2)]
            ln2 = [sb(f"ln2{p}", [P, S, E], F32, own) for p in range(2)]
            ln2t = sb("ln2t", [P, HALVES, S * P], F32, own)
            logit = sb("logit", [P, S, NX], F32, own)
            rprob = sb("rprob", [P, S, NX], F32, own)
            rtop = sb("rtop", [P, S], F32, own)
            rsum = sb("rsum", [P, S], F32, own)
            best = sb("best", [P, S, 8], F32, own)
            best_e = sb("best_e", [P, S, 8], U32, own)

            PAIRS = [(s, t) for s in range(S) for t in range(s + 1)]
            x_in = [sem("x_in0"), sem("x_in1")]
            x_stats, x_mv, x_norm, xn_made = sem("x_stats"), sem("x_mv"), sem("x_norm"), sem("xn_made")
            xn1_made = sem("xn1_made")
            xn_turned, xnt_made = sem("xn_turned"), sem("xnt_made")
            qkv_done, qkv_made = sem("qkv_done"), sem("qkv_made")
            mha_step, score_ready, exp_done, prob_made = sem("mha_step"), sem("score_ready"), sem("exp_done"), sem("prob_made")
            weighed_made = sem("weighed_made")
            att_turned, attt_made, proj_done, after_made = sem("att_turned"), sem("attt_made"), sem("proj_done"), sem("after_made")
            a_stats, a_mv, a_norm, ln2_made = sem("a_stats"), sem("a_mv"), sem("a_norm"), sem("ln2_made")
            ln2_turned, ln2t_made, router_done = sem("ln2_turned"), sem("ln2t_made"), sem("router_done")
            router_step, rexp_done = sem("router_step"), sem("rexp_done")
            ln2_out, after_out = [sem("ln2_out0"), sem("ln2_out1")], [sem("after_out0"), sem("after_out1")]
            masked_out = sem("masked_out")
            X_NORM, A_NORM = 8, 4
            MHA, ROUTE = 9, 10

            def rows_of(dram, step):
                return dram.rearrange("(s b p) e -> p b s e", s=S, p=P)[:, bass.ds(step.n, 1)].rearrange("p b s e -> p (b s) e")

            def sums_of(s):
                return bank[6 + s // 2][:, s % 2 * E:(s % 2 + 1) * E]

            with nc.Block() as block:
                @block.sync
                def _(sp):
                    def turn(t):
                        if exists(t, BT):
                            if later(t, 2):
                                sp.wait_ge(xn_made, t.n * S - S)
                            sp.dma_start(x[t.odd][:], rows_of(a["x"], t)).then_inc(x_in[t.odd], 16)
                            sp.dma_start(buf_d.rearrange("(x p n) e -> p x n e", x=NX, p=P)[:, bass.ds(t.n, 1)]
                                         .rearrange("p x n e -> p (x n) e"), zeros[:]).then_inc(zero_fill, 16)
                        t = t.back(3)
                        if exists(t, BT):
                            sp.wait_ge(after_made, t.n * 2 + 2)
                            sp.dma_start(rows_of(after_d, t), after[t.odd][:]).then_inc(after_out[t.odd], 16)
                            sp.wait_ge(ln2_made, t.n * S + S)
                            sp.dma_start(rows_of(ln2_d, t), ln2[t.odd][:]).then_inc(ln2_out[t.odd], 16)
                    turns(sp, BT, 3, turn, 5)
                    for q in (*ln2_out, *after_out):
                        sp.wait_ge(q, 16 * BT // 2)
                    sp.wait_ge(zero_fill, 16 * NX)

                @block.gpsimd
                def _(pool):
                    def inverse_root(out_, var, eps, step, tmp):
                        step(pool.tensor_scalar(tmp, var, eps, None, ALU.add))
                        step(pool.tensor_tensor(out_, tmp, neg_half[:, 0:S], ALU.pow))

                    def turn(t0):
                        t = t0
                        if exists(t, BT):
                            mean, var = mv[t.odd][:, :, 0], mv[t.odd][:, :, 1]
                            n = norm[t.odd]
                            hold(pool, x_mv, t.n * S + S, pool_passed)
                            step = Chain(pool, x_norm, t.n * X_NORM, pool_passed)
                            inverse_root(n[:, 0], var, EPS, step, n[:, 3])
                            step(pool.tensor_tensor(n[:, 4], mean, n[:, 0], ALU.mult))
                            step(pool.tensor_scalar(n[:, 1], n[:, 4], -1.0, None, ALU.mult))
                            step(pool.tensor_tensor(n[:, 5], n[:, 0], n[:, 0], ALU.mult))
                            step(pool.tensor_tensor(n[:, 6], n[:, 5], var, ALU.mult))
                            inverse_root(n[:, 2], n[:, 6], EPS, step, n[:, 7])
                        t = t0.back(2)
                        if exists(t, BT):
                            mean, var = mv2[t.odd][:, :, 0], mv2[t.odd][:, :, 1]
                            n = norm2[t.odd]
                            hold(pool, a_mv, t.n * S + S, pool_passed)
                            step = Chain(pool, a_norm, t.n * A_NORM, pool_passed)
                            inverse_root(n[:, 0], var, EPS, step, n[:, 2])
                            step(pool.tensor_tensor(n[:, 3], mean, n[:, 0], ALU.mult))
                            step(pool.tensor_scalar(n[:, 1], n[:, 3], -1.0, None, ALU.mult))
                        t = t0.back(1)
                        if exists(t, BT):
                            pool.wait_ge(prob_made, t.n + 1)
                            if later(t, 1):
                                pool.wait_ge(mha_step, t.n * MHA)
                            for i, (s, u) in enumerate(PAIRS[3:]):
                                value = qkv[t.odd][:, u, E + KVH * D:].rearrange("p (g d) -> p g d", d=D)
                                pool.tensor_tensor(
                                    weighed[:, i].rearrange("p (g r d) -> p g r d", r=REP, d=D),
                                    value.unsqueeze(2).to_broadcast((P, KVH, REP, D)),
                                    prob[:, s, :, u].rearrange("p (g r) -> p g r", r=REP).unsqueeze(3).to_broadcast((P, KVH, REP, D)),
                                    ALU.mult).then_inc(weighed_made, 1)
                    turns(pool, BT, 2, turn, 4)

                @block.scalar
                def _(act):
                    def turn(t0):
                        t = t0.back(2)
                        if exists(t, BT):
                            act.wait_ge(att_turned, t.n + 1)
                            if later(t, 1):
                                act.wait_ge(proj_done, t.n * 2)
                            for j in range(HALVES):
                                act.activation(attt[:, j], bank[2 + j][:], ACT.Copy).then_inc(attt_made, 1)
                        t = t0.back(3)
                        if exists(t, BT):
                            act.wait_ge(ln2_turned, t.n + 1)
                            if later(t, 1):
                                act.wait_ge(router_done, t.n)
                            for j in range(HALVES):
                                act.activation(ln2t[:, j], bank[2 + j][:], ACT.Copy).then_inc(ln2t_made, 1)
                        t = t0
                        if exists(t, BT):
                            act.wait_ge(x_norm, t.n * X_NORM + 4)
                            if later(t, 2):
                                act.wait_ge(proj_done, t.n * 2 - 2)
                            for s in range(S):
                                act.activation(xn[t.odd][:, s], x[t.odd][:, s], ACT.Identity,
                                               bias=norm[t.odd][:, 1, s:s + 1], scale=norm[t.odd][:, 0, s:s + 1]).then_inc(xn_made, 1)
                            act.wait_ge(x_norm, t.n * X_NORM + X_NORM)
                            act.wait_ge(xn_made, t.n * S + S)
                            if later(t, 1):
                                act.wait_ge(xn_turned, t.n)
                            for s in range(S):
                                act.activation(xn1[:, s], xn[t.odd][:, s], ACT.Copy,
                                               scale=norm[t.odd][:, 2, s:s + 1]).then_inc(xn1_made, 1)
                        t = t0
                        if exists(t, BT):
                            act.wait_ge(xn_turned, t.n + 1)
                            if later(t, 1):
                                act.wait_ge(qkv_done, t.n * S)
                            for j in range(HALVES):
                                act.activation(xnt[:, j], bank[j][:], ACT.Copy).then_inc(xnt_made, 1)
                        t = t0.back(1)
                        if exists(t, BT):
                            act.wait_ge(score_ready, t.n + 1)
                            act.activation(prob[:], shifted[:], ACT.Exp, scale=float(D) ** -0.5).then_inc(exp_done, 1)
                        t = t0.back(3)
                        if exists(t, BT):
                            act.wait_ge(router_step, t.n * ROUTE + 3)
                            act.activation(rprob[:], logit[:], ACT.Exp).then_inc(rexp_done, 1)
                        t = t0.back(2)
                        if exists(t, BT):
                            act.wait_ge(a_mv, t.n * S + S)
                            if later(t, 2):
                                act.wait_ge(after_out[t.odd], t.half * 16)
                            for k in range(2):
                                act.activation(after[t.odd][:, 2 * k:2 * k + 2].rearrange("p s e -> p (s e)"), bank[6 + k][:],
                                               ACT.Copy).then_inc(after_made, 1)
                            act.wait_ge(a_norm, t.n * A_NORM + A_NORM)
                            if later(t, 2):
                                act.wait_ge(ln2_out[t.odd], t.half * 16)
                                act.wait_ge(ln2_turned, t.n - 1)
                            for s in range(S):
                                act.activation(ln2[t.odd][:, s], sums_of(s), ACT.Identity,
                                               bias=norm2[t.odd][:, 1, s:s + 1], scale=norm2[t.odd][:, 0, s:s + 1]).then_inc(ln2_made, 1)
                        t = t0
                        if exists(t, BT):
                            if later(t, 2):
                                act.wait_ge(mha_step, t.n * MHA - MHA)
                            for s in range(S):
                                act.wait_ge(qkv_done, t.n * S + s + 1)
                                act.activation(qkv[t.odd][:, s], bank[4 + s % 2][:, 0:QKV], ACT.Copy).then_inc(qkv_made, 1)
                    turns(act, BT, 3, turn, 5)

                @block.tensor
                def _(pe):
                    def turned(src, banks, done):
                        for j in range(HALVES):
                            for s in range(S):
                                last = pe.transpose(banks[j][:, s * P:(s + 1) * P], src[:, s, j * P:(j + 1) * P], ident[:])
                        last.then_inc(done, 1)

                    def turn(t0):
                        t = t0.back(2)
                        if exists(t, BT):
                            pe.wait_ge(mha_step, t.n * MHA + MHA)
                            if later(t, 2):
                                pe.wait_ge(ln2t_made, t.n * 2 - 2)
                            turned(att[t.odd], bank[2:4], att_turned)
                            if later(t, 1):
                                pe.wait_ge(ln2_made, t.n * S)
                            for k in range(2):
                                pe.matmul(bank[6 + k][:], ident[:], xn[t.odd][:, 2 * k:2 * k + 2].rearrange("p s e -> p (s e)"),
                                          start=True, stop=False)
                        t = t0.back(3)
                        if exists(t, BT):
                            pe.wait_ge(ln2_made, t.n * S + S)
                            if exists(t.back(-1), BT):
                                pe.wait_ge(attt_made, t.n * 2 + 4)
                            turned(ln2[t.odd], bank[2:4], ln2_turned)
                        t = t0.back(2)
                        if exists(t, BT):
                            pe.wait_ge(attt_made, t.n * 2 + 2)
                            for s in range(S):
                                for j in range(HALVES):
                                    mm = pe.matmul(bank[6 + s // 2][:, s % 2 * E:(s % 2 + 1) * E], attt[:, j, s * P:(s + 1) * P],
                                                   wproj[:, j], start=False, stop=s % 2 == 1 and j == 1)
                                if s % 2:
                                    mm.then_inc(proj_done, 1)
                        t = t0.back(3)
                        if exists(t, BT):
                            pe.wait_ge(ln2t_made, t.n * 2 + 2)
                            if exists(t.back(-2), BT):
                                pe.wait_ge(qkv_made, t.back(-2).n * S + S)
                            else:
                                pe.wait_ge(qkv_made, BT * S)
                            for s in range(S):
                                for j in range(HALVES):
                                    mm = pe.matmul(bank[4][:, s * P:(s + 1) * P], ln2t[:, j, s * P:(s + 1) * P], wrouter[:, j],
                                                   start=j == 0, stop=j == 1)
                            mm.then_inc(router_done, 1)
                        t = t0
                        if exists(t, BT):
                            pe.wait_ge(xn1_made, t.n * S + S)
                            if later(t, 1):
                                pe.wait_ge(xnt_made, t.n * 2)
                            turned(xn1, bank[0:2], xn_turned)
                        t = t0
                        if exists(t, BT):
                            pe.wait_ge(xnt_made, t.n * 2 + 2)
                            for s in range(S):
                                if s == 0 and later(t, 3):
                                    pe.wait_ge(router_step, t.n * ROUTE - 3 * ROUTE + 1)
                                if s >= 2 or later(t, 1):
                                    pe.wait_ge(qkv_made, t.n * S + s - 1)
                                pe.matmul(bank[4 + s % 2][:, 0:QKV], one_row[:], brow2[:, ROW_QKV:], start=True, stop=False)
                                for j in range(HALVES):
                                    mm = pe.matmul(bank[4 + s % 2][:, 0:QKV], xnt[:, j, s * P:(s + 1) * P], wqkv[:, j],
                                                   start=False, stop=j == 1)
                                mm.then_inc(qkv_done, 1)

                    turns(pe, BT, 3, turn, 5)

                @block.vector
                def _(dve):
                    dve.memset(score[:], -1e30).then_inc(masked_out, 1)
                    dve.wait_ge(masked_out, 1)

                    def moments(src, tmp, dst, done_stats, done, t):
                        if later(t, 1):
                            dve.wait_ge(done, t.n * S)
                        for s in range(S):
                            dve.bn_stats(tmp[:, s], src[s]).then_inc(done_stats, 1)
                        hold(dve, done_stats, t.n * S + S, dve_passed)
                        for s in range(S):
                            dve.bn_aggr(dst[:, s], tmp[:, s]).then_inc(done, 1)

                    def front_stats(t):
                        dve.wait_ge(x_in[t.odd], t.half * 16 + 16)
                        moments([x[t.odd][:, s] for s in range(S)], stats, mv[t.odd], x_stats, x_mv, t)

                    def residual(t):
                        dve.wait_ge(proj_done, t.n * 2 + 2)
                        moments([sums_of(s) for s in range(S)], stats2, mv2[t.odd], a_stats, a_mv, t)

                    def products(t):
                        q = qkv[t.odd]
                        dve.wait_ge(qkv_made, t.n * S + S)
                        step = Chain(dve, mha_step, t.n * MHA)
                        if later(t, 1):
                            dve.wait_ge(mha_step, t.n * MHA)
                        for i, (s, u) in enumerate(PAIRS):
                            key = q[:, u, E:E + KVH * D].rearrange("p (g d) -> p g d", d=D).unsqueeze(2).to_broadcast((P, KVH, REP, D))
                            mul = dve.tensor_tensor(prod[:, i].rearrange("p (g r d) -> p g r d", r=REP, d=D),
                                                    q[:, s, 0:E].rearrange("p (g r d) -> p g r d", r=REP, d=D), key, ALU.mult)
                        step(mul)
                        return step

                    def scores(t, step):
                        for s in range(S):
                            first = PAIRS.index((s, 0))
                            red = dve.tensor_reduce(score[:, s, :, 0:s + 1].rearrange("p h u -> p u h"),
                                                    prod[:, first:first + s + 1].rearrange("p u (h d) -> p u h d", d=D), AX_X, ALU.add)
                        step(red)
                        step(dve.tensor_reduce(top[:], score[:].rearrange("p s h u -> p (s h) u"), AX_X, ALU.max))
                        dve.tensor_tensor(shifted[:].rearrange("p s h u -> p (s h) u"), score[:].rearrange("p s h u -> p (s h) u"),
                                          top[:].unsqueeze(2).to_broadcast((P, S * H, S)), ALU.subtract).then_inc(score_ready, 1)

                    def weigh(t, step):
                        dve.wait_ge(exp_done, t.n + 1)
                        flat = prob[:].rearrange("p s h u -> p (s h) u")
                        step(dve.tensor_reduce(total[:], flat, AX_X, ALU.add))
                        step(dve.reciprocal(total[:], total[:]))
                        dve.tensor_tensor(flat, flat, total[:].unsqueeze(2).to_broadcast((P, S * H, S)), ALU.mult).then_inc(prob_made, 1)
                        dve.wait_ge(prob_made, t.n + 1)
                        for i, (s, u) in enumerate(PAIRS[:3]):
                            value = qkv[t.odd][:, u, E + KVH * D:].rearrange("p (g d) -> p g d", d=D)
                            mul = dve.tensor_tensor(
                                (att[t.odd][:, 0] if s == 0 else prod[:, i]).rearrange("p (g r d) -> p g r d", r=REP, d=D),
                                value.unsqueeze(2).to_broadcast((P, KVH, REP, D)),
                                prob[:, s, :, u].rearrange("p (g r) -> p g r", r=REP).unsqueeze(3).to_broadcast((P, KVH, REP, D)),
                                ALU.mult)
                        step(mul)
                        step(dve.tensor_tensor(att[t.odd][:, 1], prod[:, 1], prod[:, 2], ALU.add))

                    def weigh_rest(t, step):
                        dve.wait_ge(weighed_made, t.n * 7 + 3)
                        step(dve.tensor_reduce(att[t.odd][:, 2], weighed[:, 0:3].rearrange("p u c -> p c u"), AX_X, ALU.add))
                        dve.wait_ge(weighed_made, t.n * 7 + 7)
                        step(dve.tensor_reduce(att[t.odd][:, 3], weighed[:, 3:7].rearrange("p u c -> p c u"), AX_X, ALU.add))

                    def route_scores(t):
                        step = Chain(dve, router_step, t.n * ROUTE)
                        dve.wait_ge(router_done, t.n + 1)
                        step(dve.tensor_tensor(logit[:], bank[4][:].rearrange("p (s n) -> p s n", s=S)[:, :, 0:NX],
                                               router_bias[:].unsqueeze(1).to_broadcast((P, S, NX)), ALU.add))
                        step(dve.tensor_reduce(rtop[:], logit[:], AX_X, ALU.max))
                        step(dve.tensor_tensor(logit[:], logit[:], rtop[:].unsqueeze(2).to_broadcast((P, S, NX)), ALU.subtract))
                        return step

                    def pick(t, step):
                        dve.wait_ge(rexp_done, t.n + 1)
                        step(dve.tensor_reduce(rsum[:], rprob[:], AX_X, ALU.add))
                        step(dve.reciprocal(rsum[:], rsum[:]))
                        step(dve.tensor_tensor(rprob[:], rprob[:], rsum[:].unsqueeze(2).to_broadcast((P, S, NX)), ALU.mult), dve_passed)
                        for s in range(S):
                            largest = dve.max(best[:, s], rprob[:, s])
                        step(largest, dve_passed)
                        for s in range(S):
                            at = dve.max_index(best_e[:, s], best[:, s], rprob[:, s])
                        step(at)
                        for dst, src in ((top_p, best), (top_e, best_e)):
                            step(dve.tensor_copy(dst[:, :, bass.ds(t.n, 1), :].rearrange("p s b k -> p (s b) k"), src[:, :, 0:2]))

                    def turn(t0):
                        if exists(t0, BT):
                            front_stats(t0)
                        if exists(t0.back(1), BT):
                            mha = products(t0.back(1))
                        if exists(t0.back(2), BT):
                            residual(t0.back(2))
                        if exists(t0.back(1), BT):
                            scores(t0.back(1), mha)
                        if exists(t0.back(3), BT):
                            route = route_scores(t0.back(3))
                        if exists(t0.back(1), BT):
                            weigh(t0.back(1), mha)
                        if exists(t0.back(3), BT):
                            pick(t0.back(3), route)
                            assert route.done == ROUTE, route.done
                        if exists(t0.back(1), BT):
                            weigh_rest(t0.back(1), mha)
                            assert mha.done == MHA, mha.done
                    turns(dve, BT, 3, turn, 5)

        with ExitStack() as own:
            hot = [sb(f"hot{k}", [P, TILES, NX], F32, own) for k in range(2)]
            chosen = sb("chosen", [P, TILES, NX], BF16, own)
            counts = sb("counts", [TILES, NX], F32, own)
            before = sb("before", [TILES, TILES, NX], BF16, own)
            place = sb("place", [P, TILES, NX], F32, own)
            pos = sb("pos", [P, TILES, 2], F32, own)
            keep = sb("keep", [P, TILES, 2], F32, own)
            slot = sb("slot", [P, TILES, 2], F32, own)
            route_step, counted, placed = sem("route_step"), sem("counted"), sem("placed")
            experts_of = top_e[:].rearrange("p s b k -> p (s b) k")
            probs_of = top_p[:].rearrange("p s b k -> p (s b) k")

            with nc.Block() as block:
                @block.tensor
                def _(pe):
                    pe.wait_ge(route_step, 3)
                    for e in range(NX):
                        mm = pe.matmul(bank[0][0:TILES, e:e + 1], chosen[:, :, e], ones_b[:, 0:1], start=True, stop=True)
                    mm.then_inc(counted, 1)
                    for half in range(2):
                        pe.matmul(bank[1 + half][:], tri[:], chosen[:, half * 32:half * 32 + 32].rearrange("p t e -> p (t e)"),
                                  start=True, stop=False)
                    pe.wait_ge(route_step, 5)
                    for half in range(2):
                        mm = pe.matmul(bank[1 + half][:], ones_b[0:TILES, :],
                                       before[:, half * 32:half * 32 + 32].rearrange("p t e -> p (t e)"), start=False, stop=True)
                    mm.then_inc(placed, 1)

                @block.vector
                def _(dve):
                    step = Chain(dve, route_step)
                    for k in range(2):
                        step(dve.tensor_tensor(hot[k][:], iota_e[:].unsqueeze(1).to_broadcast((P, TILES, NX)),
                                               experts_of[:, :, k].unsqueeze(2).to_broadcast((P, TILES, NX)), ALU.is_equal))
                    step(dve.tensor_tensor(chosen[:], hot[0][:], hot[1][:], ALU.add))
                    dve.wait_ge(counted, 1)
                    step(dve.tensor_copy(counts[:], bank[0][0:TILES, 0:NX]))
                    step(dve.tensor_tensor(before[:], earlier[:].unsqueeze(2).to_broadcast((TILES, TILES, NX)),
                                           counts[:].unsqueeze(1).to_broadcast((TILES, TILES, NX)), ALU.mult))
                    dve.wait_ge(placed, 1)
                    for k in range(2):
                        for half in range(2):
                            part = slice(half * 32, half * 32 + 32)
                            mul = dve.tensor_tensor(place[:, part], bank[1 + half][:].rearrange("p (t e) -> p t e", e=NX),
                                                    hot[k][:, part], ALU.mult)
                        step(mul)
                        step(dve.tensor_reduce(pos[:, :, k], place[:], AX_X, ALU.add))
                    step(dve.tensor_scalar(keep[:], pos[:], float(CAP), None, ALU.is_lt))
                    step(dve.scalar_tensor_tensor(slot[:], experts_of, float(CAP), pos[:], ALU.mult, ALU.add))
                    step(dve.tensor_tensor(gate[:], probs_of, keep[:], ALU.mult))
                    for dst, other in ((to_row, FAR), (from_row, SLOTS)):
                        step(dve.scalar_tensor_tensor(pos[:], slot[:], float(-other), keep[:], ALU.add, ALU.mult))
                        step(dve.tensor_scalar(dst[:], pos[:], float(other), None, ALU.add))

        front_only.close()
        ax_in = [sem("ax_in0"), sem("ax_in1")]
        ax_stats, ax_mv, ax_norm, axn_made = sem("ax_stats"), sem("ax_mv"), sem("ax_norm"), sem("axn_made")
        xt_done, xt_high, xt_made = sem("xt_done"), sem("xt_high"), sem("xt_made")
        aq_done, aq_stats, aq_mv, aq_norm, qkvn_made = (
            sem("aq_done"), sem("aq_stats"), sem("aq_mv"), sem("aq_norm"), sem("qkvn_made"))
        qkt_done, qt_made, kt_made = sem("qkt_done"), sem("qt_made"), sem("kt_made")
        phik_done, tk_made, phiq_done, tq_made = sem("phik_done"), sem("tk_made"), sem("phiq_done"), sem("tq_made")
        mean_step, score_done, max_step, alpha_exp, norm_step = (
            sem("mean_step"), sem("score_done"), sem("max_step"), sem("alpha_exp"), sem("norm_step"))
        alpha_turned, alpha_made, pks_made, kv_done, kv_step = (
            sem("alpha_turned"), sem("alpha_made"), sem("pks_made"), sem("kv_done"), sem("kv_step"))
        tq_plus, nd_done, attn_step, attn_turned, attnt_made = (
            sem("tq_plus"), sem("nd_done"), sem("attn_step"), sem("attn_turned"), sem("attnt_made"))
        conv_done, c_stats, c_mv, c_norm, an_made, res_step = (
            sem("conv_done"), sem("c_stats"), sem("c_mv"), sem("c_norm"), sem("an_made"), sem("res_step"))
        an_turned, ant_made, up_done, gel_made, down_done, s_made = (
            sem("an_turned"), sem("ant_made"), sem("up_done"), sem("gel_made"), sem("down_done"), sem("s_made"))
        s_out = [sem("s_out0"), sem("s_out1")]
        lt_in, scattered, where_made = [sem("lt_in0"), sem("lt_in1")], [sem("scattered0"), sem("scattered1")], sem("where_made")
        ant_high, gel_split = sem("ant_high"), sem("gel_split")
        vn_ones = sem("vn_ones")
        ends_zero = sem("ends_zero")
        F_CHUNKS = MLP // P
        PHI_BANKS = ((6, 7), (6, 7), (0, 1), (4, 5))
        PAIR = 2
        PAIRS_A = BT // PAIR
        SCATTERS, GATHERS = TILES // 2, 24
        job_in, picked_in, job_out = (
            [sem("job_in0"), sem("job_in1")], [sem("job_picked0"), sem("job_picked1")], [sem("job_out0"), sem("job_out1")])
        job_step, job_mixed, job_silu, job_made = sem("job_step"), sem("job_mixed"), sem("job_silu"), sem("job_made")
        JOBS_AHEAD = 2
        MEANS, MAXS, NORMS, KVS = 10, 7, 4, 14

        def attend(first, scatters):
            JOBS = SCATTERS if scatters else GATHERS
            with ExitStack() as own:
                def mine(name, shape, dt=F32):
                    return sb(f"{name}_{first}", shape, dt, own)

                xa_both = mine("xa", [P, 2, GROUP, E])
                xa = [xa_both[:, p] for p in range(2)]
                alpha_t = xa_both[0:H].rearrange("h a i e -> h (a i e)")
                xstats = mine("xstats", [P, GROUP, 6])
                xmv = [mine(f"xmv{p}", [P, GROUP, 2]) for p in range(2)]
                xnorm = [mine(f"xnorm{p}", [P, 4, GROUP]) for p in range(2)]
                xnb = mine("xnb", [P, BT, E])
                xtile = [[mine(f"xtile_{w}{p}", [P, HALVES, P], F32R) for w in ("hi", "lo")] for p in range(2)]
                qstats = mine("qstats", [P, 3, 6])
                qmv = [mine(f"qmv{p}", [P, 3, 2]) for p in range(2)]
                qnorm = [mine(f"qnorm{p}", [P, 4, 3]) for p in range(2)]
                qkn = [mine(f"qkn{p}", [P, 2 * E]) for p in range(2)]
                vn = mine("vn", [P, BT, HALVES, P + 1])
                knt = mine("knt", [P, HALVES, NB + 4])
                attnt = knt
                qpart = mine("qpart", [P, HALVES, BT])
                tk = mine("tk", [P, BT, E])
                tq = mine("tq", [P, HALVES, NB])
                qmean = mine("qmean", [P, HALVES])
                qmean_k = mine("qmean_k", [P, HALVES])
                qheads = mine("qheads", [P, HALVES, H])
                qheads_k = mine("qheads_k", [P, HALVES, H])
                small = mine("small", [H, 24])
                alpha = mine("alpha", [P, BT, H])
                spread = mine("spread", [P, HALVES, 2])
                pks = [mine(f"pks{p}", [P, E]) for p in range(2)]
                kvt = mine("kvt", [P, HALVES, P])
                ksum = mine("ksum", [P, HALVES, 2])
                kvblk = mine("kvblk", [P, HALVES, P + 8])
                den = mine("den", [P, HALVES, 8])
                gel = tk[:, 0:4]
                attn = [tk[:, 4 + p] for p in range(2)]
                an = [tk[:, 6 + p] for p in range(2)]
                gained = tk[:, 8]
                cstats = mine("cstats", [P, 6])
                cmv = [mine(f"cmv{p}", [P, 2]) for p in range(2)]
                cnorm = [mine(f"cnorm{p}", [P, 4]) for p in range(2)]
                ant_s = [[mine(f"ant_{w}{p}", [P, HALVES, PAIR * P], F32R) for w in ("hi", "lo")] for p in range(2)]
                gel_s = [mine(f"gel_{w}", [P, MLP // P, PAIR * P], F32R) for w in ("hi", "lo")]
                sout = [mine(f"sout{p}", [P, E]) for p in range(2)]
                where = mine("where", [P, JOBS, 2], I32)
                if scatters:
                    lt = [mine(f"lt{p}", [P, E]) for p in range(2)]
                else:
                    picked = [mine(f"job_picked{p}", [P, 2, E]) for p in range(2)]
                    job_after, job_s, job_x = ([mine(f"job_{w}{p}", [P, E]) for p in range(2)] for w in ("after", "s", "x"))

                def jobs_early(i):
                    return [i // 2] if i % 2 and 0 <= i < BT else []

                def jobs_late(i):
                    if not 0 <= i < BT:
                        return []
                    each = (JOBS - 8) / BT
                    return list(range(8 + int(each * i), 8 + int(each * (i + 1))))

                def count(h, j, each):
                    return h * (JOBS * each) + (j + 1) * each

                def count_of(h, j, each):
                    return h * (JOBS // 2 * each) + (j // 2 + 1) * each

                def tile_of(h, j):
                    return bass.ds(h * JOBS + j, 1)

                def tiles(ap, h, j):
                    return ap.rearrange("(t p) e -> p t e", p=P)[:, tile_of(h, j)].rearrange("p a e -> p (a e)")

                with nc.Block() as block:
                    @block.sync
                    def _(sp):
                        x_groups = a["x"].rearrange("(g i p) e -> p g i e", i=GROUP, p=P)
                        for g in range(2):
                            sp.dma_start(xa[g], x_groups[:, first * GROUPS + g]).then_inc(ax_in[g], 16)
                        if not scatters:
                            for q in job_out:
                                sp.sem_inc(q, 16)
                        with sp.Fori(0, 2) as h:
                            b = h + first
                            def next_x():
                                hold(sp, alpha_turned, b + 1, sp_passed)
                                for g in range(2):
                                    sp.dma_start(xa[g], x_groups[:, bass.ds(h * (-GROUPS) + ((first + 1) * GROUPS + g), 1)]
                                                 .rearrange("p a i e -> p (a i) e")).then_inc(ax_in[g], 16)

                            def load_x(g):
                                hold(sp, axn_made, b * BT + (g - 1) * GROUP, sp_passed)
                                sp.dma_start(xa[g % 2], x_groups[:, bass.ds(b * GROUPS + g, 1)].rearrange("p a i e -> p (a i) e")).then_inc(ax_in[g % 2], 16)

                            def load(j):
                                p = j % 2
                                if scatters:
                                    if j >= 2:
                                        hold(sp, scattered[p], count_of(h, j - 2, 32), sp_passed)
                                    sp.dma_start(lt[p][:], tiles(ln2_d, h, j)).then_inc(lt_in[p], 16)
                                    return
                                hold(sp, job_made, count(h, j - 2, 1) + JOBS_AHEAD, sp_passed)
                                hold(sp, job_out[p], count_of(h, j - 2, 16) + 16, sp_passed)
                                for dst, src in ((job_after, after_d), (job_s, s_d), (job_x, a["x"])):
                                    sp.dma_start(dst[p][:], tiles(src, h, j)).then_inc(job_in[p], 16)

                            def store(j):
                                hold(sp, job_made, count(h, j, 1) + JOBS_AHEAD, sp_passed)
                                sp.dma_start(tiles(out, h, j), job_x[j % 2][:]).then_inc(job_out[j % 2], 16)

                            def store_s(i):
                                hold(sp, s_made, b * BT + i + 1, sp_passed)
                                sp.dma_start(s_d.rearrange("(t p) e -> p t e", p=P)[:, bass.ds(b * BT + i, 1)]
                                             .rearrange("p a e -> p (a e)"), sout[i % 2][:]).then_inc(s_out[i % 2], 16)

                            load(0)
                            load(1)
                            load_x(2)
                            load_x(3)
                            if scatters:
                                for j in range(2, 8):
                                    load(j)
                                for i in range(BT + 5):
                                    for j in jobs_late(i):
                                        load(j)
                                    if i == 0:
                                        next_x()
                                    if i >= 5:
                                        store_s(i - 5)
                            else:
                                for j in range(JOBS):
                                    store(j)
                                    if j + 2 < JOBS:
                                        load(j + 2)
                                    if j == 8:
                                        next_x()
                                    if j >= 9:
                                        store_s(j - 9)
                                store_s(BT - 1)
                            for q in scattered if scatters else ():
                                hold(sp, q, count_of(h, JOBS - 1, 32), sp_passed)
                            for q in s_out:
                                hold(sp, q, b * (BT // 2 * 16) + (BT // 2 * 16 + 16), sp_passed)
                        if not scatters:
                            for q in job_out:
                                sp.wait_ge(q, 16 * GATHERS + 16)
                        for g in range(2):
                            sp.wait_ge(ax_in[g], (first // 2 + 1) * 80)
                        for q in s_out:
                            sp.wait_ge(q, 16 * (first + 2) * BT // 2 + 16)

                    @block.gpsimd
                    def _(pool):
                        pool.memset(vn[:, :, :, P:P + 1].rearrange("p i j c -> p (i j) c"), 1.0).then_inc(vn_ones, 1)

                        def inverse_root(n, mv_, step):
                            width = n[0].shape[-1]
                            step.also(pool.tensor_scalar(n[3], mv_[0], -1.0, None, ALU.mult))
                            step(pool.tensor_scalar(n[2], mv_[1], EPS, None, ALU.add))
                            step(pool.tensor_tensor(n[0], n[2], neg_half[:, 0:width], ALU.pow))
                            step(pool.tensor_tensor(n[1], n[3], n[0], ALU.mult))

                        with pool.Fori(0, 2) as h:
                            b = h + first
                            def norm_x(g):
                                hold(pool, ax_mv, b * BT + g * GROUP + GROUP, pool_passed)
                                inverse_root([xnorm[g % 2][:, k] for k in range(4)], [xmv[g % 2][:, :, k] for k in range(2)],
                                             Chain(pool, ax_norm, b * 4 * GROUPS + 4 * g, pool_passed))

                            def job(j):
                                p = j % 2
                                if scatters:
                                    hold(pool, lt_in[p], count_of(h, j, 16), pool_passed)
                                else:
                                    hold(pool, job_made, count(h, j - 2, 1) + JOBS_AHEAD, pool_passed)
                                for k in range(2):
                                    rows = bass.IndirectOffsetOnAxis(where[:, j, k:k + 1], axis=0)
                                    if scatters:
                                        pool.indirect_dma_start(buf_d, rows, lt[p][:], None, bounds_check=SLOTS - 1,
                                                                oob_is_err=False).then_inc(scattered[p], 16)
                                    else:
                                        pool.indirect_dma_start(picked[p][:, k], None, h2_d, rows).then_inc(picked_in[p], 16)

                            pool.tensor_copy(where[:], (to_row if scatters else from_row)[:, bass.ds(h * JOBS, JOBS)]
                                             ).then_inc(where_made, 1)
                            hold(pool, where_made, b + 1, pool_passed)
                            norm_x(0)
                            for i in range(BT + 2):
                                if 1 <= i <= BT:
                                    k = i - 1
                                    hold(pool, aq_mv, b * (3 * BT) + 3 * k + 3, pool_passed)
                                    inverse_root([qnorm[k % 2][:, r] for r in range(4)], [qmv[k % 2][:, :, r] for r in range(2)],
                                                 Chain(pool, aq_norm, b * (4 * BT) + 4 * k, pool_passed))
                                if i % GROUP == 0 and i // GROUP + 1 < GROUPS:
                                    norm_x(i // GROUP + 1)
                                for j in jobs_early(i):
                                    job(j)
                            for i in range(BT):
                                hold(pool, c_mv, b * BT + i + 1, pool_passed)
                                inverse_root([cnorm[i % 2][:, r:r + 1] for r in range(4)], [cmv[i % 2][:, r:r + 1] for r in range(2)],
                                             Chain(pool, c_norm, b * (4 * BT) + 4 * i, pool_passed))
                                for j in jobs_late(i):
                                    job(j)
                                step = Chain(pool, res_step, b * (2 * BT) + 2 * i)
                                pool.wait_ge(an_made, b * BT + i + 1)
                                step(pool.tensor_tensor(gained, an[i % 2], ga_row[:], ALU.mult))
                                step(pool.tensor_tensor(xnb[:, i], xnb[:, i], gained, ALU.add))
                            if scatters:
                                for q in scattered:
                                    hold(pool, q, count_of(h, JOBS - 1, 32), pool_passed)
                            else:
                                for q in picked_in:
                                    hold(pool, q, count_of(h, JOBS - 1, 32), pool_passed)
                            pool.wait_ge(s_made, b * BT + BT)

                    @block.scalar
                    def _(act):
                        with act.Fori(0, 2) as h:
                            b = h + first
                            def silu(jobs):
                                for j in () if scatters else jobs:
                                    act.wait_ge(job_mixed, count(h, j, 1))
                                    act.activation(picked[j % 2][:, 1], picked[j % 2][:, 0], ACT.Tanh, scale=0.5).then_inc(job_silu, 1)

                            def norm_x(i):
                                g, k = i // GROUP, i % GROUP
                                if k == 0:
                                    act.wait_ge(ax_norm, b * 4 * GROUPS + 4 * g + 4)
                                act.activation(xnb[:, i], xa[g % 2][:, k], ACT.Identity,
                                               bias=xnorm[g % 2][:, 1, k:k + 1], scale=xnorm[g % 2][:, 0, k:k + 1]).then_inc(axn_made, 1)

                            for i in range(GROUP):
                                norm_x(i)
                            for i in range(BT + 4):
                                if i < BT:
                                    act.wait_ge(xt_done, b * BT + i + 1)
                                    if i >= 2:
                                        act.wait_ge(aq_done, b * BT + i - 1)
                                    act.activation(xtile[i % 2][0][:].rearrange("p j c -> p (j c)"), bank[0][:, 0:E], ACT.Copy).then_inc(xt_high, 1)
                                if GROUP <= i + 2 < BT:
                                    norm_x(i + 2)
                                silu(jobs_early(i - 3))
                                k = i - 2
                                if 0 <= k < BT:
                                    act.wait_ge(aq_norm, b * (4 * BT) + 4 * k + 4)
                                    if k == 0:
                                        act.wait_ge(vn_ones, first // 2 + 1)
                                    if k >= 2:
                                        act.wait_ge(qkt_done, b * BT + k - 1)
                                    n = qnorm[k % 2]
                                    for r in range(3):
                                        src = bank[2 + 2 * (k % 2)][:, r * E:(r + 1) * E] if r < 2 else bank[3 + 2 * (k % 2)][:, 0:E]
                                        if r < 2:
                                            dst = qkn[k % 2][:, r * E:(r + 1) * E]
                                        else:
                                            dst, src = vn[:, k, :, 0:P], src.rearrange("p (j c) -> p j c", j=HALVES)
                                        act.activation(dst, src, ACT.Identity, bias=n[:, 1, r:r + 1],
                                                       scale=n[:, 0, r:r + 1]).then_inc(qkvn_made, 1)
                                k = i - 3
                                if 0 <= k < BT:
                                    act.wait_ge(qkt_done, b * BT + k + 1)
                                    act.wait_ge(kt_made, b * BT + k + 1)
                                    for j in range(HALVES):
                                        act.activation(tq[:, j, k * P:(k + 1) * P],
                                                       bank[6][:, j * P:(j + 1) * P], ACT.Identity,
                                                       accum_out=qpart[:, j, k:k + 1]).then_inc(qt_made, 1)
                                k = i - 4
                                if 0 <= k < BT:
                                    act.wait_ge(phik_done, b * BT + k + 1)
                                    act.activation(tk[:, k], bank[1][:, 0:E], ACT.Tanh).then_inc(tk_made, 1)

                            def phi_q(g):
                                act.wait_ge(phiq_done, b * (2 * GROUPS) + 2 * g + 2)
                                for j in range(HALVES):
                                    act.activation(tq[:, j, g * GROUP * P:(g + 1) * GROUP * P], bank[PHI_BANKS[g][j]][:], ACT.Tanh,
                                                   bias=phiq_bias[:, j:j + 1]).then_inc(tq_made, 1)

                            phi_q(0)
                            act.wait_ge(max_step, b * MAXS + MAXS)
                            for c in range(4):
                                act.activation(alpha_t[:, c * 512:(c + 1) * 512], bank[2 + c][0:H, :], ACT.Exp, bias=small[:, 8:9],
                                               accum_out=small[:, 10 + c:11 + c]).then_inc(alpha_exp, 1)
                            act.activation(small[:, 14:15], small[:, 9:10], ACT.Exp).then_inc(alpha_exp, 1)
                            phi_q(1)
                            act.wait_ge(alpha_turned, b + 1)
                            act.activation(alpha[:].rearrange("p i h -> p (i h)"), bank[2][:, 0:BT * H], ACT.Copy).then_inc(alpha_made, 1)
                            phi_q(2)
                            phi_q(3)
                            def norm_attention(k):
                                act.wait_ge(c_norm, b * (4 * BT) + 4 * k + 4)
                                if k >= 2:
                                    act.wait_ge(an_turned, b * BT + k - 1)
                                    act.wait_ge(res_step, b * (2 * BT) + 2 * (k - 1))
                                act.activation(an[k % 2], bank[6][:, 0:E], ACT.Identity, bias=cnorm[k % 2][:, 1:2],
                                               scale=cnorm[k % 2][:, 0:1]).then_inc(an_made, 1)

                            def amid_hidden(i):
                                return 0 < i - 6 and i % PAIR == 1 and i - 4 < BT

                            for i in range(BT + 7):
                                if 0 <= i - 5 < BT and not amid_hidden(i - 1):
                                    norm_attention(i - 5)
                                k = i - 1
                                if 0 <= k < BT:
                                    act.wait_ge(attn_turned, b * BT + k + 1)
                                    if k == 0:
                                        act.wait_ge(score_done, b * 2 + 2)
                                    act.activation(attnt[:, :, 2 + k * P:2 + (k + 1) * P],
                                                   bank[4][:, 0:E].rearrange("p (j c) -> p j c", j=HALVES), ACT.Copy).then_inc(attnt_made, 1)
                                k = i - 5
                                if 0 <= k < BT:
                                    g, r = k // PAIR, k % PAIR
                                    act.wait_ge(an_turned, b * BT + k + 1)
                                    if r == 0 and g >= 2:
                                        act.wait_ge(up_done, b * (PAIRS_A * F_CHUNKS) + (g - 1) * F_CHUNKS)
                                    act.activation(ant_s[g % 2][0][:, :, r * P:(r + 1) * P],
                                                   bank[5][:, 0:E].rearrange("p (j c) -> p j c", j=HALVES), ACT.Copy).then_inc(ant_high, 1)
                                silu(jobs_late(i - 6))
                                k = i - 6
                                if 0 <= k < BT and k % PAIR == PAIR - 1:
                                    g = k // PAIR
                                    for f in range(F_CHUNKS):
                                        at = b * (PAIRS_A * F_CHUNKS) + g * F_CHUNKS + f
                                        if f == F_CHUNKS // 2 and amid_hidden(i):
                                            norm_attention(i - 4)
                                        if f % 2 == 0:
                                            act.wait_ge(up_done, at + 2)
                                        if g * F_CHUNKS + f >= 4:
                                            act.wait_ge(gel_split, b * (2 * PAIRS_A * F_CHUNKS) + 2 * (g * F_CHUNKS + f - 3))
                                        act.activation(gel[:, f % 4], bank[f // 2 % 2][:, f % 2 * PAIR * P:(f % 2 + 1) * PAIR * P], ACT.Gelu, bias=b1c[:, f:f + 1]).then_inc(gel_made, 1)
                            act.wait_ge(s_made, b * BT + BT)

                    @block.tensor
                    def _(pe):
                        with pe.Fori(0, 2) as h:
                            b = h + first
                            for i in range(BT + 4):
                                if i < BT:
                                    pe.wait_ge(axn_made, b * BT + i + 1)
                                    if i >= 1:
                                        pe.wait_ge(xt_made, b * BT + i)
                                    for j in range(HALVES):
                                        mm = pe.transpose(bank[0][:, j * P:(j + 1) * P], xnb[:, i, j * P:(j + 1) * P], ident[:])
                                    mm.then_inc(xt_done, 1)
                                k = i - 1
                                if 0 <= k < BT:
                                    pe.wait_ge(xt_made, b * BT + k + 1)
                                    if k >= 2:
                                        pe.wait_ge(qkvn_made, b * (3 * BT) + 3 * (k - 1))
                                    qk_bank, v_bank = bank[2 + 2 * (k % 2)], bank[3 + 2 * (k % 2)]
                                    for dst, c, width in ((qk_bank[:], ROW_Q, 2 * E), (v_bank[:, 0:E], ROW_V, E)):
                                        pe.matmul(dst, one_row[:], brow2[:, c:c + width], start=True, stop=False)
                                        mm = split_product(pe, dst, [[w[:, j] for w in xtile[k % 2]] for j in range(HALVES)],
                                                           [[w[:, j, c:c + width] for w in wa_s] for j in range(HALVES)], start=False)
                                    mm.then_inc(aq_done, 1)
                                k = i - 3
                                if 0 <= k < BT:
                                    pe.wait_ge(qkvn_made, b * (3 * BT) + 3 * k + 2)
                                    if k >= 1:
                                        pe.wait_ge(qt_made, b * (2 * BT) + 2 * k)
                                        pe.wait_ge(kt_made, b * BT + k)
                                    for c in range(4):
                                        mm = pe.transpose(bank[6][:, c * P:(c + 1) * P], qkn[k % 2][:, c * P:(c + 1) * P], ident[:])
                                    mm.then_inc(qkt_done, 1)
                                k = i - 4
                                if 0 <= k < BT:
                                    pe.wait_ge(kt_made, b * BT + k + 1)
                                    if k >= 1:
                                        pe.wait_ge(tk_made, b * BT + k)
                                    pe.matmul(bank[1][:, 0:E], one_row[:], brow2[:, ROW_PHIK:ROW_PHIK + E], start=True, stop=False)
                                    for j in range(HALVES):
                                        mm = pe.matmul(bank[1][:, 0:E], knt[:, j, k * P:(k + 1) * P], wphi[:, 1, j], start=False, stop=j == 1)
                                    mm.then_inc(phik_done, 1)

                            def phi_q(g):
                                if g == 0:
                                    pe.wait_ge(qt_made, b * (2 * BT) + 2 * BT)
                                if g == 1:
                                    pe.wait_ge(tq_made, b * (2 * GROUPS) + 2)
                                for n in range(HALVES):
                                    for j in range(HALVES):
                                        mm = pe.matmul(bank[PHI_BANKS[g][n]][:], wphi[:, 0, j, n * P:(n + 1) * P],
                                                       tq[:, j, g * GROUP * P:(g + 1) * GROUP * P], start=j == 0, stop=j == 1)
                                    mm.then_inc(phiq_done, 1)

                            phi_q(0)
                            pe.wait_ge(mean_step, b * MEANS + MEANS)
                            pe.wait_ge(tk_made, b * BT + BT)
                            for j in range(HALVES):
                                mm = pe.matmul(bank[1][0:H, 0:1], qheads[:, j], lnk[:, 1, j:j + 1], start=j == 0, stop=j == 1)
                            mm.then_inc(score_done, 1)
                            pe.wait_ge(qkvn_made, b * (3 * BT) + 3 * BT)
                            for c in range(4):
                                for j in range(HALVES):
                                    mm = pe.matmul(bank[2 + c][0:H, :], qheads_k[:, j], knt[:, j, c * 512:(c + 1) * 512], start=j == 0, stop=j == 1)
                            mm.then_inc(score_done, 1)
                            phi_q(1)
                            pe.wait_ge(max_step, b * MAXS + 1)
                            phi_q(2)
                            hold(pe, alpha_exp, b * 5 + 5, pe_passed)
                            for i in range(BT):
                                mm = pe.transpose(bank[2][:, i * H:(i + 1) * H], alpha_t[:, i * P:(i + 1) * P], ident[0:H, 0:H])
                            mm.then_inc(alpha_turned, 1)
                            pe.wait_ge(norm_step, b * NORMS + NORMS)
                            for j in range(HALVES):
                                pe.matmul(bank[3][:, 2 * j:2 * j + 2], headmask_t[:, j * P:(j + 1) * P], small[:, 14:16], start=True, stop=True)
                            pe.wait_ge(tq_made, b * (2 * GROUPS) + 4)
                            for i in range(BT):
                                pe.wait_ge(pks_made, b * BT + i + 1)
                                for j in range(HALVES):
                                    mm = pe.matmul(bank[6 + j][:, 0:P + 1], pks[i % 2][:, j * P:(j + 1) * P], vn[:, i, j], start=i == 0, stop=i == BT - 1)
                                mm.then_inc(kv_done, 1)
                            phi_q(3)
                            for i in range(BT + 7):
                                if i < BT:
                                    if i == 0:
                                        pe.wait_ge(kv_step, b * KVS + KVS)
                                    if i % GROUP == 0:
                                        pe.wait_ge(tq_plus, b * GROUPS + i // GROUP + 1)
                                    if i >= 1:
                                        pe.wait_ge(attn_step, b * (3 * BT) + 3 * i)
                                    for j in range(HALVES):
                                        mm = pe.matmul(bank[2][:, j * (P + 8):(j + 1) * (P + 8)], tq[:, j, i * P:(i + 1) * P], kvblk[:, j], start=True, stop=True)
                                    mm.then_inc(nd_done, 1)
                                k = i - 1
                                if 0 <= k < BT:
                                    pe.wait_ge(attn_step, b * (3 * BT) + 3 * k + 3)
                                    if k == 0:
                                        pe.wait_ge(tq_made, b * (2 * GROUPS) + 2 * GROUPS)
                                    if k >= 1:
                                        pe.wait_ge(attnt_made, b * BT + k)
                                    for j in range(HALVES):
                                        mm = pe.transpose(bank[4][:, j * P:(j + 1) * P], attn[k % 2][:, j * P:(j + 1) * P], ident[:])
                                    mm.then_inc(attn_turned, 1)
                                k = i - 4
                                if 0 <= k < BT:
                                    pe.wait_ge(attnt_made, b * BT + min(k + 2, BT))
                                    pe.wait_ge(ends_zero, b + 1)
                                    if k >= 1:
                                        pe.wait_ge(an_made, b * BT + k)
                                    pe.matmul(bank[6][:, 0:E], one_row[:], brow2[:, ROW_CONV:ROW_CONV + E], start=True, stop=False)
                                    for j in range(HALVES):
                                        for tap in range(5):
                                            mm = pe.matmul(bank[6][:, j * P:(j + 1) * P], attnt[:, j, k * P + tap:k * P + tap + P], wconv[:, j, tap],
                                                           start=False, stop=j == 1 and tap == 4)
                                    mm.then_inc(conv_done, 1)
                                k = i - 5
                                if 0 <= k < BT:
                                    pe.wait_ge(an_made, b * BT + k + 1)
                                    if k >= 1:
                                        pe.wait_ge(ant_made, b * BT + k)
                                    for j in range(HALVES):
                                        mm = pe.transpose(bank[5][:, j * P:(j + 1) * P], an[k % 2][:, j * P:(j + 1) * P], ident[:])
                                    mm.then_inc(an_turned, 1)
                                k = i - 6
                                if 0 <= k < BT and k % PAIR == PAIR - 1:
                                    g = k // PAIR
                                    pe.wait_ge(ant_made, b * BT + k + 1)
                                    for f in range(F_CHUNKS):
                                        if f % 2 == 0 and g * F_CHUNKS + f >= 4:
                                            pe.wait_ge(gel_made, b * (PAIRS_A * F_CHUNKS) + g * F_CHUNKS + f - 2)
                                        mm = split_product(pe, bank[f // 2 % 2][:, f % 2 * PAIR * P:(f % 2 + 1) * PAIR * P],
                                                           [[w[:, j, f * P:(f + 1) * P] for w in w1_s] for j in range(HALVES)],
                                                           [[w[:, j] for w in ant_s[g % 2]] for j in range(HALVES)])
                                        mm.then_inc(up_done, 1)
                                k = i - 7
                                if 0 <= k < BT and k % PAIR == PAIR - 1:
                                    g = k // PAIR
                                    pe.wait_ge(gel_split, b * (2 * PAIRS_A * F_CHUNKS) + 2 * (g + 1) * F_CHUNKS)
                                    for r in range(PAIR):
                                        n = g * PAIR + r
                                        if n >= 2:
                                            pe.wait_ge(s_made, b * BT + n - 1)
                                        dst = bank[7 if n % 2 == 0 else 3][:, 0:E]
                                        pe.matmul(dst, one_row[:], brow2[:, ROW_OUT:ROW_OUT + E], start=True, stop=False)
                                        mm = split_product(pe, dst, [[w[:, f, r * P:(r + 1) * P] for w in gel_s] for f in range(F_CHUNKS)],
                                                           [[w[:, f] for w in w2_s] for f in range(F_CHUNKS)], start=False)
                                        mm.then_inc(down_done, 1)
                            pe.wait_ge(s_made, b * BT + BT)

                    @block.vector
                    def _(dve):
                        if not scatters:
                            dve.sem_inc(job_made, JOBS_AHEAD)
                        else:
                            for q in s_out:
                                dve.sem_inc(q, 16)
                        with dve.Fori(0, 2) as h:
                            b = h + first
                            def mix(j):
                                p, before = j % 2, count(h, j, 4) - 4
                                rows = picked[p]
                                g = [gate[:, tile_of(h, j), k] for k in range(2)]
                                dve.wait_ge(picked_in[p], count_of(h, j, 32))
                                dve.wait_ge(job_in[p], count_of(h, j, 48))
                                dve.tensor_scalar(rows[:, 0], rows[:, 0], g[0], None, ALU.mult).then_inc(job_step, 1)
                                dve.wait_ge(job_step, before + 1)
                                dve.scalar_tensor_tensor(rows[:, 0], rows[:, 1], g[1], rows[:, 0], ALU.mult, ALU.add).then_inc(job_step, 1)
                                dve.wait_ge(job_step, before + 2)
                                dve.tensor_tensor(rows[:, 0], rows[:, 0], job_after[p][:], ALU.add).then_inc(job_mixed, 1)

                            def join(j):
                                p = j % 2
                                dve.wait_ge(job_silu, count(h, j, 1))
                                dve.scalar_tensor_tensor(picked[p][:, 1], picked[p][:, 1], 1.0, picked[p][:, 0],
                                                         ALU.add, ALU.mult).then_inc(job_step, 1)
                                dve.wait_ge(job_step, count(h, j, 4) - 1)
                                dve.tensor_tensor(picked[p][:, 1], picked[p][:, 1], job_s[p][:], ALU.mult).then_inc(job_step, 1)
                                dve.wait_ge(job_step, count(h, j, 4))
                                dve.scalar_tensor_tensor(job_x[p][:], picked[p][:, 1], 0.5, job_x[p][:],
                                                         ALU.mult, ALU.add).then_inc(job_made, 1)

                            def jobs(joined, mixed):
                                if not scatters:
                                    for j in joined:
                                        join(j)
                                    for j in mixed:
                                        mix(j)

                            def stats_x(g, half):
                                tiles = range(2 * half, 2 * half + 2)
                                dve.wait_ge(ax_in[g % 2], h * 32 + (first // 2 * 80 + g // 2 * 16 + 16))
                                if g >= 1:
                                    dve.wait_ge(ax_mv, b * BT + g * GROUP)
                                for k in tiles:
                                    dve.bn_stats(xstats[:, k], xa[g % 2][:, k]).then_inc(ax_stats, 1)
                                hold(dve, ax_stats, b * BT + (g * GROUP + 2 * half + 2), dve_passed)
                                for k in tiles:
                                    dve.bn_aggr(xmv[g % 2][:, k], xstats[:, k]).then_inc(ax_mv, 1)

                            for g, half in ((0, 0), (0, 1), (1, 0), (1, 1)):
                                stats_x(g, half)
                            for i in range(BT + 4):
                                if i < BT:
                                    dve.wait_ge(xt_high, b * BT + i + 1)
                                    hi, lo = xtile[i % 2]
                                    dve.tensor_tensor(lo[:].rearrange("p j c -> p (j c)"), bank[0][:, 0:E],
                                                      hi[:].rearrange("p j c -> p (j c)"), ALU.subtract).then_inc(xt_made, 1)
                                k = i - 1
                                if 0 <= k < BT:
                                    dve.wait_ge(aq_done, b * BT + k + 1)
                                    if k >= 1:
                                        dve.wait_ge(aq_mv, b * (3 * BT) + 3 * k)
                                    for r in range(3):
                                        src = bank[2 + 2 * (k % 2)][:, r * E:(r + 1) * E] if r < 2 else bank[3 + 2 * (k % 2)][:, 0:E]
                                        dve.bn_stats(qstats[:, r], src).then_inc(aq_stats, 1)
                                    hold(dve, aq_stats, b * (3 * BT) + 3 * k + 3, dve_passed)
                                    if k >= 2:
                                        hold(dve, aq_norm, b * (4 * BT) + 4 * (k - 1), dve_passed)
                                    for r in range(3):
                                        dve.bn_aggr(qmv[k % 2][:, r], qstats[:, r]).then_inc(aq_mv, 1)
                                k = i - 3
                                if 0 <= k < BT:
                                    dve.wait_ge(qkt_done, b * BT + k + 1)
                                    dve.tensor_copy(knt[:, :, k * P:(k + 1) * P], bank[6][:, 2 * P:4 * P].rearrange("p (j c) -> p j c", j=HALVES)).then_inc(kt_made, 1)
                                if i % GROUP >= 2 and i // GROUP + 2 < GROUPS:
                                    stats_x(i // GROUP + 2, i % GROUP - 2)
                                jobs(jobs_early(i - 3), jobs_early(i - 2))
                            step = Chain(dve, mean_step, b * MEANS)
                            dve.wait_ge(qt_made, b * (2 * BT) + 2 * BT)
                            step(dve.tensor_reduce(qmean[:], qpart[:], AX_X, ALU.add))
                            step(dve.tensor_scalar(qmean[:], qmean[:], 1.0 / NB, None, ALU.mult))
                            step(dve.tensor_tensor(qmean[:], qmean[:], lnq[:, 0], ALU.mult))
                            step(dve.tensor_tensor(qmean[:], qmean[:], lnq[:, 1], ALU.add))
                            step(dve.tensor_scalar(qmean[:], qmean[:], float(D) ** -0.5, None, ALU.mult))
                            step(dve.tensor_tensor(qmean_k[:], qmean[:], lnk[:, 0], ALU.mult))
                            for j in range(HALVES):
                                step(dve.tensor_scalar(qheads[:, j], headmask[:, j], qmean[:, j:j + 1], None, ALU.mult))
                                step(dve.tensor_scalar(qheads_k[:, j], headmask[:, j], qmean_k[:, j:j + 1], None, ALU.mult))
                            step = Chain(dve, max_step, b * MAXS)
                            dve.wait_ge(score_done, b * 2 + 1)
                            step(dve.tensor_copy(small[:, 0:1], bank[1][0:H, 0:1]))
                            dve.wait_ge(score_done, b * 2 + 2)
                            for c in range(4):
                                mx = dve.tensor_reduce(small[:, 1 + c:2 + c], bank[2 + c][0:H, :], AX_X, ALU.max)
                            step(mx)
                            step(dve.tensor_reduce(small[:, 5:6], small[:, 1:5], AX_X, ALU.max))
                            step(dve.tensor_tensor(small[:, 6:7], small[:, 5:6], small[:, 0:1], ALU.add))
                            step(dve.tensor_scalar(small[:, 7:8], small[:, 6:7], 0.0, None, ALU.max))
                            step(dve.tensor_tensor(small[:, 8:9], small[:, 0:1], small[:, 7:8], ALU.subtract))
                            step(dve.tensor_scalar(small[:, 9:10], small[:, 7:8], -1.0, None, ALU.mult))
                            step = Chain(dve, norm_step, b * NORMS)
                            dve.wait_ge(alpha_exp, b * 5 + 5)
                            step(dve.tensor_reduce(small[:, 16:17], small[:, 10:14], AX_X, ALU.add))
                            step(dve.tensor_tensor(small[:, 16:17], small[:, 16:17], small[:, 14:15], ALU.add))
                            step(dve.reciprocal(small[:, 17:18], small[:, 16:17]))
                            step(dve.tensor_scalar(small[:, 15:16], small[:, 17:18], float(NB), None, ALU.mult))

                            def plus_one(g):
                                dve.wait_ge(tq_made, b * (2 * GROUPS) + 2 * g + 2)
                                part = tq[:, :, g * GROUP * P:(g + 1) * GROUP * P]
                                dve.tensor_scalar(part, part, 1.0, None, ALU.add).then_inc(tq_plus, 1)

                            plus_one(0)
                            plus_one(1)
                            dve.wait_ge(alpha_made, b + 1)
                            for i in range(BT):
                                if i >= 2:
                                    dve.wait_ge(kv_done, b * BT + i - 1)
                                dve.scalar_tensor_tensor(pks[i % 2][:].rearrange("p (h d) -> p h d", d=D), tk[:, i].rearrange("p (h d) -> p h d", d=D),
                                                         1.0, alpha[:, i].unsqueeze(2).to_broadcast((P, H, D)), ALU.add, ALU.mult).then_inc(pks_made, 1)
                            plus_one(2)
                            dve.wait_ge(score_done, b * 2 + 2)
                            dve.memset(attnt[:, :, 0:2], 0.0)
                            dve.memset(attnt[:, :, NB + 2:NB + 4], 0.0).then_inc(ends_zero, 1)
                            step = Chain(dve, kv_step, b * KVS)
                            dve.wait_ge(kv_done, b * BT + BT)
                            step(dve.tensor_copy(spread[:].rearrange("p j c -> p (j c)"), bank[3][:, 0:4]))
                            halves = [(j, bank[6 + j], slice(j * P, (j + 1) * P)) for j in range(HALVES)]
                            step.also(dve.tensor_tensor(ksum[:, :, 0], phik_zero[:], spread[:, :, 0], ALU.mult))
                            step.also(dve.tensor_tensor(kvt[:, 0], bank[6][:, 0:P], gv_row[:, 0:P], ALU.mult))
                            step(dve.tensor_tensor(kvt[:, 1], bank[7][:, 0:P], gv_row[:, P:E], ALU.mult))
                            for j, raw, half in halves:
                                step.also(dve.scalar_tensor_tensor(kvt[:, j], bv_row[:, half], raw[:, P:P + 1], kvt[:, j], ALU.mult, ALU.add))
                            step.also(dve.tensor_tensor(ksum[:, 0, 1:2], bank[6][:, P:P + 1], ksum[:, 0, 0:1], ALU.add))
                            step(dve.tensor_tensor(ksum[:, 1, 1:2], bank[7][:, P:P + 1], ksum[:, 1, 0:1], ALU.add))
                            for j, raw, half in halves:
                                step.also(dve.scalar_tensor_tensor(kvblk[:, j, 0:P], kvt[:, j], spread[:, j, 1:2], diag[:], ALU.mult, ALU.mult))
                            step.also(dve.tensor_scalar(ksum[:, 0, 1:2], ksum[:, 0, 1:2], spread[:, 0, 1:2], None, ALU.mult))
                            step(dve.tensor_scalar(ksum[:, 1, 1:2], ksum[:, 1, 1:2], spread[:, 1, 1:2], None, ALU.mult))
                            step.also(dve.tensor_scalar(kvblk[:, 0, P:P + 8], diag[:, 0:P:D], ksum[:, 0, 1:2], None, ALU.mult))
                            step(dve.tensor_scalar(kvblk[:, 1, P:P + 8], diag[:, 0:P:D], ksum[:, 1, 1:2], None, ALU.mult))
                            assert step.done == KVS
                            for i in range(BT + 7):
                                jobs(jobs_late(i - 7), jobs_late(i - 6))
                                if i == 2:
                                    plus_one(3)
                                if i < BT:
                                    step = Chain(dve, attn_step, b * (3 * BT) + 3 * i)
                                    dve.wait_ge(nd_done, b * BT + i + 1)
                                    both = bank[2][:, 0:2 * (P + 8)].rearrange("p (j c) -> p j c", j=HALVES)
                                    step(dve.tensor_scalar(den[:], both[:, :, P:P + 8], EPS_DEN, None, ALU.add))
                                    step(dve.reciprocal(den[:], den[:]))
                                    if i >= 2:
                                        dve.wait_ge(attn_turned, b * BT + i - 1)
                                    step(dve.tensor_tensor(attn[i % 2].rearrange("p (j h d) -> p j h d", j=HALVES, d=D),
                                                           both[:, :, 0:P].rearrange("p j (h d) -> p j h d", d=D),
                                                           den[:].unsqueeze(3).to_broadcast((P, HALVES, 8, D)), ALU.mult))
                                k = i - 4
                                if 0 <= k < BT:
                                    dve.wait_ge(conv_done, b * BT + k + 1)
                                    if k >= 1:
                                        dve.wait_ge(c_mv, b * BT + k)
                                    dve.bn_stats(cstats[:], bank[6][:, 0:E]).then_inc(c_stats, 1)
                                    hold(dve, c_stats, b * BT + k + 1, dve_passed)
                                    dve.bn_aggr(cmv[k % 2][:], cstats[:]).then_inc(c_mv, 1)
                                k = i - 5
                                if 0 <= k < BT:
                                    g, r = k // PAIR, k % PAIR
                                    dve.wait_ge(ant_high, b * BT + k + 1)
                                    part = slice(r * P, (r + 1) * P)
                                    dve.tensor_tensor(ant_s[g % 2][1][:, :, part], bank[5][:, 0:E].rearrange("p (j c) -> p j c", j=HALVES),
                                                      ant_s[g % 2][0][:, :, part], ALU.subtract).then_inc(ant_made, 1)
                                k = i - 6
                                if 0 <= k < BT and k % PAIR == PAIR - 1:
                                    g = k // PAIR
                                    if g >= 1:
                                        dve.wait_ge(down_done, b * BT + g * PAIR)
                                    for f in range(F_CHUNKS):
                                        at = b * (2 * PAIRS_A * F_CHUNKS) + 2 * (g * F_CHUNKS + f)
                                        hi, lo = gel_s
                                        dve.wait_ge(gel_made, b * (PAIRS_A * F_CHUNKS) + g * F_CHUNKS + f + 1)
                                        dve.tensor_copy(hi[:, f], gel[:, f % 4]).then_inc(gel_split, 1)
                                        dve.wait_ge(gel_split, at + 1)
                                        dve.tensor_tensor(lo[:, f], gel[:, f % 4], hi[:, f], ALU.subtract).then_inc(gel_split, 1)
                                k = i - 7
                                if 0 <= k < BT and k % PAIR == PAIR - 1:
                                    for n in range(k - PAIR + 1, k + 1):
                                        dve.wait_ge(down_done, b * BT + n + 1)
                                        dve.wait_ge(res_step, b * (2 * BT) + 2 * n + 2)
                                        dve.wait_ge(s_out[n % 2], b * (BT // 2 * 16) + (n // 2 * 16 + 16))
                                        dve.tensor_tensor(sout[n % 2][:], bank[7 if n % 2 == 0 else 3][:, 0:E], xnb[:, n], ALU.add).then_inc(s_made, 1)

        attend(0, scatters=True)

        with ExitStack() as own:
            CHUNK = 2 * P
            CHUNKS = CAP // CHUNK
            UNROLL = 2 * CHUNKS
            FC = FFN // P
            rows_in = [sb(f"rows_in{p}", [P, 2, E], F32, own) for p in range(2)]
            rows_t = sb("rows_t", [P, HALVES, CHUNK], F32, own)
            up_w = [sb(f"up_w{p}", [P, HALVES, FFN], F32, own) for p in range(2)]
            down_w = [sb(f"down_w{p}", [P, FC, E], F32, own) for p in range(2)]
            hid = [sb(f"hid{p}", [P, FC, CHUNK], F32, own) for p in range(2)]
            rows_s = [[sb(f"rows_{w}{p}", [P, HALVES, CHUNK], F32R, own) for w in ("hi", "lo")] for p in range(2)]
            up_s = [[sb(f"up_{w}{p}", [P, HALVES, FFN], F32R, own) for w in ("hi", "lo")] for p in range(2)]
            down_s = [[sb(f"down_{w}{p}", [P, FC, E], F32R, own) for w in ("hi", "lo")] for p in range(2)]
            hid_s = [[sb(f"hid_{w}{p}", [P, FC, CHUNK], F32R, own) for w in ("hi", "lo")] for p in range(2)]
            h2 = [sb(f"h2_{p}", [P, 2, E], F32, own) for p in range(2)]
            rows_loaded, weights_in = [sem("rows_loaded0"), sem("rows_loaded1")], [sem("weights_in0"), sem("weights_in1")]
            h2_out = [sem("h2_out0"), sem("h2_out1")]
            rows_turned, rows_made, e_up, e_hid, e_down, h2_made = (
                sem("rows_turned"), sem("rows_made"), sem("e_up"), sem("e_hid"), sem("e_down"), sem("h2_made"))
            rows_split, hid_split, weights_split = sem("e_rows_split"), sem("e_hid_split"), sem("weights_split")
            AHEAD, HID_AHEAD, EXPERTS_AHEAD = 2, 4, CHUNKS + 1

            def steps(b):
                for i in range(UNROLL):
                    yield i, i // CHUNKS, i % CHUNKS, i % 2

            with nc.Block() as block:
                @block.sync
                def _(sp):
                    with sp.Fori(0, NX // 2) as b:
                        for i, odd, c, p in steps(b):
                            hold(sp, rows_turned, b * UNROLL + i + 1, sp_passed)
                            sp.dma_start(rows_in[p][:], buf_d.rearrange("(t i p) e -> p t i e", p=P, i=2)
                                         [:, bass.ds(b * UNROLL + i, 1)].rearrange("p a i e -> p (a i) e")).then_inc(rows_loaded[p], 16)

                @block.scalar
                def _(act):
                    act.sem_inc(e_hid, HID_AHEAD)
                    for q in h2_out:
                        act.sem_inc(q, 16)
                    with act.Fori(0, NX // 2) as b:
                        def store(i):
                            hold(act, h2_made, b * UNROLL + i + 1 + AHEAD, act_passed)
                            act.dma_start(h2_d[0:SLOTS].rearrange("(t i p) e -> p t i e", p=P, i=2)
                                          [:, bass.ds(b * UNROLL + i, 1)].rearrange("p a i e -> p (a i) e"),
                                          h2[i % 2][:]).then_inc(h2_out[i % 2], 16)

                        for i, odd, c, p in steps(b):
                            for half in range(2):
                                act.wait_ge(e_up, b * (2 * UNROLL) + 2 * i + half + 1 + 2 * AHEAD)
                                if half == 0:
                                    act.wait_ge(e_down, b * UNROLL + i + 1 - AHEAD + EXPERTS_AHEAD)
                                for dst in (hid[p], hid_s[p][0]):
                                    act.activation(dst[:, 2 * half:2 * half + 2].rearrange("p f c -> p (f c)"),
                                                   bank[half][:], ACT.Gelu_apprx_tanh).then_inc(e_hid, 1)
                            if i:
                                store(i - 1)
                        store(UNROLL - 1)
                    for q in h2_out:
                        act.wait_ge(q, 16 * NX * CHUNKS // 2 + 16)

                @block.tensor
                def _(pe):
                    pe.sem_inc(rows_turned, AHEAD)
                    pe.sem_inc(e_up, 2 * AHEAD)
                    pe.sem_inc(e_down, EXPERTS_AHEAD)

                    with pe.Fori(0, NX // 2) as b:
                        def turn_rows(i):
                            p = i % 2
                            pe.wait_ge(rows_loaded[p], b * (UNROLL // 2 * 16) + i // 2 * 16 + 16)
                            pe.wait_ge(rows_made, b * (2 * UNROLL) + 2 * i + 2)
                            for j in range(HALVES):
                                for r in range(2):
                                    mm = pe.transpose(bank[2 + p][:, j * CHUNK + r * P:j * CHUNK + r * P + P],
                                                      rows_in[p][:, r, j * P:(j + 1) * P], ident[:])
                            mm.then_inc(rows_turned, 1)

                        def down(i):
                            odd, p = i // CHUNKS, i % 2
                            pe.wait_ge(h2_made, b * UNROLL + i + 1)
                            pe.wait_ge(weights_split, b * 8 + 4 * odd + 4)
                            pe.wait_ge(hid_split, b * (2 * UNROLL) + 2 * i + 2)
                            for r in range(2):
                                mm = split_product(pe, bank[4 + p][:, r * E:(r + 1) * E],
                                                   [[w[:, f, r * P:(r + 1) * P] for w in hid_s[p]] for f in range(FC)],
                                                   [[w[:, f] for w in down_s[odd]] for f in range(FC)])
                            mm.then_inc(e_down, 1)

                        turn_rows(0)
                        for i, odd, c, p in steps(b):
                            if i + 1 < UNROLL:
                                turn_rows(i + 1)
                            if c == 0:
                                pe.wait_ge(weights_split, b * 8 + 4 * odd + 2)
                            pe.wait_ge(rows_split, b * (2 * UNROLL) + 2 * i + 2 + 1)
                            for f in range(FC):
                                if f % 2 == 0:
                                    pe.wait_ge(e_hid, b * (4 * UNROLL) + 4 * i - 4 + f + 2 + HID_AHEAD)
                                mm = split_product(pe, bank[f // 2][:, f % 2 * CHUNK:f % 2 * CHUNK + CHUNK],
                                                   [[w[:, j, f * P:(f + 1) * P] for w in up_s[odd]] for j in range(HALVES)],
                                                   [[w[:, j] for w in rows_s[p]] for j in range(HALVES)])
                                if f % 2:
                                    mm.then_inc(e_up, 1)
                            if i:
                                down(i - 1)
                        down(UNROLL - 1)

                @block.gpsimd
                def _(pool):
                    with pool.Fori(0, NX // 2) as b:
                        for odd in range(2):
                            pool.dma_start(up_w[odd][:], a["w1_t"][bass.ds(b * 2 + odd, 1)]
                                           .rearrange("a (j p) f -> p (a j) f", p=P)).then_inc(weights_in[odd], 16)
                            pool.dma_start(down_w[odd][:], a["w2_t"][bass.ds(b * 2 + odd, 1)]
                                           .rearrange("a (j p) f -> p (a j) f", p=P)).then_inc(weights_in[odd], 16)
                            hold(pool, e_down, b * UNROLL + (odd - 1) * CHUNKS + EXPERTS_AHEAD, pool_passed)
                            hold(pool, weights_in[odd], b * 32 + 32, pool_passed)
                            step = Chain(pool, weights_split, b * 8 + 4 * odd, pool_passed)
                            for w, (hi, lo) in ((up_w[odd], up_s[odd]), (down_w[odd], down_s[odd])):
                                step(pool.tensor_copy(hi[:], w[:]))
                                step(pool.tensor_tensor(lo[:], w[:], hi[:], ALU.subtract))

                @block.vector
                def _(dve):
                    dve.sem_inc(rows_made, 2 * AHEAD)
                    dve.sem_inc(h2_made, AHEAD)
                    dve.sem_inc(rows_split, 1)
                    with dve.Fori(0, NX // 2) as b:
                        def rows_out(i):
                            p = i % 2
                            hi, lo = rows_s[p]
                            dve.wait_ge(rows_turned, b * UNROLL + i + 1 + AHEAD)
                            dve.wait_ge(rows_split, b * (2 * UNROLL) + 2 * i + 1)
                            for j in range(HALVES):
                                dve.tensor_scalar(rows_t[:, j], bank[2 + p][:, j * CHUNK:(j + 1) * CHUNK],
                                                  ln2w[:, j:j + 1], ln2b[:, j:j + 1], ALU.mult, ALU.add).then_inc(rows_made, 1)
                            dve.wait_ge(rows_made, b * (2 * UNROLL) + 2 * i + 2 + 2 * AHEAD)
                            dve.wait_ge(e_up, b * (2 * UNROLL) + 2 * i + 2)
                            dve.tensor_copy(hi[:], rows_t[:]).then_inc(rows_split, 1)
                            dve.wait_ge(rows_split, b * (2 * UNROLL) + 2 * i + 1 + 1)
                            dve.tensor_tensor(lo[:], rows_t[:], hi[:], ALU.subtract).then_inc(rows_split, 1)

                        def result_out(i):
                            dve.wait_ge(e_down, b * UNROLL + i + 1 + EXPERTS_AHEAD)
                            dve.wait_ge(h2_out[i % 2], b * (UNROLL // 2 * 16) + i // 2 * 16 + 16)
                            dve.tensor_copy(h2[i % 2][:].rearrange("p r e -> p (r e)"), bank[4 + i % 2][:]).then_inc(h2_made, 1)

                        rows_out(0)
                        for i, odd, c, p in steps(b):
                            if i + 1 < UNROLL:
                                rows_out(i + 1)
                            hi, lo = hid_s[p]
                            for half in range(2):
                                part = slice(2 * half, 2 * half + 2)
                                dve.wait_ge(e_hid, b * (4 * UNROLL) + 4 * i + 2 * half + 2 + HID_AHEAD)
                                if half == 0:
                                    dve.wait_ge(e_down, b * UNROLL + i + 1 - AHEAD + EXPERTS_AHEAD)
                                dve.tensor_tensor(lo[:, part], hid[p][:, part], hi[:, part], ALU.subtract).then_inc(hid_split, 1)
                            if i:
                                result_out(i - 1)
                        result_out(UNROLL - 1)

        attend(2, scatters=False)

        with ExitStack() as own:
            FIRST = 2 * GATHERS
            TURNS = (TILES - FIRST) // GROUP
            rows_of = [sb(f"rows_of{p}", [P, GROUP, 2], I32, own) for p in range(2)]
            picked = [sb(f"picked{p}", [P, GROUP, 2, E], F32, own) for p in range(2)]
            after_c = [sb(f"after_c{p}", [P, GROUP, E], F32, own) for p in range(2)]
            s_c = [sb(f"s_c{p}", [P, GROUP, E], F32, own) for p in range(2)]
            x_c = [sb(f"x_c{p}", [P, GROUP, E], F32, own) for p in range(2)]
            ffn = [sb(f"ffn{p}", [P, GROUP, E], F32, own) for p in range(2)]
            silu = [sb(f"silu{p}", [P, GROUP, E], F32, own) for p in range(2)]
            result = [sb(f"result{p}", [P, GROUP, E], F32, own) for p in range(2)]
            group_in, picked_in, group_out = (
                [sem("group_in0"), sem("group_in1")], [sem("picked_in0"), sem("picked_in1")], [sem("group_out0"), sem("group_out1")])
            rows_staged, ffn_made, silu_made, result_made, comb_step = (
                sem("rows_staged"), sem("ffn_made"), sem("silu_made"), sem("result_made"), sem("comb_step"))
            DSTEPS = 2 * GROUP + 1
            FFN_AHEAD, RESULT_AHEAD = 2, 2

            def tiles_of(ap, turn):
                return ap.rearrange("(t i p) e -> p t i e", p=P, i=GROUP)[:, bass.ds(turn + FIRST // GROUP, 1)].rearrange("p a i e -> p (a i) e")

            with nc.Block() as block:
                @block.sync
                def _(sp):
                    with sp.Fori(0, TURNS // 2) as b:
                        for p in range(2):
                            hold(sp, result_made, b * 2 + p - 1 + RESULT_AHEAD, sp_passed)
                            for dst, src in ((after_c, after_d), (s_c, s_d), (x_c, a["x"])):
                                sp.dma_start(dst[p][:], tiles_of(src, b * 2 + p)).then_inc(group_in[p], 16)

                @block.gpsimd
                def _(pool):
                    with pool.Fori(0, TURNS // 2) as b:
                        for p in range(2):
                            hold(pool, ffn_made, b * 2 + p - 1 + FFN_AHEAD, pool_passed)
                            pool.tensor_copy(rows_of[p][:], from_row[:, bass.ds(b * (2 * GROUP) + (p * GROUP + FIRST), GROUP)]).then_inc(rows_staged, 1)
                            hold(pool, rows_staged, b * 2 + p + 1, pool_passed)
                            for i in range(GROUP):
                                for k in range(2):
                                    pool.indirect_dma_start(picked[p][:, i, k], None, h2_d,
                                                            bass.IndirectOffsetOnAxis(rows_of[p][:, i, k:k + 1], axis=0)
                                                            ).then_inc(picked_in[p], 16)

                @block.scalar
                def _(act):
                    with act.Fori(0, TURNS // 2) as b:
                        def store(p):
                            hold(act, result_made, b * 2 + p + 1 + RESULT_AHEAD, act_passed)
                            act.dma_start(tiles_of(out, b * 2 + p), result[p][:]).then_inc(group_out[p], 16)

                        for p in range(2):
                            act.wait_ge(ffn_made, b * 2 + p + 1 + FFN_AHEAD)
                            act.activation(silu[p][:], ffn[p][:], ACT.Silu).then_inc(silu_made, 1)
                            store(p)
                    for q in group_out:
                        act.wait_ge(q, 16 * TURNS // 2 + 16)

                @block.vector
                def _(dve):
                    dve.sem_inc(ffn_made, FFN_AHEAD)
                    dve.sem_inc(result_made, RESULT_AHEAD)
                    for q in group_out:
                        dve.sem_inc(q, 16)
                    with dve.Fori(0, TURNS // 2) as b:
                        for p in range(2):
                            dve.wait_ge(picked_in[p], b * (32 * GROUP) + 32 * GROUP)
                            dve.wait_ge(group_in[p], b * 48 + 48)
                            base = b * (2 * DSTEPS) + p * DSTEPS

                            def weight(i, k):
                                return gate[:, bass.ds(b * (2 * GROUP) + (p * GROUP + i + FIRST), 1), k]

                            for i in range(GROUP):
                                dve.tensor_scalar(ffn[p][:, i], picked[p][:, i, 0], weight(i, 0), None, ALU.mult).then_inc(comb_step, 1)
                            dve.wait_ge(comb_step, base + GROUP)
                            for i in range(GROUP):
                                dve.scalar_tensor_tensor(ffn[p][:, i], picked[p][:, i, 1], weight(i, 1), ffn[p][:, i],
                                                         ALU.mult, ALU.add).then_inc(comb_step, 1)
                            dve.wait_ge(comb_step, base + 2 * GROUP)
                            dve.tensor_tensor(ffn[p][:], ffn[p][:], after_c[p][:], ALU.add).then_inc(ffn_made, 1)
                            dve.wait_ge(silu_made, b * 2 + p + 1)
                            dve.wait_ge(group_out[p], b * 16 + 16)
                            dve.tensor_tensor(silu[p][:], silu[p][:], s_c[p][:], ALU.mult).then_inc(comb_step, 1)
                            dve.wait_ge(comb_step, base + 2 * GROUP + 1)
                            dve.tensor_tensor(result[p][:], silu[p][:], x_c[p][:], ALU.add).then_inc(result_made, 1)


def kernel(**inputs):
    import numpy as _np
    import concourse.bacc as _bacc
    from concourse.bass_utils import run_bass_kernel_spmd as _run

    x = {k: _np.asarray(v) for k, v in inputs.items()}
    f, g = "L0_attn_", "L0_ffn_"
    arrays = {k[len(f):]: v for k, v in x.items() if k.startswith(f)}
    arrays["gamma"] = _np.reshape(arrays["gamma"], (1, 1))
    arrays["conv_t"] = _np.transpose(_np.reshape(arrays.pop("conv_w"), (H, D, D, 5)), (0, 2, 3, 1))
    for k in ("ln1_weight", "ln1_bias", "ln2_weight", "ln2_bias"):
        arrays[k] = x[g + k]
    arrays["qkv_t"] = x[g + "qkv_weight"].T
    arrays["proj_t"] = x[g + "proj_weight"].T
    arrays["router_t"] = x[g + "router_weight"].T
    arrays["w1_t"] = _np.transpose(x[g + "moe_w1"], (0, 2, 1))
    arrays["w2_t"] = _np.transpose(x[g + "moe_w2"], (0, 2, 1))
    arrays["x"] = _np.reshape(arrays["x"], (T, E))
    arrays = {k: _np.ascontiguousarray(v) for k, v in arrays.items()}

    nc = _bacc.Bacc("TRN2", target_bir_lowering=False, num_devices=1)
    a = {k: nc.dram_tensor(f"in_{k}", v.shape, F32, kind="ExternalInput").ap() for k, v in arrays.items()}
    out = nc.dram_tensor("out_0", (T, E), F32, kind="ExternalOutput").ap()
    build(nc, a, out)
    r = _run(nc, [{f"in_{k}": v for k, v in arrays.items()}], core_ids=[0])
    return _np.reshape(r.results[0]["out_0"], (S, NB, E))
```
